# Optimizing a Trainium2 kernel written in Bass

```python
import numpy as np
import jax
import jax.numpy as jnp

def _softmax(x, axis=-1):
    return jax.nn.softmax(x, axis=axis)

def _gelu(x):
    return jax.nn.gelu(x, approximate=True)

def _silu(x):
    return jax.nn.silu(x)

def _sigmoid(x):
    return jax.nn.sigmoid(x)

def _layernorm(x, axis=-1, eps=1e-05):
    m = jnp.mean(x, axis=axis, keepdims=True)
    v = jnp.var(x, axis=axis, keepdims=True)
    return (x - m) / jnp.sqrt(v + eps)

def _scatter_add(tgt, idx, src, axis=0):
    return tgt.at[idx].add(src)

def _segment_sum(src, seg, n):
    return jax.ops.segment_sum(src, seg, n)
kernel_name = 'mk_gnn_preln_d4_gnn_r16_dd09b7'

def setup_inputs(seed: int=0):
    np.random.seed(seed)
    _w = jnp.asarray

    def _rec_inputs():
        import jax
        import jax.numpy as jnp
        _gk = jax.random.key(seed)
        x = -0.000202 + 1 * jax.random.normal(jax.random.fold_in(_gk, 1), (6250, 128), jnp.float32)
        _s = jax.random.randint(jax.random.fold_in(_gk, 2), (50000,), 0, 6250, jnp.int32)
        _d = jax.random.randint(jax.random.fold_in(_gk, 3), (50000,), 0, 6250, jnp.int32)
        _loop = jnp.arange(6250, dtype=jnp.int32)
        src = jnp.concatenate([_s, _d, _loop])
        dst = jnp.concatenate([_d, _s, _loop])
        _o = jnp.argsort(dst, stable=True)
        src = src[_o]
        dst = dst[_o]
        edge_type_500 = jax.random.randint(jax.random.fold_in(_gk, 14), (106250,), 0, 500, jnp.int32)
        return (x, src, dst, edge_type_500)
    x, src, dst, edge_type_500 = _rec_inputs()

    def _L0_gnn_setup():
        import jax, jax.numpy as jnp
        import numpy as np
        N_NODES = 3125
        N_EDGES = 37500
        N_RELS = 500
        D = 128
        key = jax.random.key(seed)
        ks = jax.random.split(key, 8)
        h = jax.random.normal(ks[0], (N_NODES, D), dtype=jnp.float32)
        norm = jax.random.uniform(ks[1], (N_NODES, 1), dtype=jnp.float32)
        rel_emb = jax.random.normal(ks[2], (N_RELS, D), dtype=jnp.float32)
        lim = np.sqrt(6.0 / (D + D)) * np.sqrt(2.0)
        W_neighbor = jax.random.uniform(ks[3], (D, D), dtype=jnp.float32, minval=-lim, maxval=lim)
        loop_weight = jax.random.uniform(ks[4], (D, D), dtype=jnp.float32, minval=-lim, maxval=lim)
        edge_src = jax.random.randint(ks[5], (N_EDGES,), 0, N_NODES, dtype=jnp.int64 if jax.config.jax_enable_x64 else jnp.int32)
        edge_dst = jax.random.randint(ks[6], (N_EDGES,), 0, N_NODES, dtype=edge_src.dtype)
        edge_type = jax.random.randint(ks[7], (N_EDGES,), 0, N_RELS, dtype=edge_src.dtype)
        return {'h': h, 'norm': norm, 'rel_emb': rel_emb, 'W_neighbor': W_neighbor, 'loop_weight': loop_weight, 'edge_src': edge_src, 'edge_dst': edge_dst, 'edge_type': edge_type}
    _L0_gnn_all = _L0_gnn_setup()
    _L0_gnn_in = {k: v for k, v in _L0_gnn_all.items() if k in ('rel_emb', 'W_neighbor', 'loop_weight')}
    del _L0_gnn_all

    def _L1_gnn_setup():
        import jax, jax.numpy as jnp
        import numpy as np
        TOPK = 2
        key = jax.random.key(seed)
        ks = jax.random.split(key, 18)
        N, E = (1250, 20000)
        IN, H, OUT, L = (128, 256, 128, 3)
        NW, NS = (4, 4)
        NE = NW + NS

        def w(k, shape, fan):
            return jax.random.normal(k, shape, dtype=jnp.float32) / np.float32(np.sqrt(fan))
        inp = {'x': jax.random.normal(ks[0], (N, IN), dtype=jnp.float32), 'edge_index': jax.random.randint(ks[1], (2, E), 0, N, dtype=jnp.int64), 'W_in': w(ks[2], (IN, H), IN), 'b_in': jnp.zeros((H,), jnp.float32), 'router_W': w(ks[3], (L, 2 * H, NE), 2 * H), 'router_b': jnp.zeros((L, NE), jnp.float32), 'weak_W': w(ks[4], (L, NW, H, H), H), 'weak_b': jnp.zeros((L, NW, H), jnp.float32), 'strong_W1': w(ks[5], (L, NS, H, 2 * H), H), 'strong_b1': jnp.zeros((L, NS, 2 * H), jnp.float32), 'strong_W2': w(ks[6], (L, NS, 2 * H, H), 2 * H), 'strong_b2': jnp.zeros((L, NS, H), jnp.float32), 'conf_W': w(ks[7], (L, H, 1), H), 'conf_b': jnp.zeros((L, 1), jnp.float32), 'W_out': w(ks[8], (H, OUT), H), 'b_out': jnp.zeros((OUT,), jnp.float32)}
        return inp
    _L1_gnn_all = _L1_gnn_setup()
    _L1_gnn_in = {k: v for k, v in _L1_gnn_all.items() if k in ('W_in', 'b_in', 'router_W', 'router_b', 'weak_W', 'weak_b', 'strong_W1', 'strong_b1', 'strong_W2', 'strong_b2', 'conf_W', 'conf_b', 'W_out', 'b_out')}
    del _L1_gnn_all

    def _L2_gnn_setup():
        import jax, jax.numpy as jnp
        import numpy as np
        N_NODES = 3125
        N_EDGES = 50000
        IN_FEAT = 128
        OUT_FEAT = 128
        key = jax.random.key(seed)
        ks = jax.random.split(key, 9)
        s = 1.0 / np.sqrt(IN_FEAT)
        return {'x': jax.random.normal(ks[0], (N_NODES, IN_FEAT), dtype=jnp.float32), 'src': jax.random.randint(ks[1], (N_EDGES,), 0, N_NODES), 'dst': jax.random.randint(ks[2], (N_EDGES,), 0, N_NODES), 'W1': jax.random.uniform(ks[3], (IN_FEAT, OUT_FEAT), jnp.float32, -s, s), 'b1': jax.random.uniform(ks[4], (OUT_FEAT,), jnp.float32, -s, s), 'W2': jax.random.uniform(ks[5], (OUT_FEAT, 1), jnp.float32, -s, s), 'b2': jax.random.uniform(ks[6], (1,), jnp.float32, -s, s), 'W4': jax.random.uniform(ks[7], (IN_FEAT, OUT_FEAT), jnp.float32, -s, s), 'b4': jax.random.uniform(ks[8], (OUT_FEAT,), jnp.float32, -s, s)}
    _L2_gnn_all = _L2_gnn_setup()
    _L2_gnn_in = {k: v for k, v in _L2_gnn_all.items() if k in ('W1', 'b1', 'W2', 'b2', 'W4', 'b4')}
    del _L2_gnn_all

    def _L3_gnn_setup():
        import jax, jax.numpy as jnp
        import numpy as np
        EPS = 1e-12
        NUM_LAYERS = 3

        def _l2norm(v):
            n = jnp.linalg.norm(v, axis=-1, keepdims=True)
            return v / jnp.maximum(n, EPS)
        key = jax.random.key(seed)
        ks = jax.random.split(key, 6)
        N, E, D = (6250, 625000, 128)
        x = jax.random.normal(ks[0], (N, D), dtype=jnp.float32)
        edge_index = jax.random.randint(ks[1], (2, E), 0, N, dtype=jnp.int64)
        Wl = jax.random.normal(ks[2], (NUM_LAYERS, D, D), dtype=jnp.float32) * 0.05
        bl = jax.random.normal(ks[3], (NUM_LAYERS, D), dtype=jnp.float32) * 0.05
        Wr = jax.random.normal(ks[4], (NUM_LAYERS, D, D), dtype=jnp.float32) * 0.05
        return {'x': x, 'edge_index': edge_index, 'Wl': Wl, 'bl': bl, 'Wr': Wr}
    _L3_gnn_all = _L3_gnn_setup()
    _L3_gnn_in = {k: v for k, v in _L3_gnn_all.items() if k in ('Wl', 'bl', 'Wr')}
    del _L3_gnn_all
    return {'x': x, 'src': src, 'dst': dst, 'edge_type_500': edge_type_500, 'L0_gnn_rel_emb': _L0_gnn_in['rel_emb'], 'L0_gnn_W_neighbor': _L0_gnn_in['W_neighbor'], 'L0_gnn_loop_weight': _L0_gnn_in['loop_weight'], 'L1_gnn_W_in': _L1_gnn_in['W_in'], 'L1_gnn_b_in': _L1_gnn_in['b_in'], 'L1_gnn_router_W': _L1_gnn_in['router_W'], 'L1_gnn_router_b': _L1_gnn_in['router_b'], 'L1_gnn_weak_W': _L1_gnn_in['weak_W'], 'L1_gnn_weak_b': _L1_gnn_in['weak_b'], 'L1_gnn_strong_W1': _L1_gnn_in['strong_W1'], 'L1_gnn_strong_b1': _L1_gnn_in['strong_b1'], 'L1_gnn_strong_W2': _L1_gnn_in['strong_W2'], 'L1_gnn_strong_b2': _L1_gnn_in['strong_b2'], 'L1_gnn_conf_W': _L1_gnn_in['conf_W'], 'L1_gnn_conf_b': _L1_gnn_in['conf_b'], 'L1_gnn_W_out': _L1_gnn_in['W_out'], 'L1_gnn_b_out': _L1_gnn_in['b_out'], 'L2_gnn_W1': _L2_gnn_in['W1'], 'L2_gnn_b1': _L2_gnn_in['b1'], 'L2_gnn_W2': _L2_gnn_in['W2'], 'L2_gnn_b2': _L2_gnn_in['b2'], 'L2_gnn_W4': _L2_gnn_in['W4'], 'L2_gnn_b4': _L2_gnn_in['b4'], 'L3_gnn_Wl': _L3_gnn_in['Wl'], 'L3_gnn_bl': _L3_gnn_in['bl'], 'L3_gnn_Wr': _L3_gnn_in['Wr']}

def reference(x, src, dst, edge_type_500, L0_gnn_rel_emb, L0_gnn_W_neighbor, L0_gnn_loop_weight, L1_gnn_W_in, L1_gnn_b_in, L1_gnn_router_W, L1_gnn_router_b, L1_gnn_weak_W, L1_gnn_weak_b, L1_gnn_strong_W1, L1_gnn_strong_b1, L1_gnn_strong_W2, L1_gnn_strong_b2, L1_gnn_conf_W, L1_gnn_conf_b, L1_gnn_W_out, L1_gnn_b_out, L2_gnn_W1, L2_gnn_b1, L2_gnn_W2, L2_gnn_b2, L2_gnn_W4, L2_gnn_b4, L3_gnn_Wl, L3_gnn_bl, L3_gnn_Wr):
    import jax
    import jax.numpy as jnp

    def _L0_gnn_ref(h, norm, rel_emb, W_neighbor, loop_weight, edge_src, edge_dst, edge_type):
        import jax, jax.numpy as jnp
        import numpy as np
        N_NODES = 3125
        N_EDGES = 37500
        N_RELS = 500
        D = 128
        loop_message = h @ loop_weight
        relation = rel_emb[edge_type]
        node = h[edge_src]
        msg = (node + relation) @ W_neighbor
        agg = jax.ops.segment_sum(msg, edge_dst, num_segments=h.shape[0])
        node_repr = agg * norm
        node_repr = jax.nn.relu(node_repr + loop_message)
        return node_repr

    def _L1_gnn_ref(x, edge_index, W_in, b_in, router_W, router_b, weak_W, weak_b, strong_W1, strong_b1, strong_W2, strong_b2, conf_W, conf_b, W_out, b_out):
        import jax, jax.numpy as jnp
        import numpy as np
        TOPK = 2
        N = x.shape[0]
        L = router_W.shape[0]
        src = edge_index[0]
        dst = edge_index[1]
        deg = jax.ops.segment_sum(jnp.ones(src.shape, x.dtype), dst, num_segments=N)
        deg = jnp.clip(deg, 1.0)[:, None]
        h = x @ W_in + b_in
        rows = jnp.arange(N)[:, None]
        for l in range(L):
            agg = jax.ops.segment_sum(h[src], dst, num_segments=N) / deg
            logits = jnp.concatenate([h, agg], axis=-1) @ router_W[l] + router_b[l]
            vals, idx = jax.lax.top_k(logits, TOPK)
            gates = jax.nn.softmax(vals, axis=-1)
            gate_dense = jnp.zeros_like(logits).at[rows, idx].set(gates)
            weak = jax.nn.relu(jnp.einsum('nh,ehf->nef', agg, weak_W[l]) + weak_b[l])
            sh = jax.nn.relu(jnp.einsum('nh,ehf->nef', agg, strong_W1[l]) + strong_b1[l])
            strong = jnp.einsum('nef,efh->neh', sh, strong_W2[l]) + strong_b2[l]
            experts = jnp.concatenate([weak, strong], axis=1)
            moe = jnp.einsum('ne,neh->nh', gate_dense, experts)
            conf = jax.nn.sigmoid(h @ conf_W[l] + conf_b[l])
            h = h + conf * moe
        return h @ W_out + b_out

    def _L2_gnn_ref(x, src, dst, W1, b1, W2, b2, W4, b4):
        import jax, jax.numpy as jnp
        import numpy as np
        N_NODES = 3125
        N_EDGES = 50000
        IN_FEAT = 128
        OUT_FEAT = 128
        n_nodes = x.shape[0]
        theta = x[dst] - x[src]
        w = jax.nn.sigmoid(jax.nn.relu(theta @ W1 + b1) @ W2 + b2)
        w_theta = w * theta
        agg = jax.ops.segment_sum(w_theta, dst, num_segments=n_nodes)
        indeg = jax.ops.segment_sum(jnp.ones((dst.shape[0], 1), x.dtype), dst, num_segments=n_nodes)
        return agg + indeg * (x @ W4 + b4)

    def _L3_gnn_ref(x, edge_index, Wl, bl, Wr):
        import jax, jax.numpy as jnp
        import numpy as np
        EPS = 1e-12
        NUM_LAYERS = 3

        def _l2norm(v):
            n = jnp.linalg.norm(v, axis=-1, keepdims=True)
            return v / jnp.maximum(n, EPS)
        N = x.shape[0]
        src = edge_index[0]
        dst = edge_index[1]
        ones = jnp.ones((dst.shape[0], 1), dtype=x.dtype)
        cnt = jax.ops.segment_sum(ones, dst, num_segments=N)
        denom = jnp.maximum(cnt, 1.0)
        for i in range(NUM_LAYERS):
            msg = x[src]
            agg = jax.ops.segment_sum(msg, dst, num_segments=N) / denom
            agg = _l2norm(agg)
            out = agg @ Wl[i].T + bl[i]
            out = out + _l2norm(x) @ Wr[i].T
            x = jax.nn.relu(out) if i != NUM_LAYERS - 1 else out
        return x
    edge_index = jnp.stack([src, dst])
    deg = jnp.maximum(jax.ops.segment_sum(jnp.ones(dst.shape, jnp.float32), dst, num_segments=6250), 1.0)
    deg_isqrt = deg ** (-0.5)
    h = jnp.maximum(_layernorm(x, axis=-1), 0.0)
    x = x + _L0_gnn_ref(h, deg_isqrt[:, None], L0_gnn_rel_emb, L0_gnn_W_neighbor, L0_gnn_loop_weight, src, dst, edge_type_500)
    h = jnp.maximum(_layernorm(x, axis=-1), 0.0)
    x = x + _L1_gnn_ref(h, edge_index, L1_gnn_W_in, L1_gnn_b_in, L1_gnn_router_W, L1_gnn_router_b, L1_gnn_weak_W, L1_gnn_weak_b, L1_gnn_strong_W1, L1_gnn_strong_b1, L1_gnn_strong_W2, L1_gnn_strong_b2, L1_gnn_conf_W, L1_gnn_conf_b, L1_gnn_W_out, L1_gnn_b_out)
    h = jnp.maximum(_layernorm(x, axis=-1), 0.0)
    x = x + _L2_gnn_ref(h, src, dst, L2_gnn_W1, L2_gnn_b1, L2_gnn_W2, L2_gnn_b2, L2_gnn_W4, L2_gnn_b4)
    h = jnp.maximum(_layernorm(x, axis=-1), 0.0)
    x = x + _L3_gnn_ref(h, edge_index, L3_gnn_Wl, L3_gnn_bl, L3_gnn_Wr)
    return x

_drawn_inputs = setup_inputs


def setup_inputs(seed=0):
    import zlib

    import numpy as np

    out = dict(_drawn_inputs(seed))
    spreads = {'L1_gnn_b_in': (0.0, 0.1),
     'L1_gnn_router_b': (0.0, 0.1),
     'L1_gnn_weak_b': (0.0, 0.328),
     'L1_gnn_strong_b1': (0.0, 0.391),
     'L1_gnn_strong_b2': (0.0, 0.333),
     'L1_gnn_conf_b': (0.0, 0.567),
     'L1_gnn_b_out': (0.0, 0.1)}
    factors = {'L2_gnn_W1': 3.103,
     'L2_gnn_b1': 28.223,
     'L3_gnn_Wl': 8.0,
     'L3_gnn_bl': 8.0,
     'L3_gnn_Wr': 8.0}
    for name, (base, spread) in spreads.items():
        noise = np.random.default_rng([zlib.crc32(name.encode()), seed]).standard_normal(out[name].shape)
        drawn = base * np.exp(spread * noise) if base else spread * noise
        out[name] = jnp.asarray(drawn.astype(out[name].dtype))
    for name, factor in factors.items():
        out[name] = (out[name] * factor).astype(out[name].dtype)
    return out
```

```python
import concourse.bass as bass
from concourse import mybir
from contextlib import ExitStack, contextmanager

N = 6250
E = 106250
D = 128
H = 256
P = 128
RELS = 500
LAYERS = 3
NE = 8
NW = 4

RING = 16
HALF = RING // 2
QUAD = HALF // 2
BANKS = 4
TILES = -(-E // P)
STEPS = -(-TILES // RING)
TROWS = -(-TILES // P)
TCOLS = TROWS * P
NB = 50
NPAD = NB * P
NPAIR = NB // 2
LAST = N // P
LASTN = N - LAST * P
SPARE = NPAD - P
LN_EPS = 1e-5
L2_EPS = 1e-12
TINY = 1e-35

FP = mybir.dt.float32
I32 = mybir.dt.int32
U32 = mybir.dt.uint32
ALU = mybir.AluOpType
ACT = mybir.ActivationFunctionType
AX = mybir.AxisListType


@contextmanager
def phase(nc, bank, *names, pool_dmas=()):
    assert len(names) <= len(bank)
    with nc.Block() as block:
        yield block, bank[:len(names)]
    if pool_dmas:
        numbers = range(pool_dmas[0].num, pool_dmas[-1].num + 1)
        nc.gpsimd.dma_reset(numbers)
        nc.all_engine_barrier(sems_to_clear=numbers)
    nc.all_engine_barrier(sems_to_clear=range(bank[0].num, bank[-1].num + 1))


class Chain:

    def __init__(self, eng, sem):
        self.eng, self.sem, self.n = eng, sem, 0

    def loop(self, i, per_iteration):
        self.n = self.n + i * per_iteration

    def __call__(self, ins):
        self.n = self.n + 1
        ins.then_inc(self.sem, 1)
        self.eng.wait_ge(self.sem, self.n)


def gnn_kernel(nc, t, out):
    ctx = ExitStack()
    with ctx:
        def sb(name, shape, dt=FP):
            return ctx.enter_context(nc.sbuf_tensor(name, shape, dt))

        def ps(name, shape, dt=FP):
            return ctx.enter_context(nc.psum_tensor(name, shape, dt))

        def dram(name, shape, dt=FP):
            return nc.dram_tensor(name, shape, dt, kind="Internal").ap()

        rows128 = dram("rows128", [NPAD, D])
        rows256 = dram("rows256", [NPAD, H])
        rel_rows = dram("rel_rows", [TCOLS, P])
        win_dram = dram("win_dram", [TROWS, P], I32)
        x_dram = dram("x_dram", [P, NB * D])
        rdeg_dram = dram("rdeg_dram", [P, NPAD])

        feat = sb("feat", [P, 2, NPAD])
        acc = sb("acc", [P, 2, NPAD])
        big = sb("big", [P, 10240])
        src_idx = sb("src_idx", [P, TCOLS], I32)
        type_idx = sb("type_idx", [P, TCOLS], I32)
        rel = sb("rel", [P, TCOLS])
        win_base = sb("win_base", [1, TCOLS], I32)
        win = sb("win", [1, TCOLS], I32)
        more = sb("more", [1, 1], I32)
        iota_row0 = sb("iota_row0", [P, P])
        iota_col0 = sb("iota_col0", [P, 1])
        iota_row = sb("iota_row", [P, P])
        iota_col = sb("iota_col", [P, 1])
        ident = sb("ident", [P, P])
        neg_ident = sb("neg_ident", [P, P])
        ones = sb("ones", [P, P])
        mean_col = sb("mean_col", [P, 1])
        node_norm = sb("node_norm", [P, NB])
        node_rdeg = sb("node_rdeg", [P, NB])
        node_deg = sb("node_deg", [P, NB])
        x_nodes = big[:, 0:NB * D].rearrange("p (b d) -> p b d", d=D)

        bank = [ctx.enter_context(nc.semaphore(f"signal{k}")) for k in range(32)]
        gathered = [ctx.enter_context(nc.semaphore(f"gathered{k}")) for k in range(RING)]
        gathered2 = [ctx.enter_context(nc.semaphore(f"second{k}")) for k in range(RING)]
        for some in (bank, gathered + gathered2):
            assert [s.num for s in some] == list(range(some[0].num, some[0].num + len(some)))
        uses = [0]

        def sbuf(name, shape, dt):
            uses[0] += 1
            return nc.sbuf_tensor(f"{name}_{uses[0]}", shape, dt)

        def psum(name, shape, dt):
            uses[0] += 1
            return nc.psum_tensor(f"{name}_{uses[0]}", shape, dt)

        with ExitStack() as tmp:
            ip = tmp.enter_context(psum("setup_ps", [P, 8, 512], FP))
            stage = acc[:, :, :].rearrange("p a n -> p (a n)")
            irow = [stage[:, k * TCOLS:(k + 1) * TCOLS].bitcast(I32) for k in range(3)]
            frow = [stage[:, (3 + k) * TCOLS:(4 + k) * TCOLS] for k in range(3)]
            least = stage[:, 6 * TCOLS:6 * TCOLS + TROWS]
            most = stage[:, 6 * TCOLS + 8:6 * TCOLS + 8 + TROWS]
            span = stage[:, 6 * TCOLS + 16:6 * TCOLS + 17]
            spanr = stage[0:1, 6 * TCOLS + 20:6 * TCOLS + 21]
            spani = stage[0:1, 6 * TCOLS + 24:6 * TCOLS + 25].bitcast(I32)
            wini = stage[0:TROWS, 6 * TCOLS + 32:6 * TCOLS + 32 + P].bitcast(I32)
            full = (TROWS - 1) * P * P
            rest = (E - full) // P
            tail = E - full - rest * P
            with phase(nc, bank, "zeroed", "loaded", "filled", "pool_own", "consts", "dve_own", "masked",
                       "transposed", "spilled", "wrote", "win_loaded", "x_loaded", "xz") as (block, sems):
                (zeroed, loaded, filled, pool_own, consts, dve_own, masked,
                 transposed, spilled, wrote, win_loaded, x_loaded, xz) = sems

                @block.sync
                def _(sp):
                    names = (t["src"], t["dst"], t["edge_type_500"])
                    for k, a in enumerate(names):
                        sp.dma_start(irow[k][:, 0:full // P].rearrange("p (a j) -> p a j", j=P),
                                     a[0:full].rearrange("(a p j) -> p a j", p=P, j=P)).then_inc(loaded, 16)
                    sp.dma_start(irow[1][:, full // P:TCOLS],
                                 a_row(names[1], E - P).to_broadcast((P, P))).then_inc(filled, 16)
                    sp.wait_ge(filled, 16)
                    sp.wait_ge(zeroed, 1)
                    for k, a in enumerate(names):
                        sp.dma_start(irow[k][0:rest, full // P:TCOLS],
                                     a[full:full + rest * P].rearrange("(p j) -> p j", j=P)).then_inc(loaded, 16)
                        sp.dma_start(irow[k][rest:rest + 1, full // P:full // P + tail],
                                     a[E - tail:E].rearrange("(p j) -> p j", p=1)).then_inc(loaded, 16)
                    sp.wait_ge(xz, 1)
                    sp.dma_start(x_nodes[:, 0:LAST, :],
                                 t["x"][0:LAST * P, :].rearrange("(b p) d -> p b d", p=P)).then_inc(x_loaded, 16)
                    sp.dma_start(x_nodes[0:LASTN, LAST, :], t["x"][LAST * P:N, :]).then_inc(x_loaded, 16)
                    sp.wait_ge(masked, 1)
                    sp.dma_start(rel_rows.rearrange("(a p) j -> p a j", p=P),
                                 frow[1].rearrange("p (a j) -> p a j", j=P)).then_inc(wrote, 16)
                    sp.wait_ge(spilled, 5)
                    sp.dma_start(win_dram, wini).then_inc(win_loaded, 16)
                    sp.wait_ge(win_loaded, 16)
                    sp.dma_start(win_base[0:1, :], win_dram.rearrange("a p -> (a p)").rearrange("(o n) -> o n", o=1)
                                 ).then_inc(win_loaded, 16)
                    sp.wait_ge(win_loaded, 32)
                    sp.wait_ge(wrote, 16)
                    sp.wait_ge(x_loaded, 32)

                @block.gpsimd
                def _(pool):
                    nc.gpsimd.memset(irow[0][:, full // P:TCOLS], 0)
                    nc.gpsimd.memset(irow[2][:, full // P:TCOLS], 0).then_inc(zeroed, 1)
                    nc.gpsimd.memset(ident[:, :], 0.0).then_inc(pool_own, 1)
                    nc.gpsimd.iota(iota_row0[:, :], pattern=[[1, P]], base=0, channel_multiplier=0,
                                   allow_small_or_imprecise_dtypes=True)
                    nc.gpsimd.iota(iota_col0[:, :], pattern=[[1, 1]], base=0, channel_multiplier=1,
                                   allow_small_or_imprecise_dtypes=True)
                    nc.gpsimd.memset(ones[:, :], 1.0)
                    nc.gpsimd.memset(mean_col[:, :], 1.0 / P)
                    pool.wait_ge(pool_own, 1)
                    nc.gpsimd.affine_select(out=ident[:, :], in_=ident[:, :], compare_op=ALU.not_equal, fill=1.0,
                                            base=0, pattern=[[-1, P]], channel_multiplier=1).then_inc(consts, 1)
                    pool.wait_ge(dve_own, 6)
                    nc.gpsimd.affine_select(out=frow[1].rearrange("p (a j) -> p a j", j=P),
                                            in_=frow[1].rearrange("p (a j) -> p a j", j=P),
                                            compare_op=ALU.is_ge, fill=-1.0, base=E - 1,
                                            pattern=[[-P * P, TROWS], [-1, P]],
                                            channel_multiplier=-P).then_inc(masked, 1)

                @block.vector
                def _(dve):
                    own = Chain(dve, dve_own)
                    nc.vector.memset(x_nodes[:, LAST:NB, :], 0.0).then_inc(xz, 1)
                    dve.wait_ge(loaded, 16 * 9)
                    own(nc.vector.tensor_copy(frow[0], irow[0]))
                    own(nc.vector.tensor_copy(frow[2], irow[2]))
                    own(nc.vector.tensor_copy(frow[1], irow[1]))
                    v = frow[1].rearrange("p (a j) -> p a j", j=P)
                    own(nc.vector.tensor_reduce(least, v, AX.X, ALU.min))
                    own(nc.vector.tensor_reduce(most, v, AX.X, ALU.max))
                    own(nc.vector.tensor_tensor(v, v, least.unsqueeze(2).to_broadcast([P, TROWS, P]), ALU.subtract))
                    own(nc.vector.tensor_tensor(most, most, least, ALU.subtract))
                    own(nc.vector.tensor_reduce(span, most, AX.X, ALU.max))
                    dve.wait_ge(consts, 1)
                    own(nc.vector.tensor_scalar(neg_ident[:, :], ident[:, :], -1.0, None, ALU.mult))
                    dve.wait_ge(transposed, 1)
                    for g in range(2):
                        n = min(4, TROWS - 4 * g)
                        src = ip[:, g, 0:n * P]
                        nc.vector.tensor_copy(src_idx[:, 4 * g * P:(4 * g + n) * P], src)
                        nc.vector.tensor_copy(type_idx[:, 4 * g * P:(4 * g + n) * P], ip[:, 4 + g, 0:n * P])
                        last = nc.vector.tensor_copy(rel[:, 4 * g * P:(4 * g + n) * P], ip[:, 2 + g, 0:n * P])
                        last.then_inc(spilled, 1)
                    nc.vector.tensor_copy(wini, ip[0:TROWS, 6, 0:P]).then_inc(spilled, 1)
                    own(nc.vector.tensor_reduce(spanr, ip[0:1, 7, 0:P], AX.X, ALU.max))
                    own(nc.vector.tensor_copy(spani, spanr))
                    nc.vector.tensor_scalar(more[0:1, 0:1], spani, 7, None, ALU.logical_shift_right).then_inc(spilled, 2)

                @block.tensor
                def _(pe):
                    pe.wait_ge(consts, 1)
                    pe.wait_ge(masked, 1)
                    pe.wait_ge(dve_own, 8)
                    for k, f in enumerate((frow[0], frow[1], frow[2])):
                        for a in range(TROWS):
                            nc.tensor.transpose(ip[:, 2 * k + a // 4, (a % 4) * P:(a % 4 + 1) * P],
                                                f[:, a * P:(a + 1) * P], ident[:, :])
                    nc.tensor.transpose(ip[0:TROWS, 6, 0:P], least, ident[:, :])
                    nc.tensor.transpose(ip[0:1, 7, 0:P], span, ident[:, :]).then_inc(transposed, 1)

        def start_pass():
            with phase(nc, bank, "z") as (block, (z,)):
                @block.vector
                def _(dve):
                    nc.vector.memset(acc[:, 0, :], 0.0)
                    nc.vector.tensor_copy(win[0:1, :], win_base[0:1, :])
                    nc.vector.tensor_copy(iota_row[:, :], iota_row0[:, :])
                    nc.vector.tensor_copy(iota_col[:, :], iota_col0[:, :])

                @block.gpsimd
                def _(pool):
                    nc.gpsimd.memset(acc[:, 1, :], 0.0)

        def next_round():
            with phase(nc, bank, "z") as (block, (z,)):
                @block.vector
                def _(dve):
                    nc.vector.tensor_scalar(iota_row[:, :], iota_row[:, :], float(P), None, ALU.add)
                    nc.vector.tensor_scalar(iota_col[:, :], iota_col[:, :], float(P), None, ALU.add)
                    nc.vector.tensor_scalar(win[0:1, :], win[0:1, :], P, SPARE, ALU.add, ALU.min)

        def gather_pass(table, width, second=None, edge_net=None):
            start_pass()
            rounds = nc.values_load(more[0:1, 0:1], min_val=0, max_val=NPAD // P) + 1
            with nc.Fori(0, rounds), ExitStack() as tmp:
                ring = tmp.enter_context(sbuf("ring", [P, RING, H], FP))
                onehot = tmp.enter_context(sbuf("onehot", [P, 2, HALF, P], FP))
                idx = tmp.enter_context(sbuf("idx", [P, 2, 2, HALF], I32))
                sums = tmp.enter_context(psum("sums", [P, BANKS, 512], FP))
                names = ["idx_ready", "onehot_ready", "tile_done", "added"]
                if edge_net:
                    (y_w1, b1, w2, b2) = edge_net
                    spare1, spare2 = feat[:, 1, :], big[:, NB * D:]
                    half_cols = HALF * P
                    ywin = spare1[:, 0:RING * D].rearrange("p (k d) -> p k d", d=D)
                    relb = spare1[:, RING * D:RING * D + 2 * half_cols].rearrange("p (h j) -> p h j", h=2)
                    onehot_t = spare1[:, RING * D + 2 * half_cols:RING * D + 4 * half_cols].rearrange(
                        "p (h j) -> p h j", h=2)
                    hidden = spare2[:, 0:half_cols].rearrange("p (c j) -> p c j", j=P)
                    onehot_w = spare2[:, half_cols:2 * half_cols].rearrange("p (c j) -> p c j", j=P)
                    weight = tmp.enter_context(sbuf("weight", [P, HALF], FP))
                    zt = tmp.enter_context(psum("zt", [P, 2, QUAD, P], FP))
                    dot = tmp.enter_context(psum("dot", [P, 2, 512], FP))
                    names += ["rel_loaded0", "rel_loaded1", "z_done", "relu_done", "dot_done", "weight_done",
                              "weighted"] + [f"ywin{k}" for k in range(RING)]
                with phase(nc, bank, *names, pool_dmas=gathered + gathered2) as (block, sems):
                    idx_ready, onehot_ready, tile_done, added = sems[:4]
                    if edge_net:
                        rel_loaded = sems[4:6]
                        z_done, relu_done, dot_done, weight_done, weighted = sems[6:11]
                        ywin_loaded = sems[11:]

                    @block.gpsimd
                    def _(pool):
                        with pool.Fori(0, STEPS) as i:
                            for k in range(RING):
                                h, c = divmod(k, HALF)
                                if c == 0:
                                    pool.wait_ge(idx_ready, i * 2 + (h + 1))
                                pool.wait_ge(tile_done, i * RING + (k + 1))
                                pool.nop(nofuse=True)
                                nc.gpsimd.indirect_dma_start(
                                    ring[:, k, 0:width], None, table,
                                    bass.IndirectOffsetOnAxis(ap=idx[:, h, 0, c:c + 1].bitcast(U32), axis=0),
                                ).then_inc(gathered[k], 16)
                                if second is not None:
                                    nc.gpsimd.indirect_dma_start(
                                        ring[:, k, width:2 * width], None, second,
                                        bass.IndirectOffsetOnAxis(ap=idx[:, h, 1, c:c + 1].bitcast(U32), axis=0),
                                    ).then_inc(gathered2[k], 16)

                    @block.scalar
                    def _(act):
                        def stage_idx(i, h):
                            act.wait_ge(tile_done, i * RING + HALF * (h + 1))
                            last = nc.scalar.copy(idx[:, h, 0, :], src_idx[:, bass.ds(i * RING + h * HALF, HALF)])
                            if second is not None:
                                last = nc.scalar.copy(idx[:, h, 1, :], type_idx[:, bass.ds(i * RING + h * HALF, HALF)])
                            last.then_inc(idx_ready, 1)

                        with act.Fori(0, STEPS) as i:
                            for h in range(2):
                                stage_idx(i, h)
                                if edge_net:
                                    for q in range(2):
                                        act.wait_ge(z_done, i * 4 + (2 * h + q + 1))
                                        nc.scalar.activation(hidden[:, q * QUAD:(q + 1) * QUAD, :], zt[:, q, :, :],
                                                             ACT.Relu, bias=b1).then_inc(relu_done, 1)
                                    for q in range(2):
                                        act.wait_ge(dot_done, i * 4 + (2 * h + q + 1))
                                        nc.scalar.activation(weight[:, q * QUAD:(q + 1) * QUAD], dot[:, q, 0:QUAD],
                                                             ACT.Sigmoid, bias=b2).then_inc(weight_done, 1)

                    @block.sync
                    def _(sp):
                        def load_rel(i, h):
                            sp.wait_ge(tile_done, i * RING + HALF * (h + 1))
                            sp.dma_start(relb[:, h, :].rearrange("p (c j) -> p c j", j=P),
                                         bcast_rows(rel_rows, i * RING + h * HALF, HALF)
                                         ).then_inc(rel_loaded[h], 16)

                        if edge_net:
                            with sp.Fori(0, STEPS) as i:
                                for h in range(2):
                                    load_rel(i, h)
                                    for c in range(HALF):
                                        k = h * HALF + c
                                        w = sp.value_load(win[0:1, bass.ds(i * RING + k, 1)], min_val=0, max_val=SPARE)
                                        sp.dma_start(ywin[:, k, :], y_w1[bass.ds(w, P), 0:D]
                                                     ).then_inc(ywin_loaded[k], 16)
                            load_rel(STEPS, 0)

                    @block.vector
                    def _(dve):
                        def one_hots(i, h):
                            dve.wait_ge(tile_done, i * RING + HALF * (h + 1))
                            if edge_net:
                                dve.wait_ge(rel_loaded[h], i * 16 + 16)
                                nc.vector.tensor_scalar(onehot_t[:, h, :], relb[:, h, :], iota_col[:, 0:1], None,
                                                        ALU.is_equal)
                            nc.vector.tensor_tensor(
                                onehot[:, h, :, :],
                                iota_row[:, :].unsqueeze(1).to_broadcast([P, HALF, P]),
                                rel[:, bass.ds(i * RING + h * HALF, HALF)].unsqueeze(2).to_broadcast([P, HALF, P]),
                                ALU.is_equal).then_inc(onehot_ready, 1)

                        def add_tiles(i, h):
                            if edge_net:
                                dve.wait_ge(tile_done, i * RING + HALF * (h + 2))
                                for q in range(2):
                                    dve.wait_ge(weight_done, i * 4 + (2 * h + q + 1))
                                    quad = slice(q * QUAD, (q + 1) * QUAD)
                                    nc.vector.tensor_tensor(
                                        onehot_w[:, quad, :], onehot[:, h, quad, :],
                                        weight[:, quad].unsqueeze(2).to_broadcast([P, QUAD, P]),
                                        ALU.mult).then_inc(weighted, 1)
                            for c in range(HALF):
                                k = h * HALF + c
                                w = dve.value_load(win[0:1, bass.ds(i * RING + k, 1)], min_val=0, max_val=SPARE)
                                dve.wait_ge(tile_done, i * RING + (k + 1 + RING))
                                dve.wait_ge(added, i * RING + (k + BANKS))
                                n = 1 if (width == D and second is None and not edge_net) else 2
                                nc.vector.tensor_tensor(
                                    acc[:, 0:n, bass.ds(w, P)], acc[:, 0:n, bass.ds(w, P)],
                                    sums[:, k % BANKS, 0:n * P].rearrange("p (a j) -> p a j", j=P), ALU.add).then_inc(added, 1)

                        dve.sem_inc(added, BANKS)
                        one_hots(0, 0)
                        with dve.Fori(0, STEPS) as i:
                            one_hots(i, 1)
                            add_tiles(i, 0)
                            if not edge_net:
                                one_hots(i + 1, 0)
                            add_tiles(i, 1)
                            if edge_net:
                                one_hots(i + 1, 0)

                    @block.tensor
                    def _(pe):
                        pe.sem_inc(tile_done, RING)
                        with pe.Fori(0, STEPS) as i:
                            for h in range(2):
                                pe.wait_ge(onehot_ready, i * 2 + (h + 1))
                                if edge_net:
                                    for c in range(HALF):
                                        k = h * HALF + c
                                        pe.wait_ge(gathered[k], i * 16 + 16)
                                        pe.wait_ge(ywin_loaded[k], i * 16 + 16)
                                        q, j = divmod(c, QUAD)
                                        nc.tensor.matmul(zt[:, q, j, :], ring[:, k, 0:D], neg_ident[:, :], start=True,
                                                         stop=False)
                                        last = nc.tensor.matmul(zt[:, q, j, :], ywin[:, k, :],
                                                                onehot_t[:, h, c * P:(c + 1) * P], start=False, stop=True)
                                        if j == QUAD - 1:
                                            last.then_inc(z_done, 1)
                                    for c in range(HALF):
                                        q, j = divmod(c, QUAD)
                                        if j == 0:
                                            pe.wait_ge(relu_done, i * 4 + (2 * h + q + 1))
                                        last = nc.tensor.matmul(dot[:, q, j:j + 1], hidden[:, c, :], w2, start=True,
                                                                stop=True)
                                        if j == QUAD - 1:
                                            last.then_inc(dot_done, 1)
                                for c in range(HALF):
                                    k = h * HALF + c
                                    if not edge_net:
                                        pe.wait_ge(gathered[k], i * 16 + 16)
                                    if second is not None:
                                        pe.wait_ge(gathered2[k], i * 16 + 16)
                                    pe.wait_ge(added, i * RING + (k + 1))
                                    if edge_net:
                                        pe.wait_ge(weighted, i * 4 + (2 * h + c // QUAD + 1))
                                        nc.tensor.matmul(sums[:, k % BANKS, 0:P], ring[:, k, D:2 * D], onehot_w[:, c, :],
                                                         start=True, stop=True)
                                        last = nc.tensor.matmul(sums[:, k % BANKS, P:2 * P], ones[:, :], onehot_w[:, c, :],
                                                                start=True, stop=True)
                                    elif second is not None:
                                        nc.tensor.matmul(sums[:, k % BANKS, 0:P], ring[:, k, 0:D], onehot[:, h, c, :],
                                                         start=True, stop=False)
                                        nc.tensor.matmul(sums[:, k % BANKS, 0:P], ring[:, k, D:2 * D], onehot[:, h, c, :],
                                                         start=False, stop=True)
                                        last = nc.tensor.matmul(sums[:, k % BANKS, P:2 * P], ones[:, :], onehot[:, h, c, :],
                                                                start=True, stop=True)
                                    else:
                                        for a in range(width // D):
                                            last = nc.tensor.matmul(sums[:, k % BANKS, a * P:(a + 1) * P],
                                                                    ring[:, k, a * D:(a + 1) * D], onehot[:, h, c, :],
                                                                    start=True, stop=True)
                                    last.then_inc(tile_done, 1)
                next_round()

        def degrees():
            with ExitStack() as tmp:
                dstage = tmp.enter_context(sbuf("dstage", [P, 2, P], FP))
                dps = tmp.enter_context(psum("dps", [P, NB], FP))
                with phase(nc, bank, "staged", "done", "own", "root", "rd", "stored") as (block, (staged, done, own_s, root, rd, stored)):
                    @block.scalar
                    def _(act):
                        with act.Fori(0, NPAIR) as i:
                            for u in range(2):
                                act.wait_ge(done, i * 2 + (u + 1))
                                nc.scalar.copy(dstage[:, u, :], acc[:, 1, bass.ds((i * 2 + u) * P, P)]).then_inc(staged, 1)
                        act.wait_ge(own_s, 2)
                        nc.scalar.activation(node_norm[:, :], node_rdeg[:, :], ACT.Sqrt).then_inc(root, 1)

                    @block.tensor
                    def _(pe):
                        pe.sem_inc(done, 2)
                        with pe.Fori(0, NPAIR) as i:
                            for u in range(2):
                                pe.wait_ge(staged, i * 2 + (u + 1))
                                nc.tensor.matmul(dps[:, bass.ds(i * 2 + u, 1)], dstage[:, u, :], mean_col[:, :],
                                                 start=True, stop=True).then_inc(done, 1)

                    @block.vector
                    def _(dve):
                        own = Chain(dve, own_s)
                        dve.wait_ge(done, NB + 2)
                        own(nc.vector.tensor_copy(node_deg[:, :], dps[:, :]))
                        own(nc.vector.tensor_scalar(node_rdeg[:, :], node_deg[:, :], 1.0, None, ALU.max))
                        dve.wait_ge(root, 1)
                        own(nc.vector.reciprocal(node_rdeg[:, :], node_rdeg[:, :]))
                        own(nc.vector.reciprocal(node_norm[:, :], node_norm[:, :]))
                        own(nc.vector.tensor_scalar(acc[:, 1, :], acc[:, 1, :], 1.0, None, ALU.max))
                        nc.vector.reciprocal(acc[:, 1, :], acc[:, 1, :]).then_inc(rd, 1)

                    @block.sync
                    def _(sp):
                        sp.wait_ge(rd, 1)
                        sp.dma_start(rdeg_dram, acc[:, 1, :]).then_inc(stored, 16)
                        sp.wait_ge(stored, 16)

        def normalize(kind, w=None, bias=None, bcols=None):
            with ExitStack() as tmp:
                st = tmp.enter_context(sbuf("st", [P, NB, 6], FP))
                col = [tmp.enter_context(sbuf(f"col{k}", [P, NB], FP)) for k in range(4)]
                hs = tmp.enter_context(sbuf("hs", [P, 2, D], FP))
                hts = tmp.enter_context(sbuf("hts", [P, 2, P], FP))
                row = tmp.enter_context(sbuf("row", [P, 2, H], FP))
                pt = tmp.enter_context(psum("pt", [P, 2, 512], FP))
                pw = tmp.enter_context(psum("pw", [P, 2, 512], FP))
                pf = tmp.enter_context(psum("pf", [P, 2, 512], FP))
                with phase(nc, bank, "own_s", "var_s", "root", "scaled", "h_done", "t_done", "ht_done", "w_done",
                           "row_done", "f_done", "spill_done", "out0", "out1") as (block, sems):
                    (own_s, var_s, root, scaled, h_done, t_done, ht_done, w_done, row_done, f_done, spill_done,
                     out0, out1) = sems
                    outs = (out0, out1)
                    rows = hs if kind == "h" else row
                    width = D if kind == "h" else H
                    rows_done = h_done if kind == "h" else row_done
                    table = rows128 if kind == "h" else rows256

                    @block.vector
                    def _(dve):
                        own = Chain(dve, own_s)
                        with dve.Fori(0, NB) as b:
                            nc.vector.bn_stats(st[:, bass.ds(b, 1), :], x_nodes[:, bass.ds(b, 1), :]).then_inc(own_s, 1)
                        dve.wait_ge(own_s, NB)
                        own.n = NB
                        m0, v0, m1, v1 = st[:, :, 1], st[:, :, 2], st[:, :, 4], st[:, :, 5]
                        mean, var, rstd, shift = (c[:, :] for c in col)
                        own(nc.vector.tensor_tensor(mean, m0, m1, ALU.subtract))
                        own(nc.vector.tensor_scalar(mean, mean, 0.5, None, ALU.mult))
                        own(nc.vector.tensor_tensor(rstd, mean, mean, ALU.mult))
                        own(nc.vector.tensor_tensor(var, v0, v1, ALU.add))
                        own(nc.vector.tensor_scalar(var, var, 1.0 / D, LN_EPS, ALU.mult, ALU.add))
                        own(nc.vector.tensor_tensor(var, var, rstd, ALU.add))
                        own(nc.vector.tensor_tensor(mean, m0, m1, ALU.add))
                        nc.vector.tensor_scalar(mean, mean, -0.5, None, ALU.mult).then_inc(var_s, 1)
                        dve.wait_ge(root, 1)
                        own(nc.vector.reciprocal(rstd, rstd))
                        nc.vector.tensor_tensor(shift, mean, rstd, ALU.mult).then_inc(scaled, 1)
                        with dve.Fori(0, NPAIR) as i:
                            for u in range(2):
                                blk = bass.ds((i * 2 + u) * P, P)
                                dve.wait_ge(t_done, i * 2 + (u + 1))
                                if kind != "h":
                                    dve.wait_ge(w_done, i * 2 + (u + 1))
                                    nc.vector.tensor_copy(hts[:, u, :], pt[:, u, 0:P]).then_inc(ht_done, 1)
                                if kind != "h w":
                                    nc.vector.tensor_copy(feat[:, 0, blk], pt[:, u, 0:P]).then_inc(spill_done, 1)
                            for u in range(2):
                                blk = bass.ds((i * 2 + u) * P, P)
                                if kind != "h":
                                    dve.wait_ge(outs[u], i * 16)
                                    dve.wait_ge(w_done, i * 2 + (u + 3))
                                if kind == "h w":
                                    dve.wait_ge(f_done, i * 2 + (u + 1))
                                    nc.vector.tensor_tensor(row[:, u, :], pw[:, u, 0:H], bias, ALU.add).then_inc(row_done, 1)
                                if kind == "y h":
                                    nc.vector.tensor_copy(row[:, u, D:H], hs[:, u, :])
                                    nc.vector.tensor_copy(row[:, u, 0:D], pw[:, u, 0:D]).then_inc(row_done, 1)
                            if kind == "h w":
                                for u in range(2):
                                    dve.wait_ge(f_done, i * 2 + (u + 3))
                                    blk = bass.ds((i * 2 + u) * P, P)
                                    nc.vector.tensor_copy(feat[:, :, blk],
                                                          pf[:, u, 0:H].rearrange("p (a j) -> p a j", j=P)
                                                          ).then_inc(spill_done, 1)

                    @block.scalar
                    def _(act):
                        act.wait_ge(var_s, 1)
                        nc.scalar.activation(col[2][:, :], col[1][:, :], ACT.Sqrt).then_inc(root, 1)
                        act.wait_ge(scaled, 1)
                        with act.Fori(0, NPAIR) as i:
                            for u in range(2):
                                b = bass.ds(i * 2 + u, 1)
                                act.wait_ge(t_done, i * 2)
                                if kind == "h":
                                    act.wait_ge(outs[u], i * 16)
                                elif kind == "y h":
                                    act.wait_ge(row_done, i * 2)
                                nc.scalar.activation(hs[:, u, :], x_nodes[:, b, :].rearrange("p b d -> p (b d)"),
                                                     ACT.Relu, bias=col[3][:, b], scale=col[2][:, b]).then_inc(h_done, 1)

                    @block.tensor
                    def _(pe):
                        pe.sem_inc(w_done, 2)
                        pe.sem_inc(f_done, 2)
                        with pe.Fori(0, NPAIR) as i:
                            for u in range(2):
                                pe.wait_ge(h_done, i * 2 + (u + 1))
                                if kind != "h":
                                    pe.wait_ge(ht_done, i * 2)
                                if kind != "h w":
                                    pe.wait_ge(spill_done, i * 2)
                                nc.tensor.transpose(pt[:, u, 0:P], hs[:, u, :], ident[:, :]).then_inc(t_done, 1)
                            if kind != "h":
                                for u in range(2):
                                    pe.wait_ge(ht_done, i * 2 + (u + 1))
                                    pe.wait_ge(row_done, i * 2)
                                    nc.tensor.matmul(pw[:, u, 0:w.shape[1]], hts[:, u, :], w, start=True,
                                                     stop=True).then_inc(w_done, 1)
                            if kind == "h w":
                                for u in range(2):
                                    pe.wait_ge(row_done, i * 2 + (u + 1))
                                    pe.wait_ge(spill_done, i * 2)
                                    for a in range(2):
                                        last = nc.tensor.transpose(pf[:, u, a * P:(a + 1) * P],
                                                                   row[:, u, a * P:(a + 1) * P], ident[:, :])
                                    last.then_inc(f_done, 1)

                    @block.sync
                    def _(sp):
                        with sp.Fori(0, NPAIR) as i:
                            for u in range(2):
                                sp.wait_ge(rows_done, i * 2 + (u + 1))
                                sp.dma_start(table[bass.ds((i * 2 + u) * P, P), :], rows[:, u, 0:width]
                                             ).then_inc(outs[u], 16)
                        sp.wait_ge(out0, NPAIR * 16)
                        sp.wait_ge(out1, NPAIR * 16)

        def load(pairs):
            with phase(nc, bank, "loaded") as (block, (loaded,)):
                @block.sync
                def _(sp):
                    for dst, src in pairs:
                        sp.dma_start(dst, src).then_inc(loaded, 16)
                    sp.wait_ge(loaded, 16 * len(pairs))

        def layer0_nodes(wn, wl):
            with ExitStack() as tmp:
                st = tmp.enter_context(sbuf("st", [P, 2, 2, P], FP))
                tt = tmp.enter_context(sbuf("tt", [P, 2, D], FP))
                hl = tmp.enter_context(sbuf("hl", [P, 2, D], FP))
                po = tmp.enter_context(psum("po", [P, 2, 512], FP))
                with phase(nc, bank, "staged", "done", "own", "hlc", "updated") as (block, (staged, done, own_s, hlc, updated)):
                    @block.scalar
                    def _(act):
                        with act.Fori(0, NPAIR) as i:
                            for u in range(2):
                                blk = bass.ds((i * 2 + u) * P, P)
                                act.wait_ge(done, i * 2 + (u + 1))
                                nc.scalar.copy(st[:, u, 0, :], acc[:, 0, blk])
                                nc.scalar.copy(st[:, u, 1, :], feat[:, 0, blk]).then_inc(staged, 1)
                            for u in range(2):
                                act.wait_ge(done, i * 2 + (u + 3))
                                act.wait_ge(updated, i * 2 + (u + 1))
                                nc.scalar.copy(hl[:, u, :], po[:, u, D:2 * D]).then_inc(hlc, 1)

                    @block.tensor
                    def _(pe):
                        pe.sem_inc(done, 2)
                        with pe.Fori(0, NPAIR) as i:
                            for u in range(2):
                                pe.wait_ge(staged, i * 2 + (u + 1))
                                pe.wait_ge(updated, i * 2 + (u + 1))
                                nc.tensor.matmul(po[:, u, 0:D], st[:, u, 0, :], wn, start=True, stop=True)
                                nc.tensor.matmul(po[:, u, D:2 * D], st[:, u, 1, :], wl, start=True,
                                                 stop=True).then_inc(done, 1)

                    @block.vector
                    def _(dve):
                        own = Chain(dve, own_s)
                        dve.sem_inc(updated, 2)
                        with dve.Fori(0, NPAIR) as i:
                            own.loop(i, 2)
                            for u in range(2):
                                b = bass.ds(i * 2 + u, 1)
                                xb = x_nodes[:, b, :].rearrange("p b d -> p (b d)")
                                dve.wait_ge(hlc, i * 2 + (u + 1))
                                own(nc.vector.scalar_tensor_tensor(out=tt[:, u, :], in0=po[:, u, 0:D],
                                                                   scalar=node_norm[:, b], in1=hl[:, u, :],
                                                                   op0=ALU.mult, op1=ALU.add))
                                nc.vector.scalar_tensor_tensor(out=xb, in0=tt[:, u, :], scalar=0.0, in1=xb,
                                                               op0=ALU.max, op1=ALU.add).then_inc(updated, 1)

        def spill_x(store):
            with phase(nc, bank, "moved") as (block, (moved,)):
                @block.sync
                def _(sp):
                    if store:
                        sp.dma_start(x_dram, big[:, 0:NB * D]).then_inc(moved, 16)
                    else:
                        sp.dma_start(big[:, 0:NB * D], x_dram).then_inc(moved, 16)
                    sp.wait_ge(moved, 16)

        def experts(l):
            with ExitStack() as tmp:
                def sbt(name, shape, dt=FP):
                    return tmp.enter_context(sbuf(name, shape, dt))

                def pst(name, shape):
                    return tmp.enter_context(psum(name, shape, FP))

                weak_w = big[:, 0:2048].rearrange("p (k e f) -> p k e f", k=2, e=NW)
                s1_w = big[:, 2048:6144].rearrange("p (k e f) -> p k e f", k=2, e=NW)
                s2_w = big[:, 6144:10240].rearrange("p (k e f) -> p k e f", k=4, e=NW)
                router = sbt("router", [P, 4, NE + 1])
                router_b = sbt("router_b", [P, NE + 1])
                weak_b = sbt("weak_b", [P, NW, 2])
                s1_b = sbt("s1_b", [P, NW, 4])
                s2_b = sbt("s2_b", [NE, H])
                iota8 = iota_row0[:, 0:NE]
                rdegb = sbt("rdegb", [P, 2, P])
                agg = sbt("agg", [P, 2, 2, P])
                hst = sbt("hst", [P, 2, 2, P])
                lg = sbt("lg", [P, 2, NE + 1])
                top = sbt("top", [P, 2, 8])
                topi = sbt("topi", [P, 2, 8], U32)
                topf = sbt("topf", [P, 2, 2])
                gcol = sbt("gcol", [P, 2, 8])
                ecol = sbt("ecol", [P, 2, 2])
                g1 = sbt("g1", [P, NE])
                g2 = sbt("g2", [P, NE])
                gate = sbt("gate", [P, 2, NE])
                gdiag = sbt("gdiag", [P, NE, P])
                gts = sbt("gts", [NE, 2, P])
                weak_h = sbt("weak_h", [P, NE, P])
                strong_h = sbt("strong_h", [P, 2, 4, P])
                moe = sbt("moe", [P, 2, 2, P])
                hid = pst("hid", [P, 2, 4, P])
                gb = pst("gb", [P, NE, P])
                yout = pst("yout", [P, 2, 512])
                misc = pst("misc", [P, 2, 512])
                names = ["w_loaded", "w_zero", "rd0", "rd1", "agg_done", "hs_done", "logits_done", "own_s", "exp_in",
                         "exp_done", "gate_done", "diag_done", "gb_done", "gt_done", "gts_done", "hid_done", "relu_done",
                         "scaled", "y_done", "used", "gb_used", "weak_used", "h_written"]
                with phase(nc, bank, *names) as (block, sems):
                    (w_loaded, w_zero, rd0, rd1, agg_done, hs_done, logits_done, own_s, exp_in, exp_done, gate_done,
                     diag_done, gb_done, gt_done, gts_done, hid_done, relu_done, scaled, y_done, used, gb_used,
                     weak_used, h_written) = sems
                    rds = (rd0, rd1)

                    @block.sync
                    def _(sp):
                        one = bass.ds(l, 1)
                        n = 0
                        for k in range(2):
                            sp.dma_start(weak_w[:, k, :, :], t["L1_gnn_weak_W"][one, :, k * P:(k + 1) * P, :]
                                         .rearrange("o e p f -> p (o e) f")).then_inc(w_loaded, 16)
                            sp.dma_start(s1_w[:, k, :, :], t["L1_gnn_strong_W1"][one, :, k * P:(k + 1) * P, :]
                                         .rearrange("o e p f -> p (o e) f")).then_inc(w_loaded, 16)
                            n += 2
                        for k in range(4):
                            sp.dma_start(s2_w[:, k, :, :], t["L1_gnn_strong_W2"][one, :, k * P:(k + 1) * P, :]
                                         .rearrange("o e p f -> p (o e) f")).then_inc(w_loaded, 16)
                            sp.dma_start(router[:, k, 0:NE], t["L1_gnn_router_W"][one, k * P:(k + 1) * P, :]
                                         .rearrange("o p f -> (o p) f")).then_inc(w_loaded, 16)
                            n += 2
                        sp.wait_ge(w_zero, 1)
                        with nc.allow_non_contiguous_dma("columns of biases"):
                            for k in range(2):
                                sp.dma_start(router[:, k, NE:NE + 1], t["L1_gnn_conf_W"][one, k * P:(k + 1) * P, :]
                                             .rearrange("o p f -> (o p) f")).then_inc(w_loaded, 16)
                            for e in range(NW):
                                sp.dma_start(weak_b[:, e, :], t["L1_gnn_weak_b"][one, e, :]
                                             .rearrange("o (m p) -> p (o m)", p=P)).then_inc(w_loaded, 16)
                                sp.dma_start(s1_b[:, e, :], t["L1_gnn_strong_b1"][one, e, :]
                                             .rearrange("o (m p) -> p (o m)", p=P)).then_inc(w_loaded, 16)
                            n += 2 + 2 * NW
                        sp.dma_start(s2_b[NW:NE, :], t["L1_gnn_strong_b2"][one, :, :]
                                     .rearrange("o e f -> (o e) f")).then_inc(w_loaded, 16)
                        sp.dma_start(router_b[:, 0:NE], t["L1_gnn_router_b"][one, :].to_broadcast((P, NE))
                                     ).then_inc(w_loaded, 16)
                        sp.dma_start(router_b[:, NE:NE + 1], t["L1_gnn_conf_b"][one, :].to_broadcast((P, 1))
                                     ).then_inc(w_loaded, 16)
                        n += 3
                        with sp.Fori(0, NPAIR) as i:
                            for u in range(2):
                                sp.wait_ge(agg_done, i * 2 + (u + 1))
                                sp.dma_start(rdegb[:, u, :], rdeg_dram[:, bass.ds((i * 2 + u) * P, P)]
                                             ).then_inc(rds[u], 16)
                        sp.wait_ge(w_loaded, 16 * n)
                        sp.sem_inc(w_zero, 1)

                    @block.gpsimd
                    def _(pool):
                        nc.gpsimd.memset(router[:, :, NE:NE + 1], 0.0)
                        nc.gpsimd.memset(s2_b[:, :], 0.0).then_inc(w_zero, 1)

                    W_LOADED = 16 * (8 + 4 + 2 + 2 * NW + 3 - 0)

                    @block.scalar
                    def _(act):
                        act.wait_ge(w_loaded, W_LOADED)
                        with act.Fori(0, NPAIR) as i:
                            for u in range(2):
                                blk = bass.ds((i * 2 + u) * P, P)
                                act.wait_ge(used, i * 2 + (u + 1))
                                nc.scalar.copy(hst[:, u, :, :], feat[:, :, blk]).then_inc(hs_done, 1)
                            for u in range(2):
                                b = i * 2 + u
                                act.wait_ge(exp_in, b + 1)
                                nc.scalar.activation(ecol[:, u, :], gcol[:, u, 0:2], ACT.Exp).then_inc(exp_done, 1)
                                for q in range(2):
                                    act.wait_ge(hid_done, b * 6 + (q + 1))
                                    if q == 0:
                                        act.wait_ge(weak_used, b)
                                    for j in range(4):
                                        e, m = 2 * q + j // 2, j % 2
                                        last = nc.scalar.activation(weak_h[:, 2 * e + m, :], hid[:, q, j, :], ACT.Relu,
                                                                    bias=weak_b[:, e, m:m + 1])
                                    last.then_inc(relu_done, 1)
                                act.wait_ge(gt_done, b + 1)
                                nc.scalar.copy(gts[:, u, :], misc[0:NE, u, 16:16 + P]).then_inc(gts_done, 1)
                                for e in range(NW):
                                    q = e % 2
                                    act.wait_ge(hid_done, b * 6 + (2 + e + 1))
                                    act.wait_ge(y_done, b * 4 + (e - 1 + 2))
                                    for j in range(4):
                                        last = nc.scalar.activation(strong_h[:, q, j, :], hid[:, q, j, :], ACT.Relu,
                                                                    bias=s1_b[:, e, j:j + 1])
                                    last.then_inc(relu_done, 1)

                    @block.vector
                    def _(dve):
                        own = Chain(dve, own_s)
                        dve.sem_inc(used, 2)
                        dve.sem_inc(agg_done, 2)
                        with dve.Fori(0, NPAIR) as i:
                            own.loop(i, 2 * 14)
                            for u in range(2):
                                b = i * 2 + u
                                blk = bass.ds(b * P, P)
                                dve.wait_ge(rds[u], i * 16 + 16)
                                dve.wait_ge(used, b + 1)
                                nc.vector.tensor_tensor(agg[:, u, :, :], acc[:, :, blk],
                                                        rdegb[:, u, :].unsqueeze(1).to_broadcast([P, 2, P]),
                                                        ALU.mult).then_inc(agg_done, 1)
                            for u in range(2):
                                b = i * 2 + u
                                blk = bass.ds(b * P, P)
                                dve.wait_ge(logits_done, b + 1)
                                own(nc.vector.tensor_tensor(lg[:, u, :], misc[:, u, 0:NE + 1], router_b[:, :], ALU.add))
                                dve.nop(nofuse=True)
                                own(nc.vector.max(top[:, u, :], lg[:, u, 0:NE]))
                                dve.nop(nofuse=True)
                                own(nc.vector.max_index(topi[:, u, :], top[:, u, :], lg[:, u, 0:NE]))
                                own(nc.vector.tensor_copy(topf[:, u, :], topi[:, u, 0:2]))
                                own(nc.vector.tensor_tensor(gcol[:, u, 0:1], top[:, u, 1:2], top[:, u, 0:1], ALU.subtract))
                                nc.vector.tensor_scalar(gcol[:, u, 1:2], lg[:, u, NE:NE + 1], -1.0, None,
                                                        ALU.mult).then_inc(exp_in, 1)
                                dve.wait_ge(exp_done, b + 1)
                                own(nc.vector.tensor_scalar(gcol[:, u, 2:4], ecol[:, u, :], 1.0, None, ALU.add))
                                own(nc.vector.reciprocal(gcol[:, u, 4:6], gcol[:, u, 2:4]))
                                own(nc.vector.tensor_tensor(gcol[:, u, 6:7], gcol[:, u, 4:5], gcol[:, u, 5:6], ALU.mult))
                                own(nc.vector.tensor_tensor(gcol[:, u, 7:8], gcol[:, u, 6:7], ecol[:, u, 0:1], ALU.mult))
                                own(nc.vector.tensor_scalar(g1[:, :], iota8, topf[:, u, 0:1], gcol[:, u, 6:7],
                                                            ALU.is_equal, ALU.mult))
                                own(nc.vector.tensor_scalar(g2[:, :], iota8, topf[:, u, 1:2], gcol[:, u, 7:8],
                                                            ALU.is_equal, ALU.mult))
                                own(nc.vector.tensor_tensor(gate[:, u, :], g1[:, :], g2[:, :], ALU.add))
                                nc.vector.sem_inc(gate_done, 1)
                                dve.wait_ge(gb_done, b)
                                nc.vector.tensor_tensor(
                                    gdiag[:, :, :], ident[:, :].unsqueeze(1).to_broadcast([P, NE, P]),
                                    gate[:, u, :].unsqueeze(2).to_broadcast([P, NE, P]), ALU.mult).then_inc(diag_done, 1)
                                dve.wait_ge(gb_done, b + 1)
                                dve.wait_ge(relu_done, b * 6 + 2)
                                wh = weak_h[:, :, :].rearrange("p (e m) n -> p e m n", m=2)
                                own(nc.vector.tensor_tensor(
                                    wh, wh, gb[:, 0:NW, :].unsqueeze(2).to_broadcast([P, NW, 2, P]), ALU.mult))
                                nc.vector.tensor_reduce(moe[:, u, :, :], weak_h[:, :, :].rearrange("p (e m) n -> p m n e", m=2),
                                                        AX.X, ALU.add).then_inc(weak_used, 1)
                                for e in range(NW):
                                    q = e % 2
                                    dve.wait_ge(relu_done, b * 6 + (3 + e))
                                    nc.vector.tensor_tensor(
                                        strong_h[:, q, :, :], strong_h[:, q, :, :],
                                        gb[:, NW + e, :].unsqueeze(1).to_broadcast([P, 4, P]), ALU.mult).then_inc(scaled, 1)
                                dve.wait_ge(y_done, b * 4 + 4 + 2)
                                dve.wait_ge(weak_used, b + 1)
                                own(nc.vector.tensor_tensor(moe[:, u, :, :], moe[:, u, :, :],
                                                            yout[:, u, 0:H].rearrange("p (m n) -> p m n", n=P), ALU.add))
                                nc.vector.tensor_tensor(feat[:, :, blk], hst[:, u, :, :], moe[:, u, :, :],
                                                        ALU.add).then_inc(used, 1)

                    @block.tensor
                    def _(pe):
                        pe.sem_inc(y_done, 2)
                        pe.wait_ge(w_loaded, W_LOADED)
                        with pe.Fori(0, NPAIR) as i:
                            for u in range(2):
                                b = i * 2 + u
                                pe.wait_ge(hs_done, b + 1)
                                pe.wait_ge(agg_done, b + 3)
                                for k in range(4):
                                    st = hst[:, u, k, :] if k < 2 else agg[:, u, k - 2, :]
                                    last = nc.tensor.matmul(misc[:, u, 0:NE + 1], st, router[:, k, :], start=(k == 0),
                                                            stop=(k == 3))
                                last.then_inc(logits_done, 1)
                            for u in range(2):
                                b = i * 2 + u

                                def product(out_ap, wts, cols):
                                    for k in range(len(wts)):
                                        pe_last = nc.tensor.matmul(out_ap, wts[k], cols[k], start=(k == 0),
                                                                   stop=(k == len(wts) - 1))
                                    return pe_last

                                a2 = [agg[:, u, k, :] for k in range(2)]
                                for q in range(2):
                                    pe.wait_ge(relu_done, b * 6)
                                    for j in range(4):
                                        e, m = 2 * q + j // 2, j % 2
                                        last = product(hid[:, q, j, :], [weak_w[:, k, e, m * P:(m + 1) * P] for k in range(2)], a2)
                                    last.then_inc(hid_done, 1)
                                pe.wait_ge(gate_done, b + 1)
                                nc.tensor.matmul(misc[0:NE, u, 16:16 + P], gate[:, u, :], ident[:, :], start=True,
                                                 stop=True).then_inc(gt_done, 1)
                                pe.wait_ge(diag_done, b + 1)
                                pe.wait_ge(scaled, b * 4)
                                for g in range(2):
                                    last = nc.tensor.matmul(gb[:, 4 * g:4 * g + 4, :], ones[:, :],
                                                            gdiag[:, 4 * g:4 * g + 4, :], start=True, stop=True)
                                last.then_inc(gb_done, 1)

                                def up(e):
                                    q = e % 2
                                    pe.wait_ge(relu_done, b * 6 + (e + 1))
                                    for j in range(4):
                                        last = product(hid[:, q, j, :], [s1_w[:, k, e, j * P:(j + 1) * P] for k in range(2)], a2)
                                    last.then_inc(hid_done, 1)

                                def down(e):
                                    pe.wait_ge(scaled, b * 4 + (e + 1))
                                    for m in range(2):
                                        for k in range(4):
                                            last = nc.tensor.matmul(yout[:, u, m * P:(m + 1) * P],
                                                                    s2_w[:, k, e, m * P:(m + 1) * P],
                                                                    strong_h[:, e % 2, k, :],
                                                                    start=False, stop=(e == NW - 1 and k == 3),
                                                                    skip_group_check=True)
                                    last.then_inc(y_done, 1)

                                up(0)
                                pe.wait_ge(gts_done, b + 1)
                                pe.wait_ge(used, b + 1)
                                for m in range(2):
                                    nc.tensor.matmul(yout[:, u, m * P:(m + 1) * P], s2_b[:, m * P:(m + 1) * P],
                                                     gts[:, u, :], start=(m == 0), stop=False, skip_group_check=True)
                                up(1)
                                down(0)
                                up(2)
                                down(1)
                                up(3)
                                down(2)
                                down(3)

        def publish256():
            with ExitStack() as tmp:
                st = tmp.enter_context(sbuf("st", [P, 2, 2, P], FP))
                row = tmp.enter_context(sbuf("row", [P, 2, H], FP))
                pt = tmp.enter_context(psum("pt", [P, 2, 512], FP))
                with phase(nc, bank, "staged", "done", "row_done", "out0", "out1") as (block, (staged, done, row_done, out0, out1)):
                    outs = (out0, out1)

                    @block.scalar
                    def _(act):
                        with act.Fori(0, NPAIR) as i:
                            for u in range(2):
                                act.wait_ge(done, i * 2 + (u + 1))
                                nc.scalar.copy(st[:, u, :, :], feat[:, :, bass.ds((i * 2 + u) * P, P)]).then_inc(staged, 1)

                    @block.tensor
                    def _(pe):
                        pe.sem_inc(done, 2)
                        with pe.Fori(0, NPAIR) as i:
                            for u in range(2):
                                pe.wait_ge(staged, i * 2 + (u + 1))
                                pe.wait_ge(row_done, i * 2)
                                for a in range(2):
                                    last = nc.tensor.transpose(pt[:, u, a * P:(a + 1) * P], st[:, u, a, :], ident[:, :])
                                last.then_inc(done, 1)

                    @block.vector
                    def _(dve):
                        with dve.Fori(0, NPAIR) as i:
                            for u in range(2):
                                dve.wait_ge(done, i * 2 + (u + 3))
                                dve.wait_ge(outs[u], i * 16)
                                nc.vector.tensor_copy(row[:, u, :], pt[:, u, 0:H]).then_inc(row_done, 1)

                    @block.sync
                    def _(sp):
                        with sp.Fori(0, NPAIR) as i:
                            for u in range(2):
                                sp.wait_ge(row_done, i * 2 + (u + 1))
                                sp.dma_start(rows256[bass.ds((i * 2 + u) * P, P), :], row[:, u, :]).then_inc(outs[u], 16)
                        sp.wait_ge(out0, NPAIR * 16)
                        sp.wait_ge(out1, NPAIR * 16)

        def layer1_out(w_out, b_out):
            with ExitStack() as tmp:
                st = tmp.enter_context(sbuf("st", [P, 2, 2, P], FP))
                tt = tmp.enter_context(sbuf("tt", [P, 2, D], FP))
                po = tmp.enter_context(psum("po", [P, 2, 512], FP))
                with phase(nc, bank, "staged", "done", "own_s", "updated") as (block, (staged, done, own_s, updated)):
                    @block.scalar
                    def _(act):
                        with act.Fori(0, NPAIR) as i:
                            for u in range(2):
                                act.wait_ge(done, i * 2 + (u + 1))
                                nc.scalar.copy(st[:, u, :, :], feat[:, :, bass.ds((i * 2 + u) * P, P)]).then_inc(staged, 1)

                    @block.tensor
                    def _(pe):
                        pe.sem_inc(done, 2)
                        with pe.Fori(0, NPAIR) as i:
                            for u in range(2):
                                pe.wait_ge(staged, i * 2 + (u + 1))
                                pe.wait_ge(updated, i * 2 + (u + 1))
                                for k in range(2):
                                    last = nc.tensor.matmul(po[:, u, 0:D], st[:, u, k, :], w_out[:, k, :],
                                                            start=(k == 0), stop=(k == 1))
                                last.then_inc(done, 1)

                    @block.vector
                    def _(dve):
                        own = Chain(dve, own_s)
                        dve.sem_inc(updated, 2)
                        with dve.Fori(0, NPAIR) as i:
                            own.loop(i, 2)
                            for u in range(2):
                                xb = x_nodes[:, bass.ds(i * 2 + u, 1), :].rearrange("p b d -> p (b d)")
                                dve.wait_ge(done, i * 2 + (u + 3))
                                own(nc.vector.tensor_tensor(tt[:, u, :], po[:, u, 0:D], b_out, ALU.add))
                                nc.vector.tensor_tensor(xb, xb, tt[:, u, :], ALU.add).then_inc(updated, 1)

        def layer2_nodes(w4, b4):
            with ExitStack() as tmp:
                st = tmp.enter_context(sbuf("st", [P, 2, 2, P], FP))
                tt = tmp.enter_context(sbuf("tt", [P, 2, D], FP))
                po = tmp.enter_context(psum("po", [P, 2, 512], FP))
                with phase(nc, bank, "h_staged", "staged", "done", "own_s", "updated") as (block, (h_staged, staged, done, own_s, updated)):
                    @block.scalar
                    def _(act):
                        with act.Fori(0, NPAIR) as i:
                            for u in range(2):
                                act.wait_ge(done, i * 2 + (u + 1))
                                nc.scalar.copy(st[:, u, 1, :], feat[:, 0, bass.ds((i * 2 + u) * P, P)]).then_inc(h_staged, 1)

                    @block.tensor
                    def _(pe):
                        pe.sem_inc(done, 2)
                        with pe.Fori(0, NPAIR) as i:
                            for u in range(2):
                                pe.wait_ge(h_staged, i * 2 + (u + 1))
                                pe.wait_ge(staged, i * 2 + (u + 1))
                                pe.wait_ge(updated, i * 2 + (u + 1))
                                nc.tensor.transpose(po[:, u, 0:D], st[:, u, 0, :], ident[:, :])
                                nc.tensor.matmul(po[:, u, D:2 * D], st[:, u, 1, :], w4, start=True,
                                                 stop=True).then_inc(done, 1)

                    @block.vector
                    def _(dve):
                        own = Chain(dve, own_s)
                        dve.sem_inc(updated, 2)
                        with dve.Fori(0, NPAIR) as i:
                            own.loop(i, 8)
                            for u in range(2):
                                blk = bass.ds((i * 2 + u) * P, P)
                                dve.wait_ge(done, i * 2 + (u + 1))
                                own(nc.vector.tensor_tensor(st[:, u, 0, :], acc[:, 1, blk], feat[:, 0, blk], ALU.mult))
                                nc.vector.tensor_tensor(st[:, u, 0, :], st[:, u, 0, :], acc[:, 0, blk],
                                                        ALU.subtract).then_inc(staged, 1)
                            for u in range(2):
                                b = bass.ds(i * 2 + u, 1)
                                xb = x_nodes[:, b, :].rearrange("p b d -> p (b d)")
                                dve.wait_ge(done, i * 2 + (u + 3))
                                own(nc.vector.tensor_tensor(tt[:, u, :], po[:, u, D:2 * D], b4, ALU.add))
                                own(nc.vector.scalar_tensor_tensor(out=tt[:, u, :], in0=tt[:, u, :],
                                                                   scalar=node_deg[:, b], in1=po[:, u, 0:D],
                                                                   op0=ALU.mult, op1=ALU.add))
                                own(nc.vector.tensor_tensor(xb, xb, tt[:, u, :], ALU.add))
                                nc.vector.sem_inc(updated, 1)

        def layer3_weights(l, wts):
            with ExitStack() as tmp:
                raw = tmp.enter_context(sbuf("raw", [P, 2, D], FP))
                pt = tmp.enter_context(psum("pt", [P, 2 * D], FP))
                with phase(nc, bank, "loaded", "done") as (block, (loaded, done)):
                    @block.sync
                    def _(sp):
                        one = bass.ds(l, 1)
                        sp.dma_start(raw[:, 0, :], t["L3_gnn_Wl"][one, :, :].rearrange("o p f -> (o p) f")).then_inc(loaded, 16)
                        sp.dma_start(raw[:, 1, :], t["L3_gnn_Wr"][one, :, :].rearrange("o p f -> (o p) f")).then_inc(loaded, 16)
                        sp.dma_start(wts[:, 2, :], t["L3_gnn_bl"][one, :].to_broadcast((P, D))).then_inc(loaded, 16)
                        sp.wait_ge(loaded, 48)

                    @block.tensor
                    def _(pe):
                        pe.wait_ge(loaded, 48)
                        nc.tensor.transpose(pt[:, 0:D], raw[:, 0, :], ident[:, :])
                        nc.tensor.transpose(pt[:, D:2 * D], raw[:, 1, :], ident[:, :]).then_inc(done, 1)

                    @block.vector
                    def _(dve):
                        dve.wait_ge(done, 1)
                        nc.vector.tensor_copy(wts[:, 0:2, :], pt[:, :].rearrange("p (a j) -> p a j", j=D))

        def layer3_nodes(wts, final):
            with ExitStack() as tmp:
                st = tmp.enter_context(sbuf("st", [P, 2, 2, P], FP))
                sq = tmp.enter_context(sbuf("sq", [P, 2, 2, P], FP))
                nrm = tmp.enter_context(sbuf("nrm", [P, 2, 4], FP))
                tt = tmp.enter_context(sbuf("tt", [P, 2, D], FP))
                row = tmp.enter_context(sbuf("row", [P, 2, D], FP))
                po = tmp.enter_context(psum("po", [P, 2, 512], FP))
                pt = tmp.enter_context(psum("pt", [P, 2, 512], FP))
                with phase(nc, bank, "staged", "done", "nsq", "root", "own_s", "row_done", "t_done", "spill", "out0",
                           "out1") as (block, sems):
                    staged, done, nsq, root, own_s, row_done, t_done, spill, out0, out1 = sems
                    outs = (out0, out1)

                    @block.scalar
                    def _(act):
                        with act.Fori(0, NPAIR) as i:
                            for u in range(2):
                                blk = bass.ds((i * 2 + u) * P, P)
                                act.wait_ge(done, i * 2 + (u + 1))
                                nc.scalar.copy(st[:, u, 0, :], acc[:, 0, blk])
                                nc.scalar.copy(st[:, u, 1, :], feat[:, 0, blk])
                                nc.scalar.activation(sq[:, u, 0, :], acc[:, 0, blk], ACT.Square)
                                nc.scalar.activation(sq[:, u, 1, :], feat[:, 0, blk], ACT.Square).then_inc(staged, 1)
                            for u in range(2):
                                act.wait_ge(nsq, i * 2 + (u + 1))
                                nc.scalar.activation(nrm[:, u, 2:4], nrm[:, u, 0:2], ACT.Sqrt).then_inc(root, 1)

                    @block.tensor
                    def _(pe):
                        pe.sem_inc(done, 2)
                        with pe.Fori(0, NPAIR) as i:
                            for u in range(2):
                                pe.wait_ge(staged, i * 2 + (u + 1))
                                pe.wait_ge(row_done, i * 2 + (u + 1))
                                for a in range(2):
                                    nc.tensor.matmul(po[:, u, a * D:(a + 1) * D], st[:, u, a, :], wts[:, a, :],
                                                     start=True, stop=True)
                                for a in range(2):
                                    last = nc.tensor.matmul(po[:, u, 2 * D + a:2 * D + a + 1], sq[:, u, a, :],
                                                            ones[:, 0:1], start=True, stop=True)
                                last.then_inc(done, 1)
                            if not final:
                                for u in range(2):
                                    pe.wait_ge(row_done, i * 2 + (u + 3))
                                    pe.wait_ge(spill, i * 2)
                                    nc.tensor.transpose(pt[:, u, 0:P], row[:, u, :], ident[:, :]).then_inc(t_done, 1)

                    @block.vector
                    def _(dve):
                        own = Chain(dve, own_s)
                        dve.sem_inc(row_done, 2)
                        with dve.Fori(0, NPAIR) as i:
                            own.loop(i, 2 * 6)
                            for u in range(2):
                                dve.wait_ge(done, i * 2 + (u + 3))
                                nc.vector.tensor_scalar(nrm[:, u, 0:2], po[:, u, 2 * D:2 * D + 2], TINY, None,
                                                        ALU.max).then_inc(nsq, 1)
                            for u in range(2):
                                b = bass.ds(i * 2 + u, 1)
                                dve.wait_ge(root, i * 2 + (u + 1))
                                own(nc.vector.tensor_scalar(nrm[:, u, 2:3], nrm[:, u, 2:3], node_rdeg[:, b], None, ALU.mult))
                                own(nc.vector.tensor_scalar(nrm[:, u, 2:4], nrm[:, u, 2:4], L2_EPS, None, ALU.max))
                                own(nc.vector.reciprocal(nrm[:, u, 2:4], nrm[:, u, 2:4]))
                                own(nc.vector.tensor_scalar(nrm[:, u, 2:3], nrm[:, u, 2:3], node_rdeg[:, b], None, ALU.mult))
                                own(nc.vector.scalar_tensor_tensor(out=tt[:, u, :], in0=po[:, u, 0:D],
                                                                   scalar=nrm[:, u, 2:3], in1=wts[:, 2, :],
                                                                   op0=ALU.mult, op1=ALU.add))
                                own(nc.vector.scalar_tensor_tensor(out=tt[:, u, :], in0=po[:, u, D:2 * D],
                                                                   scalar=nrm[:, u, 3:4], in1=tt[:, u, :],
                                                                   op0=ALU.mult, op1=ALU.add))
                                if final:
                                    xb = x_nodes[:, b, :].rearrange("p b d -> p (b d)")
                                    nc.vector.tensor_tensor(xb, xb, tt[:, u, :], ALU.add).then_inc(row_done, 1)
                                else:
                                    dve.wait_ge(outs[u], i * 16)
                                    dve.wait_ge(t_done, i * 2)
                                    nc.vector.tensor_scalar(row[:, u, :], tt[:, u, :], 0.0, None,
                                                            ALU.max).then_inc(row_done, 1)
                            if not final:
                                for u in range(2):
                                    dve.wait_ge(t_done, i * 2 + (u + 1))
                                    nc.vector.tensor_copy(feat[:, 0, bass.ds((i * 2 + u) * P, P)],
                                                          pt[:, u, 0:P]).then_inc(spill, 1)

                    @block.sync
                    def _(sp):
                        if not final:
                            with sp.Fori(0, NPAIR) as i:
                                for u in range(2):
                                    sp.wait_ge(row_done, i * 2 + (u + 3))
                                    sp.dma_start(rows128[bass.ds((i * 2 + u) * P, P), :], row[:, u, :]).then_inc(outs[u], 16)
                            sp.wait_ge(out0, NPAIR * 16)
                            sp.wait_ge(out1, NPAIR * 16)

        def store_out():
            with phase(nc, bank, "stored") as (block, (stored,)):
                @block.sync
                def _(sp):
                    sp.dma_start(out[0:LAST * P, :].rearrange("(b p) d -> p b d", p=P), x_nodes[:, 0:LAST, :]).then_inc(stored, 16)
                    sp.dma_start(out[LAST * P:N, :], x_nodes[0:LASTN, LAST, :]).then_inc(stored, 16)
                    sp.wait_ge(stored, 32)

        with ExitStack() as lay:
            w0 = lay.enter_context(sbuf("w0", [P, 2, D], FP))
            load([(w0[:, 0, :], t["L0_gnn_W_neighbor"]), (w0[:, 1, :], t["L0_gnn_loop_weight"])])
            normalize("h")
            gather_pass(rows128, D, second=t["L0_gnn_rel_emb"])
            degrees()
            layer0_nodes(w0[:, 0, :], w0[:, 1, :])

        with ExitStack() as lay:
            w_in = lay.enter_context(sbuf("w_in", [P, H], FP))
            b_in = lay.enter_context(sbuf("b_in", [P, H], FP))
            load([(w_in[:, :], t["L1_gnn_W_in"]), (b_in[:, :], bcast_vec(t["L1_gnn_b_in"]))])
            normalize("h w", w_in[:, :], b_in[:, :])
        spill_x(True)
        with nc.Fori(0, LAYERS) as l:
            gather_pass(rows256, H)
            experts(l)
            publish256()
        spill_x(False)
        with ExitStack() as lay:
            w_out = lay.enter_context(sbuf("w_out", [P, 2, D], FP))
            b_out = lay.enter_context(sbuf("b_out", [P, D], FP))
            load([(w_out[:, 0, :], t["L1_gnn_W_out"][0:P, :]), (w_out[:, 1, :], t["L1_gnn_W_out"][P:H, :]),
                  (b_out[:, :], bcast_vec(t["L1_gnn_b_out"]))])
            layer1_out(w_out, b_out[:, :])

        with ExitStack() as lay:
            w2 = lay.enter_context(sbuf("w2", [P, 2, D], FP))
            c2 = lay.enter_context(sbuf("c2", [P, 3], FP))
            b4 = lay.enter_context(sbuf("b4", [P, D], FP))
            load([(w2[:, 0, :], t["L2_gnn_W1"]), (w2[:, 1, :], t["L2_gnn_W4"]),
                  (c2[:, 0:1], t["L2_gnn_b1"].rearrange("(p o) -> p o", o=1)), (c2[:, 1:2], t["L2_gnn_W2"]),
                  (c2[:, 2:3], bcast_vec(t["L2_gnn_b2"])), (b4[:, :], bcast_vec(t["L2_gnn_b4"]))])
            normalize("y h", w2[:, 0, :])
            gather_pass(rows256, H, edge_net=(rows256, c2[:, 0:1], c2[:, 1:2], c2[:, 2:3]))
            layer2_nodes(w2[:, 1, :], b4[:, :])

        with ExitStack() as lay:
            w3 = lay.enter_context(sbuf("w3", [P, 3, D], FP))
            normalize("h")
            with nc.Fori(0, LAYERS - 1) as l:
                gather_pass(rows128, D)
                layer3_weights(l, w3)
                layer3_nodes(w3, final=False)
            gather_pass(rows128, D)
            layer3_weights(LAYERS - 1, w3)
            layer3_nodes(w3, final=True)
        store_out()


def a_row(vec, start):
    return vec[start:start + P].rearrange("(o j) -> o j", o=1)


def bcast_vec(vec):
    return vec.rearrange("(o j) -> o j", o=1).to_broadcast((P, vec.shape[0]))


def bcast_rows(rows, start, n):
    return rows[bass.ds(start, n), :].unsqueeze(0).to_broadcast((P, n, P))


_INS = ['x', 'src', 'dst', 'edge_type_500', 'L0_gnn_rel_emb', 'L0_gnn_W_neighbor', 'L0_gnn_loop_weight',
        'L1_gnn_W_in', 'L1_gnn_b_in', 'L1_gnn_router_W', 'L1_gnn_router_b', 'L1_gnn_weak_W', 'L1_gnn_weak_b',
        'L1_gnn_strong_W1', 'L1_gnn_strong_b1', 'L1_gnn_strong_W2', 'L1_gnn_strong_b2', 'L1_gnn_conf_W',
        'L1_gnn_conf_b', 'L1_gnn_W_out', 'L1_gnn_b_out', 'L2_gnn_W1', 'L2_gnn_b1', 'L2_gnn_W2', 'L2_gnn_b2',
        'L2_gnn_W4', 'L2_gnn_b4', 'L3_gnn_Wl', 'L3_gnn_bl', 'L3_gnn_Wr']


def kernel(**inputs):
    import numpy as _np
    import concourse.bacc as _bacc
    from concourse import mybir as _mybir
    from concourse.bass_utils import run_bass_kernel_spmd as _run

    nc = _bacc.Bacc("TRN2", target_bir_lowering=False, num_devices=1)
    arrays, handles = {}, {}
    for name in _INS:
        a = _np.ascontiguousarray(inputs[name])
        arrays[f"in_{name}"] = a
        handles[name] = nc.dram_tensor(f"in_{name}", a.shape, _mybir.dt.from_np(a.dtype), kind="ExternalInput").ap()
    out = nc.dram_tensor("out_x", (N, D), _mybir.dt.float32, kind="ExternalOutput").ap()
    gnn_kernel(nc, handles, out)
    r = _run(nc, [arrays], core_ids=[0])
    return r.results[0]["out_x"]
```

```python
import concourse.bass as bass
from concourse import mybir
from contextlib import ExitStack, contextmanager

N = 6250
E = 106250
D = 128
H = 256
RELS = 500
NE = 8
NW = 4
P = 128

GROUP = 4
WIN = 64
RING = 16
HALF = RING // 2
GROUPS = RING // GROUP
TILES = -(-E // P)
STEPS = -(-TILES // RING)
ROW = GROUP * P
SETS = -(-E // (ROW * P))
TCOLS = SETS * P * GROUP
GCOLS = SETS * P
NB = -(-N // P) + 1
SPARE_BLOCK = NB - 1
NPAD = NB * P
SPARE = SPARE_BLOCK * P
LAST = N // P
LASTN = N - LAST * P
REL_BLOCKS = -(-RELS // P)
LN_EPS = 1e-5
L2_EPS = 1e-12
TINY = 1e-35

FP = mybir.dt.float32
F16 = mybir.dt.float16
FR = mybir.dt.float32r
I32 = mybir.dt.int32
U32 = mybir.dt.uint32
ALU = mybir.AluOpType
ACT = mybir.ActivationFunctionType
AX = mybir.AxisListType


@contextmanager
def phase(nc, bank, *names, pool_dmas=()):
    assert len(names) <= len(bank), len(names)
    with nc.Block() as block:
        yield block, bank[:len(names)]
    if pool_dmas:
        numbers = range(pool_dmas[0].num, pool_dmas[-1].num + 1)
        nc.gpsimd.dma_reset(numbers)
        nc.all_engine_barrier(sems_to_clear=numbers)
    nc.all_engine_barrier(sems_to_clear=range(bank[0].num, bank[-1].num + 1))


class Chain:

    def __init__(self, eng, sem):
        self.eng, self.sem, self.n = eng, sem, 0

    def __call__(self, ins):
        self.n = self.n + 1
        ins.then_inc(self.sem, 1)
        self.eng.wait_ge(self.sem, self.n)


class Results:

    def __init__(self, sem, names):
        self.sem, self.names = sem, names.split()
        assert len(set(self.names)) == len(self.names)

    def at(self, name, i):
        return i * len(self.names) + (len(self.names) + self.names.index(name) + 1)

    def before(self, name, i):
        return i * len(self.names) + (self.names.index(name) + 1)


class Maker:

    def __init__(self, eng, mine, i):
        self.eng, self.mine, self.i, self.next = eng, mine, i, 0

    def done(self, name, ins, wait=False):
        assert self.mine.names[self.next] == name, (self.mine.names[self.next], name)
        self.next += 1
        ins.then_inc(self.mine.sem, 1)
        if wait:
            self.need(self.mine, name)

    def need(self, results, name):
        self.eng.wait_ge(results.sem, results.at(name, self.i))

    def need_before(self, results, name):
        self.eng.wait_ge(results.sem, results.before(name, self.i))

    def apart(self):
        self.eng.nop(nofuse=True)


def gnn_kernel(nc, t, out):
    ctx = ExitStack()
    with ctx:
        def sb(name, shape, dt=FP):
            return ctx.enter_context(nc.sbuf_tensor(name, shape, dt))

        def dram(name, shape, dt=FP):
            return nc.dram_tensor(name, shape, dt, kind="Internal").ap()

        bank = [ctx.enter_context(nc.semaphore(f"signal{k}")) for k in range(32)]
        gathered = [ctx.enter_context(nc.semaphore(f"gathered{k}")) for k in range(RING)]
        for some in (bank, gathered):
            assert [s.num for s in some] == list(range(some[0].num, some[0].num + len(some)))
        uses = [0]

        def sbuf(name, shape, dt=FP):
            uses[0] += 1
            return nc.sbuf_tensor(f"{name}_{uses[0]}", shape, dt)

        def psum(name, shape):
            uses[0] += 1
            return nc.psum_tensor(f"{name}_{uses[0]}", shape, FP)

        rows128 = [dram(f"rows128_{k}", [NPAD, D]) for k in range(2)]
        rows256 = [dram(f"rows256_{k}", [NPAD, H]) for k in range(2)]
        x_rows = dram("x_rows", [NPAD, D])
        rdeg_dram = dram("rdeg_dram", [P, NPAD])
        rel_rows = dram("rel_rows", [GCOLS, ROW])
        win_dram = dram("win_dram", [SETS, P], I32)

        acc = sb("acc", [P, 2, NPAD])
        big = sb("big", [P, 10240])
        src_idx = sb("src_idx", [P, TCOLS], I32)
        types = sb("types", [P, TCOLS])
        rel = sb("rel", [P, TCOLS])
        win_base = sb("win_base", [1, GCOLS], I32)
        win = sb("win", [1, GCOLS], I32)
        more = sb("more", [1, 1], I32)
        step_block = sb("step_block", [1, STEPS], I32)
        tail_start = sb("tail_start", [1, 1], I32)
        iota_row0 = sb("iota_row0", [P, P])
        iota_row = sb("iota_row", [P, WIN])
        iota_col0 = sb("iota_col0", [P, 1])
        iota_col = sb("iota_col", [P, 1])
        ident = sb("ident", [P, P])
        ones = sb("ones", [P, P])
        mean_col = sb("mean_col", [P, 1])
        zeros = sb("zeros", [P, P])
        node_rdeg = sb("node_rdeg", [P, NB])
        node_deg = sb("node_deg", [P, NB])
        x_nodes = big[:, 0:NB * D].rearrange("p (b d) -> p b d", d=D)

        def setup():
            with ExitStack() as tmp:
                ip = tmp.enter_context(psum("setup_ps", [P, 8, 512]))
                stage = acc[:, :, :].rearrange("p a n -> p (a n)")
                at = [0]

                def part(n, rows=P):
                    at[0] += n
                    return stage[0:rows, at[0] - n:at[0]]

                irow = [part(TCOLS).bitcast(I32) for _ in range(3)]
                frow = [part(TCOLS) for _ in range(3)]
                least, most, span = part(SETS), part(SETS), part(1)
                spani = part(1, 1).bitcast(I32)
                mayber, morer = part(1, 1), part(1, 1)
                wini = part(P, SETS).bitcast(I32)
                basef = part(GCOLS, 1)
                minr = part(STEPS, 1)
                endr = part(NB, 1)
                stepr = part(STEPS, 1)
                br = part(NB, 1)
                touch = part(NB * STEPS, 1).rearrange("o (b s) -> o b s", s=STEPS)
                lastr, timer = part(NB, 1), part(NB, 1)
                hit = part(STEPS * NB, 1).rearrange("o (s b) -> o s b", b=NB)
                blockr, tailr = part(STEPS, 1), part(1, 1)
                whole = (SETS - 1) * P * ROW
                rest = (E - whole) // ROW
                tail = E - whole - rest * ROW
                cols = (SETS - 1) * ROW
                vecs = (t["src"], t["dst"], t["edge_type_500"])
                with phase(nc, bank, "zeroed", "loaded", "filled", "pool_own", "consts", "own_s", "masked",
                           "transposed", "spilled", "wrote", "moved", "x_loaded", "x_zero") as (block, sems):
                    (zeroed, loaded, filled, pool_own, consts, own_s, masked, transposed, spilled, wrote, moved,
                     x_loaded, x_zero) = sems

                    @block.sync
                    def _(sp):
                        for k, v in enumerate(vecs):
                            sp.dma_start(irow[k][:, 0:cols].rearrange("p (a j) -> p a j", j=ROW),
                                         v[0:whole].rearrange("(a p j) -> p a j", p=P, j=ROW)).then_inc(loaded, 16)
                        sp.dma_start(irow[1][:, cols:TCOLS], vecs[1][E - ROW:E].rearrange("(o j) -> o j", o=1)
                                     .to_broadcast((P, ROW))).then_inc(filled, 16)
                        sp.wait_ge(filled, 16)
                        sp.wait_ge(zeroed, 1)
                        for k, v in enumerate(vecs):
                            sp.dma_start(irow[k][0:rest, cols:TCOLS],
                                         v[whole:whole + rest * ROW].rearrange("(p j) -> p j", j=ROW)).then_inc(loaded, 16)
                            sp.dma_start(irow[k][rest:rest + 1, cols:cols + tail],
                                         v[E - tail:E].rearrange("(p j) -> p j", p=1)).then_inc(loaded, 16)
                        sp.wait_ge(x_zero, 1)
                        sp.dma_start(x_nodes[:, 0:LAST, :],
                                     t["x"][0:LAST * P, :].rearrange("(b p) d -> p b d", p=P)).then_inc(x_loaded, 16)
                        sp.dma_start(x_nodes[0:LASTN, LAST, :], t["x"][LAST * P:N, :]).then_inc(x_loaded, 16)
                        sp.wait_ge(masked, 1)
                        sp.dma_start(rel_rows.rearrange("(a p) j -> p a j", p=P),
                                     frow[1].rearrange("p (a j) -> p a j", j=ROW)).then_inc(wrote, 16)
                        sp.wait_ge(spilled, 1)
                        sp.dma_start(win_dram, wini).then_inc(moved, 16)
                        sp.wait_ge(moved, 16)
                        sp.dma_start(win_base[0:1, :], win_dram.rearrange("a p -> (a p)").rearrange("(o n) -> o n", o=1)
                                     ).then_inc(moved, 16)
                        sp.wait_ge(x_loaded, 32)
                        sp.dma_start(x_rows.rearrange("(b p) d -> p b d", p=P), x_nodes).then_inc(wrote, 16)
                        sp.wait_ge(wrote, 32)

                    @block.gpsimd
                    def _(pool):
                        nc.gpsimd.memset(irow[0][:, cols:TCOLS], 0)
                        nc.gpsimd.memset(irow[2][:, cols:TCOLS], 0).then_inc(zeroed, 1)
                        nc.gpsimd.memset(ident[:, :], 0.0).then_inc(pool_own, 1)
                        nc.gpsimd.memset(zeros[:, :], 0.0)
                        nc.gpsimd.iota(iota_row0[:, :], pattern=[[1, P]], base=0, channel_multiplier=0,
                                       allow_small_or_imprecise_dtypes=True)
                        nc.gpsimd.iota(iota_col0[:, :], pattern=[[1, 1]], base=0, channel_multiplier=1,
                                       allow_small_or_imprecise_dtypes=True)
                        nc.gpsimd.iota(endr, pattern=[[P, NB]], base=P - 1, channel_multiplier=0,
                                       allow_small_or_imprecise_dtypes=True)
                        nc.gpsimd.iota(stepr, pattern=[[1, STEPS]], base=0, channel_multiplier=0,
                                       allow_small_or_imprecise_dtypes=True)
                        nc.gpsimd.iota(br, pattern=[[1, NB]], base=0, channel_multiplier=0,
                                       allow_small_or_imprecise_dtypes=True)
                        nc.gpsimd.memset(ones[:, :], 1.0)
                        nc.gpsimd.memset(mean_col[:, :], 1.0 / P)
                        pool.wait_ge(pool_own, 1)
                        nc.gpsimd.affine_select(out=ident[:, :], in_=ident[:, :], compare_op=ALU.not_equal, fill=1.0,
                                                base=0, pattern=[[-1, P]], channel_multiplier=1).then_inc(consts, 1)
                        pool.wait_ge(own_s, 6)
                        for a in range(SETS):
                            last = nc.gpsimd.affine_select(
                                out=frow[1][:, a * ROW:(a + 1) * ROW], in_=frow[1][:, a * ROW:(a + 1) * ROW],
                                compare_op=ALU.is_ge, fill=-1.0, base=E - 1 - a * P * ROW,
                                pattern=[[-1, ROW]], channel_multiplier=-ROW)
                        last.then_inc(masked, 1)

                    @block.vector
                    def _(dve):
                        own = Chain(dve, own_s)
                        nc.vector.memset(x_nodes[:, LAST:NB, :], 0.0).then_inc(x_zero, 1)
                        dve.wait_ge(loaded, 16 * 9)
                        for k in (0, 2, 1):
                            own(nc.vector.tensor_copy(frow[k], irow[k]))
                        v = frow[1].rearrange("p (a j) -> p a j", j=ROW)
                        own(nc.vector.tensor_reduce(least, v, AX.X, ALU.min))
                        own(nc.vector.tensor_reduce(most, v, AX.X, ALU.max))
                        own(nc.vector.tensor_tensor(v, v, least.unsqueeze(2).to_broadcast([P, SETS, ROW]), ALU.subtract))
                        own(nc.vector.tensor_tensor(most, most, least, ALU.subtract))
                        own(nc.vector.tensor_reduce(span, most, AX.X, ALU.max))
                        dve.wait_ge(transposed, 1)
                        nc.vector.tensor_copy(wini, ip[0:SETS, 6, 0:P]).then_inc(spilled, 1)
                        for k, dst in ((0, src_idx), (1, rel), (2, types)):
                            for a in range(SETS):
                                own(nc.vector.tensor_copy(
                                    dst[:, a * ROW:(a + 1) * ROW].rearrange("p (g q) -> p q g", q=GROUP),
                                    ip[:, SETS * k + a, :].rearrange("p (q g) -> p q g", q=GROUP)))
                        own(nc.vector.tensor_reduce(morer, ip[0:1, 7, 0:P], AX.X, ALU.max))
                        own(nc.vector.tensor_copy(spani, morer))
                        own(nc.vector.tensor_scalar(more[0:1, 0:1], spani, WIN.bit_length() - 1, None,
                                                    ALU.logical_shift_right))
                        own(nc.vector.tensor_copy(mayber, more[0:1, 0:1]))
                        dve.wait_ge(moved, 32)
                        dve.wait_ge(consts, 1)
                        own(nc.vector.tensor_copy(basef, win_base[0:1, :]))
                        own(nc.vector.tensor_reduce(minr, basef[:, 0:STEPS * GROUPS].rearrange("o (s g) -> o s g", g=GROUPS),
                                                    AX.X, ALU.min))
                        own(nc.vector.tensor_tensor(touch, minr.unsqueeze(1).to_broadcast([1, NB, STEPS]),
                                                    endr.unsqueeze(2).to_broadcast([1, NB, STEPS]), ALU.is_le))
                        own(nc.vector.tensor_tensor(touch, touch, stepr.unsqueeze(1).to_broadcast([1, NB, STEPS]), ALU.mult))
                        own(nc.vector.tensor_reduce(lastr, touch, AX.X, ALU.max))
                        own(nc.vector.tensor_tensor(lastr, lastr, br, ALU.subtract))
                        own(nc.vector.tensor_tensor_scan(timer, lastr, lastr, 0.0, ALU.max, ALU.max))
                        own(nc.vector.tensor_tensor(timer, timer, br, ALU.add))
                        own(nc.vector.tensor_scalar(mayber, mayber, float(2 * STEPS), 1.0, ALU.mult, ALU.add))
                        own(nc.vector.tensor_scalar(timer, timer, mayber, None, ALU.add))
                        own(nc.vector.tensor_tensor(hit, timer.unsqueeze(1).to_broadcast([1, STEPS, NB]),
                                                    stepr.unsqueeze(2).to_broadcast([1, STEPS, NB]), ALU.is_equal))
                        own(nc.vector.memset(hit[:, STEPS - 1:STEPS, :], 0.0))
                        own(nc.vector.tensor_reduce(tailr, hit.rearrange("o s b -> o (s b)"), AX.X, ALU.add))
                        own(nc.vector.tensor_copy(tail_start[0:1, :], tailr))
                        own(nc.vector.tensor_scalar(br, br, float(-SPARE_BLOCK), None, ALU.add))
                        own(nc.vector.tensor_tensor(hit, hit, br.unsqueeze(1).to_broadcast([1, STEPS, NB]), ALU.mult))
                        own(nc.vector.tensor_reduce(blockr, hit, AX.X, ALU.add))
                        nc.vector.tensor_scalar(step_block[0:1, :], blockr, float(SPARE_BLOCK), None, ALU.add)

                    @block.tensor
                    def _(pe):
                        pe.wait_ge(consts, 1)
                        pe.wait_ge(masked, 1)
                        pe.wait_ge(own_s, 8)
                        for k in range(3):
                            for a in range(SETS):
                                for q in range(GROUP):
                                    c = a * ROW + q * P
                                    nc.tensor.transpose(ip[:, SETS * k + a, q * P:(q + 1) * P], frow[k][:, c:c + P],
                                                        ident[:, :])
                        nc.tensor.transpose(ip[0:SETS, 6, 0:P], least, ident[:, :])
                        nc.tensor.transpose(ip[0:1, 7, 0:P], span, ident[:, :]).then_inc(transposed, 1)

        def first_norm():
            with ExitStack() as tmp:
                st = tmp.enter_context(sbuf("st", [P, NB, 6]))
                mean, var, rstd, shift = (tmp.enter_context(sbuf(f"c{k}", [P, NB]))[:, :] for k in range(4))
                h_nodes = acc[:, :, :].rearrange("p a n -> p (a n)")[:, 0:NB * D].rearrange("p (b d) -> p b d", d=D)
                parts = 5
                per = NB // parts
                with phase(nc, bank, "own_s", "var_s", "root", "scaled", "h_done", "stored") as (block, sems):
                    own_s, var_s, root, scaled, h_done, stored = sems

                    @block.vector
                    def _(dve):
                        own = Chain(dve, own_s)
                        with dve.Fori(0, NB) as b:
                            nc.vector.bn_stats(st[:, bass.ds(b, 1), :], x_nodes[:, bass.ds(b, 1), :]).then_inc(own_s, 1)
                        dve.wait_ge(own_s, NB)
                        own.n = NB
                        m0, v0, m1, v1 = st[:, :, 1], st[:, :, 2], st[:, :, 4], st[:, :, 5]
                        own(nc.vector.tensor_tensor(mean, m0, m1, ALU.subtract))
                        own(nc.vector.tensor_scalar(mean, mean, 0.5, None, ALU.mult))
                        own(nc.vector.tensor_tensor(rstd, mean, mean, ALU.mult))
                        own(nc.vector.tensor_tensor(var, v0, v1, ALU.add))
                        own(nc.vector.tensor_scalar(var, var, 1.0 / D, LN_EPS, ALU.mult, ALU.add))
                        own(nc.vector.tensor_tensor(var, var, rstd, ALU.add))
                        own(nc.vector.tensor_tensor(mean, m0, m1, ALU.add))
                        nc.vector.tensor_scalar(mean, mean, -0.5, None, ALU.mult).then_inc(var_s, 1)
                        dve.wait_ge(root, 1)
                        own(nc.vector.reciprocal(rstd, rstd))
                        nc.vector.tensor_tensor(shift, mean, rstd, ALU.mult).then_inc(scaled, 1)

                    @block.scalar
                    def _(act):
                        act.wait_ge(var_s, 1)
                        nc.scalar.activation(rstd, var, ACT.Sqrt).then_inc(root, 1)
                        act.wait_ge(scaled, 1)
                        with act.Fori(0, NB) as b:
                            one = bass.ds(b, 1)
                            nc.scalar.activation(h_nodes[:, one, :].rearrange("p b d -> p (b d)"),
                                                 x_nodes[:, one, :].rearrange("p b d -> p (b d)"),
                                                 ACT.Relu, bias=shift[:, one], scale=rstd[:, one]).then_inc(h_done, 1)

                    @block.sync
                    def _(sp):
                        for q in range(parts):
                            sp.wait_ge(h_done, per * (q + 1))
                            sp.dma_start(rows128[0][q * per * P:(q + 1) * per * P, :].rearrange("(b p) d -> p b d", p=P),
                                         h_nodes[:, q * per:(q + 1) * per, :]).then_inc(stored, 16)
                        sp.wait_ge(stored, 16 * parts)

        def start_sums():
            with phase(nc, bank, "none") as (block, _sems):
                @block.vector
                def _(dve):
                    nc.vector.memset(acc[:, 0, :], 0.0)

                @block.gpsimd
                def _(pool):
                    nc.gpsimd.memset(acc[:, 1, :], 0.0)

        def first_round():
            with phase(nc, bank, "none") as (block, _sems):
                @block.vector
                def _(dve):
                    nc.vector.tensor_copy(win[0:1, :], win_base[0:1, :])
                    nc.vector.tensor_copy(iota_row[:, :], iota_row0[:, 0:WIN])
                    nc.vector.tensor_copy(iota_col[:, :], iota_col0[:, :])

        def next_round():
            with phase(nc, bank, "none") as (block, _sems):
                @block.vector
                def _(dve):
                    nc.vector.tensor_scalar(iota_row[:, :], iota_row[:, :], float(WIN), None, ALU.add)
                    nc.vector.tensor_scalar(iota_col[:, :], iota_col[:, :], float(WIN), None, ALU.add)
                    nc.vector.tensor_scalar(win[0:1, :], win[0:1, :], WIN, SPARE, ALU.add, ALU.min)

        def edge_pass(table, width, work, rel_emb=None, edge_net=None, prologue=None):
            first_round()
            two = width == H or rel_emb is not None
            n_sums = 2 if (two or edge_net) else 1
            rounds = nc.values_load(more[0:1, 0:1], min_val=0, max_val=NPAD // WIN) + 1
            with ExitStack() as tmp:
                ring = tmp.enter_context(sbuf("ring", [P, RING, width]))
                onehot = tmp.enter_context(sbuf("onehot", [P, 2, HALF, WIN]))
                idx = tmp.enter_context(sbuf("idx", [P, 2, HALF], I32))
                sums = tmp.enter_context(psum("sums", [P, 2, 512]))
                bufs = work.buffers(tmp)
                names = ["idx_ready", "onehot_ready", "tiles_done", "added", "finished", "block_in", "late_in", "block_out",
                         "pe_result", "act_result", "dve_result", "pe_late", "act_late", "dve_late",
                         "small_loaded", "large_loaded"]
                if rel_emb is not None:
                    iota16 = tmp.enter_context(sbuf("iota16", [P, REL_BLOCKS * P], F16))
                    onehot16 = tmp.enter_context(sbuf("onehot16", [P, 2, HALF, WIN], F16))
                    ones16 = tmp.enter_context(sbuf("ones16", [P, P], F16))
                    type_hot = tmp.enter_context(sbuf("type_hot", [P, HALF, REL_BLOCKS * P], F16))
                    counts = tmp.enter_context(sbuf("counts", [P, 2, REL_BLOCKS, WIN]))
                    counts_ps = tmp.enter_context(psum("counts_ps", [P, 2, 512]))
                    names += ["type_hot_ready", "counted", "counts_ready", "consts_ready"]
                if edge_net:
                    (b1, w2, b2) = edge_net
                    onehot_t = tmp.enter_context(sbuf("onehot_t", [WIN, 2, HALF * P]))
                    relb = tmp.enter_context(sbuf("relb", [WIN, 2, HALF * P]))
                    ywin = tmp.enter_context(sbuf("ywin", [WIN, GROUPS, D]))
                    hidden = tmp.enter_context(sbuf("hidden", [P, 2, GROUP, P]))
                    weight = tmp.enter_context(sbuf("weight", [P, 2, GROUP]))
                    onehot_w = tmp.enter_context(sbuf("onehot_w", [P, 2, GROUP, WIN]))
                    neg_ident = tmp.enter_context(sbuf("neg_ident", [P, P]))
                    zt = tmp.enter_context(psum("zt", [P, 2, GROUP, P]))
                    dot = tmp.enter_context(psum("dot", [P, 512]))
                    names += ["rel_loaded0", "rel_loaded1", "z_done", "relu_done", "dot_done", "weight_done",
                              "weighted", "consts_ready"] + [f"ywin_loaded{g}" for g in range(GROUPS)]

                def programs(block, sems, loop):
                    sem = dict(zip(names, sems))
                    tiles_done, added, finished = sem["tiles_done"], sem["added"], sem["finished"]
                    idx_ready, onehot_ready = sem["idx_ready"], sem["onehot_ready"]
                    work.bind(sem, bufs, loop == "edges")

                    def over(eng, per_tile, per_tile_last=None):
                        def step(i, works, per_tile=per_tile):
                            due = [[w, 0] for w in works]
                            for k in range(RING):
                                per_tile(i, k)
                                for one in due:
                                    while one[1] <= k:
                                        one[1] = next(one[0], RING)
                            for w, _ in due:
                                assert next(w, None) is None, "all of a block's work has its place in the step"

                        def block_at(i):
                            return eng.value_load(step_block[0:1, bass.ds(i, 1)], min_val=0, max_val=SPARE_BLOCK)

                        if loop == "edges":
                            work.credits(eng)
                            step(0, [work.part(eng, 0, SPARE_BLOCK, BANKS_FREE)] if work.LATE else [])

                            def full_step(i, per_tile):
                                b = block_at(i)
                                added_before = i * GROUPS + BANKS_FREE
                                if work.LATE:
                                    works = [work.late_part(eng, i - 1, block_at(i - 1)), work.part(eng, i, b, added_before)]
                                    step(i, works[::-1] if eng is nc.sync else works, per_tile)
                                else:
                                    step(i, [work.part(eng, i - 1, b, added_before)], per_tile)

                            with eng.Fori(1, STEPS - (1 if per_tile_last else 0)) as i:
                                full_step(i, per_tile)
                            if per_tile_last:
                                full_step(STEPS - 1, per_tile_last)
                            work.leave(eng, STEPS - 1)
                        else:
                            start = eng.value_load(tail_start[0:1, 0:1], min_val=0, max_val=LAST)
                            work.credits(eng)
                            with eng.Fori(0, LAST + 1 - start) as i:
                                b = nc.s_assert_within(start + i, 0, LAST, skip_runtime_bounds_check_because="i ends at LAST")
                                for _ in work.part(eng, i, b, None):
                                    pass
                                if work.LATE:
                                    for _ in work.late_part(eng, i, b):
                                        pass

                    BANKS_FREE = 2

                    @block.gpsimd
                    def _(pool):
                        if loop != "edges":
                            return
                        with pool.Fori(0, STEPS) as i:
                            for k in range(RING):
                                h, c = divmod(k, HALF)
                                if c == 0:
                                    pool.wait_ge(idx_ready, i * 2 + (h + 1))
                                pool.wait_ge(tiles_done, i * RING + (k + 1))
                                pool.nop(nofuse=True)
                                nc.gpsimd.indirect_dma_start(
                                    ring[:, k, :], None, table,
                                    bass.IndirectOffsetOnAxis(ap=idx[:, h, c:c + 1].bitcast(U32), axis=0),
                                ).then_inc(gathered[k], 16)

                    @block.scalar
                    def _(act):
                        def load_rel(i, h):
                            act.wait_ge(onehot_ready, (i - 1) * 2 + (h + 1))
                            load_targets(i, h)

                        def load_targets(i, h):
                            act.dma_start(relb[:, h, :].rearrange("p (g j) -> p g j", j=ROW),
                                          rel_rows[bass.ds(i * GROUPS + h * 2, 2), :].unsqueeze(0).to_broadcast((WIN, 2, ROW))
                                          ).then_inc(sem[f"rel_loaded{h}"], 16)

                        def load_window(i, g):
                            w = act.value_load(win[0:1, bass.ds(i * GROUPS + g, 1)], min_val=0, max_val=SPARE)
                            act.wait_ge(tiles_done, i * RING + GROUP * (g + 1))
                            act.dma_start(ywin[:, g, :], table[bass.ds(w, WIN), 0:D]).then_inc(sem[f"ywin_loaded{g}"], 16)

                        def stage(i, h, col):
                            nc.scalar.copy(idx[:, h, :], src_idx[:, bass.ds(col, HALF)]).then_inc(idx_ready, 1)

                        def tile(i, k):
                            g, q = divmod(k, GROUP)
                            if k % HALF == HALF - 1:
                                for j in range(k - HALF + 1, k + 1):
                                    act.wait_ge(gathered[j], i * 16 + 16)
                                act.nop(nofuse=True)
                                stage(i, k // HALF, (i + 1) * RING + k // HALF * HALF)
                            if rel_emb is not None and q == GROUP - 1:
                                act.wait_ge(sem["counted"], i * GROUPS + (g + 1))
                                nc.scalar.copy(counts[:, g % 2, :, :],
                                               counts_ps[:, g % 2, 0:REL_BLOCKS * WIN].rearrange("p (m j) -> p m j", j=WIN)
                                               ).then_inc(sem["counts_ready"], 1)
                            if edge_net and q == 0:
                                if g % 2 == 0:
                                    load_rel(i + 1, g // 2)
                                load_window(i + (g + 2) // GROUPS, (g + 2) % GROUPS)
                                act.wait_ge(sem["z_done"], i * GROUPS + (g + 1))
                                nc.scalar.activation(hidden[:, g % 2, :, :], zt[:, g % 2, :, :], ACT.Relu,
                                                     bias=b1).then_inc(sem["relu_done"], 1)
                                act.wait_ge(sem["dot_done"], i * GROUPS + (g + 1))
                                nc.scalar.activation(weight[:, g % 2, :], dot[:, 0:GROUP], ACT.Sigmoid,
                                                     bias=b2).then_inc(sem["weight_done"], 1)

                        if loop == "edges":
                            for h in range(2):
                                stage(0, h, h * HALF)
                            if edge_net:
                                for k in range(2):
                                    load_targets(0, k)
                                    load_window(0, k)
                        over(act, tile)
                        if edge_net and loop == "edges":
                            for k in range(2):
                                act.wait_ge(sem[f"rel_loaded{k}"], STEPS * 16 + 16)
                                act.wait_ge(sem[f"ywin_loaded{k}"], STEPS * 16 + 16)

                    @block.sync
                    def _(sp):
                        if prologue and loop == "edges":
                            prologue(sp, sem["small_loaded"], sem["large_loaded"])

                        over(sp, lambda i, k: None)

                    @block.vector
                    def _(dve):
                        def one_hots(i, h):
                            dve.wait_ge(tiles_done, i * RING + HALF * (h + 1))
                            cols = rel[:, bass.ds(i * RING + h * HALF, HALF)].unsqueeze(2).to_broadcast([P, HALF, WIN])
                            places = iota_row[:, :].unsqueeze(1).to_broadcast([P, HALF, WIN])
                            if edge_net:
                                dve.wait_ge(sem[f"rel_loaded{h}"], i * 16 + 16)
                                nc.vector.tensor_scalar(onehot_t[:, h, :], relb[:, h, :], iota_col[0:WIN, 0:1], None,
                                                        ALU.is_equal)
                            if rel_emb is not None:
                                nc.vector.tensor_tensor(onehot16[:, h, :, :], places, cols, ALU.is_equal)
                            nc.vector.tensor_tensor(onehot[:, h, :, :], places, cols, ALU.is_equal).then_inc(onehot_ready, 1)

                        def type_hots(i, g):
                            if rel_emb is not None:
                                dve.wait_ge(tiles_done, i * RING + GROUP * (g + 3))
                                for q in range(GROUP):
                                    k = g * GROUP + q
                                    last = nc.vector.tensor_scalar(type_hot[:, k % HALF, :], iota16[:, :],
                                                                   types[:, bass.ds(i * RING + k, 1)], None, ALU.is_equal)
                                last.then_inc(sem["type_hot_ready"], 1)

                        def tile(i, k):
                            g, q = divmod(k, GROUP)
                            if q == 0 and g % 2 == 0:
                                one_hots(i + g // 2, 1 - g // 2)
                            if q == 0:
                                type_hots(i + (g + 1) // GROUPS, (g + 1) % GROUPS)
                            if edge_net and q == 0:
                                dve.wait_ge(sem["weight_done"], i * GROUPS + (g + 1))
                                dve.wait_ge(tiles_done, i * RING + GROUP * (g + 3))
                                j = k % HALF
                                nc.vector.tensor_tensor(onehot_w[:, g % 2, :, :], onehot[:, g // 2, j:j + GROUP, :],
                                                        weight[:, g % 2, :].unsqueeze(2).to_broadcast([P, GROUP, WIN]),
                                                        ALU.mult).then_inc(sem["weighted"], 1)
                            if q < GROUP - 1:
                                return
                            w = dve.value_load(win[0:1, bass.ds(i * GROUPS + g, 1)], min_val=0, max_val=SPARE)
                            dve.wait_ge(tiles_done, i * RING + (GROUP * (g + 1) + RING))
                            dve.wait_ge(added, i * GROUPS + (g + 2))
                            nc.vector.tensor_tensor(
                                acc[:, 0:n_sums, bass.ds(w, WIN)], acc[:, 0:n_sums, bass.ds(w, WIN)],
                                sums[:, g % 2, 0:n_sums * WIN].rearrange("p (a j) -> p a j", j=WIN),
                                ALU.add).then_inc(added, 1)

                        if loop == "edges":
                            dve.sem_inc(added, 2)
                            if rel_emb is not None:
                                nc.vector.memset(ones16[:, :], 1.0)
                                for m in range(REL_BLOCKS):
                                    last = nc.vector.tensor_scalar(iota16[:, m * P:(m + 1) * P], iota_row0[:, :],
                                                                   float(m * P), None, ALU.add)
                                last.then_inc(sem["consts_ready"], 1)
                                dve.wait_ge(sem["consts_ready"], 1)
                            if edge_net:
                                nc.vector.tensor_scalar(neg_ident[:, :], ident[:, :], -1.0, None,
                                                        ALU.mult).then_inc(sem["consts_ready"], 1)
                            one_hots(0, 0)
                            if rel_emb is not None:
                                dve.wait_ge(tiles_done, RING)
                                for q in range(GROUP):
                                    last = nc.vector.tensor_scalar(type_hot[:, q, :], iota16[:, :], types[:, q:q + 1],
                                                                   None, ALU.is_equal)
                                last.then_inc(sem["type_hot_ready"], 1)
                        over(dve, tile)

                    @block.tensor
                    def _(pe):
                        def tile_sum(ap, lhs, rhs, first, last=False):
                            return nc.tensor.matmul(ap, lhs, rhs, start=first, stop=last, skip_group_check=True)

                        def hidden_net(i, k):
                            g, q = divmod(k, GROUP)
                            if k % HALF == 0:
                                pe.wait_ge(onehot_ready, i * 2 + (k // HALF + 1))
                            pe.wait_ge(gathered[k], i * 16 + 16)
                            if q == 0:
                                pe.wait_ge(sem[f"ywin_loaded{g}"], i * 16 + 16)
                            nc.tensor.matmul(zt[:, g % 2, q, :], ring[:, k, 0:D], neg_ident[:, :], start=True, stop=False)
                            last = nc.tensor.matmul(zt[:, g % 2, q, :], ywin[:, g, :],
                                                    onehot_t[:, g // 2, (k % HALF) * P:(k % HALF + 1) * P],
                                                    start=False, stop=True)
                            if q == GROUP - 1:
                                last.then_inc(sem["z_done"], 1)

                        def net_tile(i, k, ahead=True):
                            g, q = divmod(k, GROUP)
                            if q == 0:
                                pe.wait_ge(sem["relu_done"], i * GROUPS + (g + 1))
                                pe.wait_ge(sem["weight_done"], i * GROUPS + g)
                                for j in range(GROUP):
                                    last = nc.tensor.matmul(dot[:, j:j + 1], hidden[:, g % 2, j, :], w2, start=True, stop=True)
                                last.then_inc(sem["dot_done"], 1)
                            if k + GROUP < RING:
                                hidden_net(i, k + GROUP)
                            elif ahead:
                                hidden_net(i + 1, k + GROUP - RING)
                            if q < GROUP - 1:
                                return
                            pe.wait_ge(added, i * GROUPS + (g + 1))
                            pe.wait_ge(sem["weighted"], i * GROUPS + (g + 1))
                            for j in range(GROUP):
                                hot = onehot_w[:, g % 2, j, :]
                                tile_sum(sums[:, g % 2, 0:WIN], ring[:, g * GROUP + j, D:2 * D], hot, j == 0)
                                last = tile_sum(sums[:, g % 2, WIN:2 * WIN], ones[:, :], hot, False, j == GROUP - 1)
                            last.then_inc(tiles_done, GROUP)

                        def tile(i, k):
                            g, q = divmod(k, GROUP)
                            if k % HALF == 0:
                                pe.wait_ge(onehot_ready, i * 2 + (k // HALF + 1))
                            if q == 0:
                                pe.wait_ge(added, i * GROUPS + (g + 1))
                            pe.wait_ge(gathered[k], i * 16 + 16)
                            hot = onehot[:, g // 2, k % HALF, :]
                            if rel_emb is None:
                                for a in range(width // D):
                                    last = tile_sum(sums[:, g % 2, a * WIN:(a + 1) * WIN], ring[:, k, a * D:(a + 1) * D],
                                                    hot, q == 0 and a == 0, q == GROUP - 1)
                            else:
                                hot16 = onehot16[:, g // 2, k % HALF, :]
                                if q == 0:
                                    pe.wait_ge(sem["type_hot_ready"], i * GROUPS + (g + 1))
                                tile_sum(sums[:, g % 2, 0:WIN], ring[:, k, :], hot, q == 0)
                                tile_sum(sums[:, g % 2, WIN:2 * WIN], ones16[:, :], hot16, False)
                                for m in range(REL_BLOCKS):
                                    last = tile_sum(counts_ps[:, g % 2, m * WIN:(m + 1) * WIN],
                                                    type_hot[:, k % HALF, m * P:(m + 1) * P], hot16,
                                                    q == 0 and m == 0, q == GROUP - 1 and m == REL_BLOCKS - 1)
                                if q == GROUP - 1:
                                    last.then_inc(sem["counted"], 1)
                                    pe.wait_ge(sem["counts_ready"], i * GROUPS + (g + 1))
                                    for m in range(REL_BLOCKS):
                                        last = tile_sum(sums[:, g % 2, 0:WIN], rel_emb[:, m, :], counts[:, g % 2, m, :],
                                                        False, m == REL_BLOCKS - 1)
                            if q == GROUP - 1:
                                last.then_inc(tiles_done, GROUP)

                        if loop == "edges":
                            pe.sem_inc(tiles_done, RING)
                            if edge_net:
                                pe.wait_ge(sem["consts_ready"], 1)
                                for k in range(GROUP):
                                    hidden_net(0, k)
                        if edge_net:
                            over(pe, net_tile, lambda i, k: net_tile(i, k, ahead=False))
                        else:
                            over(pe, tile)

                with nc.Fori(0, rounds):
                    with phase(nc, bank, *names, pool_dmas=gathered) as (block, sems):
                        programs(block, sems, "edges")
                    next_round()
                with phase(nc, bank, *names) as (block, sems):
                    programs(block, sems, "blocks")

        class Work:
            LATE = False

            def bind(self, sem, bufs, in_pass):
                self.sem, self.b, self.in_pass = sem, bufs, in_pass
                self.pe = Results(sem["pe_result"], self.PE)
                self.act = Results(sem["act_result"], self.ACT)
                self.dve = Results(sem["dve_result"], self.DVE)
                self.pe2 = self.act2 = self.dve2 = None
                if self.LATE:
                    self.pe2 = Results(sem["pe_late"], self.PE_LATE)
                    self.act2 = Results(sem["act_late"], self.ACT_LATE)
                    self.dve2 = Results(sem["dve_late"], self.DVE_LATE)

            def results(self, eng):
                for e, both in ((nc.tensor, (self.pe, self.pe2)), (nc.scalar, (self.act, self.act2)),
                                (nc.vector, (self.dve, self.dve2))):
                    if e is eng:
                        return both
                return (None, None)

            def credits(self, eng):
                for r in self.results(eng):
                    if r is not None:
                        eng.sem_inc(r.sem, len(r.names))

            def part(self, eng, i, b, added):
                for e, f in ((nc.tensor, self.on_pe), (nc.scalar, self.on_act), (nc.vector, self.on_dve), (nc.sync, self.on_sp)):
                    if e is eng:
                        if not self.LATE:
                            eng.wait_ge(self.sem["finished"], i)
                        yield from f(eng, Maker(eng, self.results(eng)[0], i), i, b, added)

            def late_part(self, eng, i, b):
                for e, f in ((nc.tensor, self.late_pe), (nc.scalar, self.late_act), (nc.vector, self.late_dve),
                             (nc.sync, self.late_sp)):
                    if e is eng:
                        yield from f(eng, Maker(eng, self.results(eng)[1], i), i, b)

            def leave(self, eng, blocks):
                pass

            def loads(self, m, pairs):
                m.apart()
                for dst, src in pairs:
                    m.eng.dma_start(dst, src).then_inc(self.sem["block_in"], 16)

            def loaded(self, m, n):
                m.eng.wait_ge(self.sem["block_in"], m.i * (16 * n) + 16 * n)

            def sums_ready(self, m, added):
                if added is not None:
                    m.eng.wait_ge(self.sem["added"], added)
                m.apart()

            def stored(self, m, stores):
                m.apart()
                for dst, src in stores:
                    m.eng.dma_start(dst, src).then_inc(self.sem["block_out"], 16)

            def finish(self, m, n):
                m.eng.wait_ge(self.sem["block_out"], m.i * (16 * n) + 16 * n)
                m.apart()
                m.eng.sem_inc(self.sem["finished"], 1)

            NORM_DVE = "stats meanvar var_eps rstd shift"
            NORM_ACT = "norm_root h_row"

            def norm_dve(self, m, x, s, at):
                m.done("stats", nc.vector.bn_stats(s[:, 0:6], x), wait=True)
                m.eng.nop(nofuse=True)
                m.done("meanvar", nc.vector.bn_aggr(s[:, 6:8], s[:, 0:6]), wait=True)
                m.done("var_eps", nc.vector.tensor_scalar(s[:, 8:9], s[:, 7:8], LN_EPS, None, ALU.add))
                yield at
                m.need(self.act, "norm_root")
                m.done("rstd", nc.vector.reciprocal(s[:, 10:11], s[:, 9:10]), wait=True)
                m.done("shift", nc.vector.scalar_tensor_tensor(out=s[:, 11:12], in0=s[:, 6:7], scalar=-1.0,
                                                               in1=s[:, 10:11], op0=ALU.mult, op1=ALU.mult))

            def norm_act(self, m, x, s, h, at):
                m.need(self.dve, "var_eps")
                m.done("norm_root", nc.scalar.activation(s[:, 9:10], s[:, 8:9], ACT.Sqrt))
                yield at
                m.need(self.dve, "shift")
                m.done("h_row", nc.scalar.activation(h, x, ACT.Relu, bias=s[:, 11:12], scale=s[:, 10:11]))

        def rows_of(table, b, lo=0, hi=None):
            return table[bass.ds(b * P, P), lo:(hi or table.shape[1])]

        class Layer0(Work):
            PE = "agg_w deg_col h_t h_wl h2_t h_win"
            ACT = "sums_in cleared deg_root norm_root h_row h2_t_sb"
            DVE = ("deg_sb deg1 rdeg rdeg_row1 rdeg_row norm scaled_agg h_t_sb joined new_x "
                   + Work.NORM_DVE + " next_row")

            def __init__(self, wn, wl, w_in, b_in):
                self.wn, self.wl, self.w_in, self.b_in = wn, wl, w_in, b_in

            def buffers(self, tmp):
                s = {n: tmp.enter_context(sbuf(n, [P, w])) for n, w in
                     (("h", D), ("x", D), ("agg", P), ("deg", P), ("ht", P), ("rdeg", P), ("u", D), ("col", 4),
                      ("st", 12), ("h2", D), ("h2t", P), ("row", H))}
                p = {n: tmp.enter_context(psum(n, [P, 512])) for n in ("pa", "pb", "pc")}
                return s, p

            def on_sp(self, sp, m, i, b, added):
                s, _ = self.b
                self.loads(m, [(s["h"][:, :], rows_of(rows128[0], b)), (s["x"][:, :], rows_of(x_rows, b))])
                m.need(self.dve, "rdeg_row")
                self.stored(m, [(rdeg_dram[:, bass.ds(b * P, P)], s["rdeg"][:, :])])
                m.need(self.dve, "new_x")
                self.stored(m, [(rows_of(x_rows, b), s["x"][:, :])])
                m.need(self.dve, "next_row")
                self.stored(m, [(rows_of(rows256[0], b), s["row"][:, :])])
                self.finish(m, 3)
                yield RING

            def on_act(self, act, m, i, b, added):
                s, p = self.b
                blk = bass.ds(b * P, P)
                self.sums_ready(m, added)
                nc.scalar.copy(s["agg"][:, :], acc[:, 0, blk])
                m.done("sums_in", nc.scalar.copy(s["deg"][:, :], acc[:, 1, blk]), wait=True)
                m.apart()
                nc.scalar.copy(acc[:, 0, blk], zeros[:, :])
                m.done("cleared", nc.scalar.copy(acc[:, 1, blk], zeros[:, :]))
                yield 3
                m.need(self.dve, "deg1")
                m.done("deg_root", nc.scalar.activation(s["col"][:, 2:3], s["col"][:, 1:2], ACT.Sqrt))
                yield 7
                yield from self.norm_act(m, s["x"][:, :], s["st"], s["h2"][:, :], 8)
                yield 9
                m.need(self.pe, "h2_t")
                m.done("h2_t_sb", nc.scalar.copy(s["h2t"][:, :], p["pa"][:, 0:P]))

            def on_dve(self, dve, m, i, b, added):
                s, p = self.b
                col = s["col"]
                yield 2
                m.need(self.pe, "deg_col")
                m.done("deg_sb", nc.vector.tensor_copy(node_deg[:, bass.ds(b, 1)], p["pb"][:, P:P + 1]))
                m.done("deg1", nc.vector.tensor_scalar(col[:, 1:2], p["pb"][:, P:P + 1], 1.0, None, ALU.max), wait=True)
                m.done("rdeg", nc.vector.reciprocal(node_rdeg[:, bass.ds(b, 1)], col[:, 1:2]))
                m.done("rdeg_row1", nc.vector.tensor_scalar(s["rdeg"][:, :], s["deg"][:, :], 1.0, None, ALU.max), wait=True)
                m.done("rdeg_row", nc.vector.reciprocal(s["rdeg"][:, :], s["rdeg"][:, :]))
                yield 4
                m.need(self.act, "deg_root")
                m.done("norm", nc.vector.reciprocal(col[:, 3:4], col[:, 2:3]), wait=True)
                m.need(self.pe, "agg_w")
                m.done("scaled_agg", nc.vector.tensor_scalar(s["u"][:, :], p["pb"][:, 0:D], col[:, 3:4], None, ALU.mult))
                m.need(self.pe, "h_t")
                m.done("h_t_sb", nc.vector.tensor_copy(s["ht"][:, :], p["pa"][:, 0:P]))
                yield 6
                m.need(self.dve, "scaled_agg")
                m.need(self.pe, "h_wl")
                m.done("joined", nc.vector.tensor_tensor(s["u"][:, :], s["u"][:, :], p["pc"][:, 0:D], ALU.add), wait=True)
                self.loaded(m, 2)
                m.done("new_x", nc.vector.scalar_tensor_tensor(out=s["x"][:, :], in0=s["u"][:, :], scalar=0.0,
                                                               in1=s["x"][:, :], op0=ALU.max, op1=ALU.add), wait=True)
                yield from self.norm_dve(m, s["x"][:, :], s["st"], 8)
                yield 11
                m.need(self.pe, "h_win")
                m.done("next_row", nc.vector.tensor_tensor(s["row"][:, :], p["pc"][:, 0:H], self.b_in, ALU.add))

            def on_pe(self, pe, m, i, b, added):
                s, p = self.b
                yield 1
                m.need(self.act, "sums_in")
                m.done("agg_w", nc.tensor.matmul(p["pb"][:, 0:D], s["agg"][:, :], self.wn, start=True, stop=True))
                m.done("deg_col", nc.tensor.matmul(p["pb"][:, P:P + 1], s["deg"][:, :], mean_col[:, :], start=True,
                                                   stop=True))
                yield 3
                self.loaded(m, 2)
                m.done("h_t", nc.tensor.transpose(p["pa"][:, 0:P], s["h"][:, :], ident[:, :]))
                yield 5
                m.need(self.dve, "h_t_sb")
                m.done("h_wl", nc.tensor.matmul(p["pc"][:, 0:D], s["ht"][:, :], self.wl, start=True, stop=True))
                yield 9
                m.need(self.act, "h_row")
                m.done("h2_t", nc.tensor.transpose(p["pa"][:, 0:P], s["h2"][:, :], ident[:, :]))
                yield 10
                m.need(self.act, "h2_t_sb")
                m.done("h_win", nc.tensor.matmul(p["pc"][:, 0:H], s["h2t"][:, :], self.w_in, start=True, stop=True))

        class Layer1(Work):
            LATE = True
            PE = "h_t logits gate_t"
            ACT = "cleared exps"
            DVE = "h_t_sb agg logits_sb top topi topf diff neg_conf plus1 recips gate0 gate1 pick0 pick1 gates gates_hi gates_lo"
            PE_LATE = "gate_rows weak0 weak1 up0 up1 down0 up2 down1 up3 down2 down3 moe_t"
            ACT_LATE = "agg_kept h_kept gates_kept weak_relu0 weak_relu1 relu0 relu1 relu2 relu3"
            DVE_LATE = "weak_scaled weak_sum scaled0 scaled1 scaled2 scaled3 moe next_row"
            PE_LAST = " h2_t h2_w"
            ACT_LAST = " norm_root h_row h2_t_sb"
            DVE_LAST = " new_h_t x_part new_x " + Work.NORM_DVE + " next_y next_h"

            def __init__(self, cur, nxt, w, last=None):
                self.cur, self.nxt, self.w, self.last = cur, nxt, w, last
                if last:
                    self.PE_LATE = self.PE_LATE.replace(" moe_t", " h_out") + self.PE_LAST
                    self.ACT_LATE = self.ACT_LATE.replace(" h_kept", " h_t_kept") + self.ACT_LAST
                    self.DVE_LATE = self.DVE_LATE.replace(" next_row", "") + self.DVE_LAST

            def buffers(self, tmp):
                s = {n: tmp.enter_context(sbuf(n, sh)) for n, sh in
                     (("h", [P, H]), ("ht", [P, 2, P]), ("agg", [P, 2, P]), ("rdeg", [P, P]), ("lg", [P, NE + 1]),
                      ("top", [P, 8]), ("topf", [P, 2]), ("col", [P, 8]), ("ecol", [P, 2]), ("g1", [P, NE]),
                      ("g2", [P, NE]), ("gate", [P, NE]), ("gates", [P, 2 * NE]),
                      ("gt", [2 * NE, P]), ("agg2", [P, 2, P]), ("h2", [P, H]),
                      ("weak", [P, NE, P]), ("strong", [P, 2, 4, P]), ("moe", [P, 2, P]), ("row", [P, H]))}
                s["topi"] = tmp.enter_context(sbuf("topi", [P, 8], U32))
                if self.last:
                    s |= {n: tmp.enter_context(sbuf(n, sh)) for n, sh in
                          (("ht2", [P, 2, P]), ("x", [P, D]), ("st", [P, 12]), ("hn", [P, D]), ("hnt", [P, P]), ("u", [P, D]))}
                p = {"hid": tmp.enter_context(psum("hid", [P, 2, 4, P])), "gb": tmp.enter_context(psum("gb", [P, NE, P])),
                     "y": tmp.enter_context(psum("y", [P, 512])), "misc": tmp.enter_context(psum("misc", [P, 512]))}
                return s, p

            def on_sp(self, sp, m, i, b, added):
                s, _ = self.b
                m.need_before(self.act2, "gates_kept")
                self.loads(m, [(s["h"][:, :], rows_of(rows256[self.cur], b)), (s["rdeg"][:, :], rdeg_dram[:, bass.ds(b * P, P)])])
                yield RING

            def on_act(self, act, m, i, b, added):
                s, p = self.b
                yield 4
                m.need(self.dve, "agg")
                m.apart()
                for a in range(2):
                    ins = nc.scalar.copy(acc[:, a, bass.ds(b * P, P)], zeros[:, :])
                m.done("cleared", ins)
                yield 6
                m.need(self.dve, "neg_conf")
                m.done("exps", nc.scalar.activation(s["ecol"][:, :], s["col"][:, 0:2], ACT.Exp))

            def on_dve(self, dve, m, i, b, added):
                s, p = self.b
                col = s["col"]
                yield 4
                m.need(self.pe, "h_t")
                m.need_before(self.act2, "gates_kept")
                m.done("h_t_sb", nc.vector.tensor_copy(s["ht"][:, :, :], p["misc"][:, 0:H].rearrange("p (a j) -> p a j", j=P)))
                self.sums_ready(m, added)
                self.loaded(m, 2)
                m.done("agg", nc.vector.tensor_tensor(s["agg"][:, :, :], acc[:, :, bass.ds(b * P, P)],
                                                      s["rdeg"][:, :].unsqueeze(1).to_broadcast([P, 2, P]), ALU.mult))
                yield 6
                if self.in_pass:
                    dve.wait_ge(self.sem["small_loaded"], self.w["small"])
                m.need(self.pe, "logits")
                lg = s["lg"][:, 0:NE]
                m.done("logits_sb", nc.vector.tensor_tensor(s["lg"][:, :], p["misc"][:, 0:NE + 1],
                                                            self.w["router_b"][:, :], ALU.add), wait=True)
                dve.nop(nofuse=True)
                m.done("top", nc.vector.max(s["top"][:, :], lg), wait=True)
                dve.nop(nofuse=True)
                m.done("topi", nc.vector.max_index(s["topi"][:, :], s["top"][:, :], lg), wait=True)
                m.done("topf", nc.vector.tensor_copy(s["topf"][:, :], s["topi"][:, 0:2]))
                m.done("diff", nc.vector.tensor_tensor(col[:, 0:1], s["top"][:, 1:2], s["top"][:, 0:1], ALU.subtract))
                m.done("neg_conf", nc.vector.tensor_scalar(col[:, 1:2], s["lg"][:, NE:NE + 1], -1.0, None, ALU.mult))
                yield 8
                m.need(self.act, "exps")
                m.done("plus1", nc.vector.tensor_scalar(col[:, 2:4], s["ecol"][:, :], 1.0, None, ALU.add), wait=True)
                m.done("recips", nc.vector.reciprocal(col[:, 4:6], col[:, 2:4]), wait=True)
                m.done("gate0", nc.vector.tensor_tensor(col[:, 6:7], col[:, 4:5], col[:, 5:6], ALU.mult), wait=True)
                m.done("gate1", nc.vector.tensor_tensor(col[:, 7:8], col[:, 6:7], s["ecol"][:, 0:1], ALU.mult), wait=True)
                m.done("pick0", nc.vector.tensor_scalar(s["g1"][:, :], iota_row0[:, 0:NE], s["topf"][:, 0:1], col[:, 6:7],
                                                        ALU.is_equal, ALU.mult))
                m.done("pick1", nc.vector.tensor_scalar(s["g2"][:, :], iota_row0[:, 0:NE], s["topf"][:, 1:2], col[:, 7:8],
                                                        ALU.is_equal, ALU.mult), wait=True)
                m.done("gates", nc.vector.tensor_tensor(s["gate"][:, :], s["g1"][:, :], s["g2"][:, :], ALU.add), wait=True)
                m.done("gates_hi", nc.vector.tensor_copy(s["gates"][:, 0:NE].bitcast(FR), s["gate"][:, :]), wait=True)
                m.done("gates_lo", nc.vector.tensor_tensor(s["gates"][:, NE:2 * NE].bitcast(FR), s["gate"][:, :],
                                                           s["gates"][:, 0:NE], ALU.subtract))

            def on_pe(self, pe, m, i, b, added):
                s, p = self.b
                w = self.w
                yield 3
                if self.in_pass:
                    pe.wait_ge(self.sem["small_loaded"], w["small"])
                self.loaded(m, 2)
                m.need_before(self.act2, "gates_kept")
                for a in range(2):
                    ins = nc.tensor.transpose(p["misc"][:, a * P:(a + 1) * P], s["h"][:, a * P:(a + 1) * P], ident[:, :])
                m.done("h_t", ins)
                yield 5
                m.need(self.dve, "agg")
                cols = [s["ht"][:, k, :] for k in range(2)] + [s["agg"][:, k, :] for k in range(2)]
                for k in range(4):
                    ins = nc.tensor.matmul(p["misc"][:, 0:NE + 1], cols[k], w["router"][:, k, :], start=(k == 0),
                                           stop=(k == 3))
                m.done("logits", ins)
                yield 10
                m.need(self.dve, "gates_lo")
                m.done("gate_t", nc.tensor.matmul(p["misc"][0:2 * NE, 16:16 + P], s["gates"][:, :], ident[:, :], start=True,
                                                  stop=True))

            def late_sp(self, sp, m, i, b):
                s, _ = self.b
                n = 2 if self.last else 1
                if self.last:
                    sp.wait_ge(self.sem["block_out"], i * (16 * n))
                    sp.nop(nofuse=True)
                    sp.dma_start(s["x"][:, :], rows_of(x_rows, b)).then_inc(self.sem["late_in"], 16)
                    m.need(self.dve2, "new_x")
                    self.stored(m, [(rows_of(x_rows, b), s["x"][:, :])])
                m.need(self.dve2, "next_h" if self.last else "next_row")
                self.stored(m, [(rows_of(rows256[self.nxt], b), s["row"][:, :])])
                if not self.in_pass:
                    sp.wait_ge(self.sem["block_out"], i * (16 * n) + 16 * n)
                    sp.nop(nofuse=True)
                yield RING

            def leave(self, eng, blocks):
                if eng is nc.sync:
                    eng.wait_ge(self.sem["block_out"], blocks * (32 if self.last else 16))
                    eng.nop(nofuse=True)

            def late_act(self, act, m, i, b):
                s, p = self.b
                m.need(self.dve, "agg")
                m.need_before(self.pe2, "up3")
                m.need_before(self.dve2, "moe" if self.last else "next_row")
                m.done("agg_kept", nc.scalar.copy(s["agg2"][:, :, :], s["agg"][:, :, :]))
                if self.last:
                    m.need_before(self.dve2, "new_h_t")
                    m.done("h_t_kept", nc.scalar.copy(s["ht2"][:, :, :], s["ht"][:, :, :]))
                else:
                    self.loaded(m, 2)
                    m.done("h_kept", nc.scalar.copy(s["h2"][:, :], s["h"][:, :]))
                m.need(self.pe, "gate_t")
                m.need_before(self.pe2, "down0")
                m.done("gates_kept", nc.scalar.copy(s["gt"][:, :].bitcast(FR), p["misc"][0:2 * NE, 16:16 + P]))
                yield 1
                if self.in_pass:
                    act.wait_ge(self.sem["small_loaded"], self.w["small"])
                for q in range(2):
                    if q:
                        yield 2
                    m.need(self.pe2, f"weak{q}")
                    m.need_before(self.dve2, "weak_sum")
                    for j in range(4):
                        e, mm = 2 * q + j // 2, j % 2
                        ins = nc.scalar.activation(s["weak"][:, 2 * e + mm, :], p["hid"][:, q, j, :], ACT.Relu,
                                                   bias=self.w["weak_b"][:, e, mm:mm + 1])
                    m.done(f"weak_relu{q}", ins)
                for e, at in enumerate((4, 5, 8, 11)):
                    yield at
                    m.need(self.pe2, f"up{e}")
                    if e >= 2:
                        m.need(self.pe2, f"down{e - 2}")
                    else:
                        m.need_before(self.pe2, f"down{e + 2}")
                    for j in range(4):
                        ins = nc.scalar.activation(s["strong"][:, e % 2, j, :], p["hid"][:, e % 2, j, :], ACT.Relu,
                                                   bias=self.w["s1_b"][:, e, j:j + 1])
                    m.done(f"relu{e}", ins)
                if self.last:
                    yield 15
                    m.need(self.dve2, "var_eps")
                    m.done("norm_root", nc.scalar.activation(s["st"][:, 9:10], s["st"][:, 8:9], ACT.Sqrt))
                    m.need(self.dve2, "shift")
                    m.done("h_row", nc.scalar.activation(s["hn"][:, :], s["x"][:, :], ACT.Relu, bias=s["st"][:, 11:12],
                                                         scale=s["st"][:, 10:11]))
                    m.need(self.pe2, "h2_t")
                    m.done("h2_t_sb", nc.scalar.copy(s["hnt"][:, :], p["hid"][:, 1, 0, :]))

            def late_dve(self, dve, m, i, b):
                s, p = self.b
                yield 3
                m.need(self.pe2, "gate_rows")
                m.need(self.act2, "weak_relu1")
                m.need_before(self.pe2, "h_out" if self.last else "moe_t")
                gb = p["gb"]
                wh = s["weak"][:, :, :].rearrange("p (e m) n -> p e m n", m=2)
                m.done("weak_scaled", nc.vector.tensor_tensor(
                    wh, wh, gb[:, 0:NW, :].unsqueeze(2).to_broadcast([P, NW, 2, P]), ALU.mult))
                yield 4
                m.need(self.dve2, "weak_scaled")
                m.done("weak_sum", nc.vector.tensor_reduce(
                    s["moe"][:, :, :], s["weak"][:, :, :].rearrange("p (e m) n -> p m n e", m=2), AX.X, ALU.add))
                for e, at in enumerate((5, 6, 8, 11)):
                    yield at
                    m.need(self.act2, f"relu{e}")
                    m.done(f"scaled{e}", nc.vector.tensor_tensor(
                        s["strong"][:, e % 2, :, :], s["strong"][:, e % 2, :, :],
                        gb[:, NW + e, :].unsqueeze(1).to_broadcast([P, 4, P]), ALU.mult))
                yield 14
                m.need(self.pe2, "down3")
                m.need(self.dve2, "weak_sum")
                m.done("moe", nc.vector.tensor_tensor(s["moe"][:, :, :], s["moe"][:, :, :],
                                                      p["y"][:, 0:H].rearrange("p (m n) -> p m n", n=P), ALU.add),
                       wait=bool(self.last))
                if not self.last:
                    yield 15
                    m.need(self.pe2, "moe_t")
                    dve.wait_ge(self.sem["block_out"], i * 16)
                    m.done("next_row", nc.vector.tensor_tensor(
                        s["row"][:, :].rearrange("p (a j) -> p a j", j=P), s["h2"][:, :].rearrange("p (a j) -> p a j", j=P),
                        p["hid"][:, 0, 0:2, :], ALU.add))
                    return
                m.need(self.act2, "h_t_kept")
                m.done("new_h_t", nc.vector.tensor_tensor(s["ht2"][:, :, :], s["ht2"][:, :, :], s["moe"][:, :, :], ALU.add))
                yield 15
                m.need(self.pe2, "h_out")
                m.done("x_part", nc.vector.tensor_tensor(s["u"][:, :], p["hid"][:, 0, 0, :], self.last["b_out"], ALU.add),
                       wait=True)
                dve.wait_ge(self.sem["late_in"], i * 16 + 16)
                m.done("new_x", nc.vector.tensor_tensor(s["x"][:, :], s["x"][:, :], s["u"][:, :], ALU.add), wait=True)
                x, st = s["x"][:, :], s["st"]
                m.done("stats", nc.vector.bn_stats(st[:, 0:6], x))
                m.need(self.dve2, "stats")
                dve.nop(nofuse=True)
                m.done("meanvar", nc.vector.bn_aggr(st[:, 6:8], st[:, 0:6]), wait=True)
                m.done("var_eps", nc.vector.tensor_scalar(st[:, 8:9], st[:, 7:8], LN_EPS, None, ALU.add))
                m.need(self.act2, "norm_root")
                m.done("rstd", nc.vector.reciprocal(st[:, 10:11], st[:, 9:10]), wait=True)
                m.done("shift", nc.vector.scalar_tensor_tensor(out=st[:, 11:12], in0=st[:, 6:7], scalar=-1.0,
                                                               in1=st[:, 10:11], op0=ALU.mult, op1=ALU.mult))
                m.need(self.pe2, "h2_w")
                dve.wait_ge(self.sem["block_out"], i * 32)
                m.done("next_y", nc.vector.tensor_copy(s["row"][:, 0:D], p["y"][:, 0:D]))
                m.done("next_h", nc.vector.tensor_copy(s["row"][:, D:H], s["hn"][:, :]))

            def late_pe(self, pe, m, i, b):
                s, p = self.b
                w = self.w
                m.need(self.act2, "gates_kept")
                m.need_before(self.dve2, "next_y" if self.last else "moe")
                for e in range(NE):
                    ins = nc.tensor.matmul(p["gb"][:, e, :], w["pick_row"][:, e, :].bitcast(FR), s["gt"][:, :].bitcast(FR),
                                           start=True, stop=True)
                m.done("gate_rows", ins)
                yield 1
                if self.in_pass:
                    pe.wait_ge(self.sem["large_loaded"], w["large"])

                def product(ap, weights):
                    for k in range(2):
                        ins = nc.tensor.matmul(ap, weights(k), s["agg2"][:, k, :], start=(k == 0), stop=(k == 1))
                    return ins

                m.need(self.act2, "agg_kept")
                for q in range(2):
                    if q == 0:
                        m.need_before(self.dve2, "x_part" if self.last else "next_row")
                    else:
                        yield 2
                        m.need_before(self.act2, "h2_t_sb" if self.last else "relu3")
                    for j in range(4):
                        e, mm = 2 * q + j // 2, j % 2
                        ins = product(p["hid"][:, q, j, :], lambda k: w["weak"][:, k, e, mm * P:(mm + 1) * P])
                    m.done(f"weak{q}", ins)

                def up(e):
                    m.need(self.act2, f"weak_relu{e}" if e < 2 else f"relu{e - 2}")
                    for j in range(4):
                        ins = product(p["hid"][:, e % 2, j, :], lambda k: w["s1"][:, k, e, j * P:(j + 1) * P])
                    m.done(f"up{e}", ins)

                def down(e):
                    m.need(self.dve2, f"scaled{e}")
                    for mm in range(2):
                        for k in range(4):
                            ins = nc.tensor.matmul(p["y"][:, mm * P:(mm + 1) * P], w["s2"][:, k, e, mm * P:(mm + 1) * P],
                                                   s["strong"][:, e % 2, k, :], start=False,
                                                   stop=(e == NW - 1 and k == 3), skip_group_check=True)
                    m.done(f"down{e}", ins)

                yield 3
                up(0)
                yield 4
                up(1)
                yield 6
                for mm in range(2):
                    nc.tensor.matmul(p["y"][:, mm * P:(mm + 1) * P], w["s2_b"][:, mm * P:(mm + 1) * P], s["gt"][:, :],
                                     start=(mm == 0), stop=False, skip_group_check=True)
                down(0)
                yield 7
                up(2)
                yield 9
                down(1)
                yield 10
                up(3)
                yield 12
                down(2)
                yield 13
                down(3)
                yield 15
                if not self.last:
                    m.need(self.dve2, "moe")
                    for a in range(2):
                        ins = nc.tensor.transpose(p["hid"][:, 0, a, :], s["moe"][:, a, :], ident[:, :])
                    m.done("moe_t", ins)
                    return
                m.need(self.dve2, "new_h_t")
                for k in range(2):
                    ins = nc.tensor.matmul(p["hid"][:, 0, 0, :], s["ht2"][:, k, :], self.last["w_out"][:, k, :],
                                           start=(k == 0), stop=(k == 1))
                m.done("h_out", ins)
                m.need(self.act2, "h_row")
                m.done("h2_t", nc.tensor.transpose(p["hid"][:, 1, 0, :], s["hn"][:, :], ident[:, :]))
                m.need(self.act2, "h2_t_sb")
                m.done("h2_w", nc.tensor.matmul(p["y"][:, 0:D], s["hnt"][:, :], self.last["w1"], start=True, stop=True))

        class Layer2(Work):
            PE = "agg_t w_col h_t h_w4"
            ACT = "sums_in cleared norm_root h_row"
            DVE = "w_sb h_t_sb part0 part1 part2 new_x " + Work.NORM_DVE

            def __init__(self, cur, w4, b4):
                self.cur, self.w4, self.b4 = cur, w4, b4

            def buffers(self, tmp):
                s = {n: tmp.enter_context(sbuf(n, [P, w])) for n, w in
                     (("h", D), ("x", D), ("agg", P), ("wsum", P), ("ht", P), ("u", D), ("v", D), ("col", 1),
                      ("st", 12), ("h2", D))}
                p = {n: tmp.enter_context(psum(n, [P, 512])) for n in ("pa", "pb", "pc")}
                return s, p

            def on_sp(self, sp, m, i, b, added):
                s, _ = self.b
                self.loads(m, [(s["h"][:, :], rows_of(rows256[self.cur], b, D, H)), (s["x"][:, :], rows_of(x_rows, b))])
                m.need(self.dve, "new_x")
                self.stored(m, [(rows_of(x_rows, b), s["x"][:, :])])
                m.need(self.act, "h_row")
                self.stored(m, [(rows_of(rows128[0], b), s["h2"][:, :])])
                self.finish(m, 2)
                yield RING

            def on_act(self, act, m, i, b, added):
                s, _ = self.b
                blk = bass.ds(b * P, P)
                self.sums_ready(m, added)
                nc.scalar.copy(s["agg"][:, :], acc[:, 0, blk])
                m.done("sums_in", nc.scalar.copy(s["wsum"][:, :], acc[:, 1, blk]), wait=True)
                m.apart()
                nc.scalar.copy(acc[:, 0, blk], zeros[:, :])
                m.done("cleared", nc.scalar.copy(acc[:, 1, blk], zeros[:, :]))
                yield 8
                yield from self.norm_act(m, s["x"][:, :], s["st"], s["h2"][:, :], 10)

            def on_dve(self, dve, m, i, b, added):
                s, p = self.b
                yield 2
                m.need(self.pe, "w_col")
                m.done("w_sb", nc.vector.tensor_copy(s["col"][:, :], p["pb"][:, P:P + 1]))
                yield 5
                m.need(self.pe, "h_t")
                m.done("h_t_sb", nc.vector.tensor_copy(s["ht"][:, :], p["pa"][:, 0:P]))
                self.loaded(m, 2)
                m.need(self.dve, "w_sb")
                m.done("part0", nc.vector.scalar_tensor_tensor(out=s["u"][:, :], in0=s["h"][:, :], scalar=s["col"][:, :],
                                                               in1=p["pb"][:, 0:P], op0=ALU.mult, op1=ALU.subtract))
                yield 7
                m.need(self.pe, "h_w4")
                m.done("part1", nc.vector.tensor_tensor(s["v"][:, :], p["pc"][:, 0:D], self.b4, ALU.add), wait=True)
                m.done("part2", nc.vector.scalar_tensor_tensor(out=s["v"][:, :], in0=s["v"][:, :],
                                                               scalar=node_deg[:, bass.ds(b, 1)], in1=s["u"][:, :],
                                                               op0=ALU.mult, op1=ALU.add), wait=True)
                m.done("new_x", nc.vector.tensor_tensor(s["x"][:, :], s["x"][:, :], s["v"][:, :], ALU.add), wait=True)
                yield from self.norm_dve(m, s["x"][:, :], s["st"], 9)

            def on_pe(self, pe, m, i, b, added):
                s, p = self.b
                yield 1
                m.need(self.act, "sums_in")
                m.done("agg_t", nc.tensor.transpose(p["pb"][:, 0:P], s["agg"][:, :], ident[:, :]))
                m.done("w_col", nc.tensor.matmul(p["pb"][:, P:P + 1], s["wsum"][:, :], mean_col[:, :], start=True, stop=True))
                yield 4
                self.loaded(m, 2)
                m.done("h_t", nc.tensor.transpose(p["pa"][:, 0:P], s["h"][:, :], ident[:, :]))
                yield 6
                m.need(self.dve, "h_t_sb")
                m.done("h_w4", nc.tensor.matmul(p["pc"][:, 0:D], s["ht"][:, :], self.w4, start=True, stop=True))

        class Layer3(Work):
            PE = "agg_w agg_sq h_t h_w"
            ACT = "sums_in squares cleared roots"
            DVE = "h_t_sb h_sq big0 big1 root_deg floor scales scale_deg part0 part1 next_row"

            def __init__(self, cur, nxt, w3):
                self.cur, self.nxt, self.w3 = cur, nxt, w3

            def buffers(self, tmp):
                s = {n: tmp.enter_context(sbuf(n, [P, w])) for n, w in
                     (("h", D), ("x", D), ("agg", P), ("sq", P), ("ht", P), ("u", D), ("n", 5), ("row", D))}
                p = {n: tmp.enter_context(psum(n, [P, 512])) for n in ("pa", "pb", "pc")}
                return s, p

            def on_sp(self, sp, m, i, b, added):
                s, _ = self.b
                pairs = [(s["h"][:, :], rows_of(rows128[self.cur], b))]
                if self.nxt is None:
                    pairs.append((s["x"][:, :], rows_of(x_rows, b)))
                self.loads(m, pairs)
                m.need(self.dve, "next_row")
                self.stored(m, [(rows_of(out if self.nxt is None else rows128[self.nxt], b), s["row"][:, :])])
                self.finish(m, 1)
                yield RING

            def on_act(self, act, m, i, b, added):
                s, _ = self.b
                blk = bass.ds(b * P, P)
                self.sums_ready(m, added)
                m.done("sums_in", nc.scalar.copy(s["agg"][:, :], acc[:, 0, blk]))
                m.done("squares", nc.scalar.activation(s["sq"][:, :], acc[:, 0, blk], ACT.Square), wait=True)
                m.apart()
                m.done("cleared", nc.scalar.copy(acc[:, 0, blk], zeros[:, :]))
                yield 6
                m.need(self.dve, "big1")
                m.done("roots", nc.scalar.activation(s["n"][:, 3:5], s["n"][:, 1:3], ACT.Sqrt))

            def on_dve(self, dve, m, i, b, added):
                s, p = self.b
                n = s["n"]
                rdeg = node_rdeg[:, bass.ds(b, 1)]
                nl = 2 if self.nxt is None else 1
                yield 4
                m.need(self.pe, "h_t")
                m.done("h_t_sb", nc.vector.tensor_copy(s["ht"][:, :], p["pa"][:, 0:P]))
                self.loaded(m, nl)
                m.done("h_sq", nc.vector.tensor_tensor_reduce(out=s["u"][:, :], in0=s["h"][:, :], in1=s["h"][:, :],
                                                              scale=1.0, scalar=0.0, op0=ALU.mult, op1=ALU.add,
                                                              accum_out=n[:, 0:1]), wait=True)
                m.need(self.pe, "agg_sq")
                m.done("big0", nc.vector.tensor_scalar(n[:, 1:2], p["pb"][:, D:D + 1], TINY, None, ALU.max))
                m.done("big1", nc.vector.tensor_scalar(n[:, 2:3], n[:, 0:1], TINY, None, ALU.max))
                yield 6
                m.need(self.act, "roots")
                m.done("root_deg", nc.vector.tensor_scalar(n[:, 3:4], n[:, 3:4], rdeg, None, ALU.mult), wait=True)
                m.done("floor", nc.vector.tensor_scalar(n[:, 3:5], n[:, 3:5], L2_EPS, None, ALU.max), wait=True)
                m.done("scales", nc.vector.reciprocal(n[:, 3:5], n[:, 3:5]), wait=True)
                m.done("scale_deg", nc.vector.tensor_scalar(n[:, 3:4], n[:, 3:4], rdeg, None, ALU.mult), wait=True)
                m.need(self.pe, "h_w")
                m.done("part0", nc.vector.scalar_tensor_tensor(out=s["u"][:, :], in0=p["pb"][:, 0:D], scalar=n[:, 3:4],
                                                               in1=self.w3[:, 2, :], op0=ALU.mult, op1=ALU.add), wait=True)
                m.done("part1", nc.vector.scalar_tensor_tensor(out=s["u"][:, :], in0=p["pc"][:, 0:D], scalar=n[:, 4:5],
                                                               in1=s["u"][:, :], op0=ALU.mult, op1=ALU.add), wait=True)
                if self.nxt is None:
                    m.done("next_row", nc.vector.tensor_tensor(s["row"][:, :], s["u"][:, :], s["x"][:, :], ALU.add))
                else:
                    m.done("next_row", nc.vector.tensor_scalar(s["row"][:, :], s["u"][:, :], 0.0, None, ALU.max))

            def on_pe(self, pe, m, i, b, added):
                s, p = self.b
                yield 1
                m.need(self.act, "squares")
                m.done("agg_w", nc.tensor.matmul(p["pb"][:, 0:D], s["agg"][:, :], self.w3[:, 0, :], start=True, stop=True))
                m.done("agg_sq", nc.tensor.matmul(p["pb"][:, D:D + 1], s["sq"][:, :], ones[:, 0:1], start=True, stop=True))
                yield 3
                self.loaded(m, 2 if self.nxt is None else 1)
                m.done("h_t", nc.tensor.transpose(p["pa"][:, 0:P], s["h"][:, :], ident[:, :]))
                yield 5
                m.need(self.dve, "h_t_sb")
                m.done("h_w", nc.tensor.matmul(p["pc"][:, 0:D], s["ht"][:, :], self.w3[:, 1, :], start=True, stop=True))

        def load(pairs):
            with phase(nc, bank, "loaded") as (block, (loaded,)):
                @block.sync
                def _(sp):
                    for dst, src in pairs:
                        sp.dma_start(dst, src).then_inc(loaded, 16)
                    sp.wait_ge(loaded, 16 * len(pairs))

        def expert_tables(lay):
            w = {
                "weak": big[:, 0:2048].rearrange("p (k e f) -> p k e f", k=2, e=NW),
                "s1": big[:, 2048:6144].rearrange("p (k e f) -> p k e f", k=2, e=NW),
                "s2": big[:, 6144:10240].rearrange("p (k e f) -> p k e f", k=4, e=NW),
                "router": lay.enter_context(sbuf("router", [P, 4, NE + 1])),
                "router_b": lay.enter_context(sbuf("router_b", [P, NE + 1])),
                "weak_b": lay.enter_context(sbuf("weak_b", [P, NW, 2])),
                "s1_b": lay.enter_context(sbuf("s1_b", [P, NW, 4])),
                "s2_b": lay.enter_context(sbuf("s2_b", [2 * NE, H])),
                "pick_row": lay.enter_context(sbuf("pick_row", [2 * NE, NE, P])),
                "small": 16 * 15, "large": 16 * 8,
            }
            row = lay.enter_context(sbuf("row", [2 * NE, 1]))
            with phase(nc, bank, "own_s") as (block, (own_s,)):
                @block.gpsimd
                def _(pool):
                    nc.gpsimd.memset(w["router"][:, :, NE:NE + 1], 0.0)
                    nc.gpsimd.memset(w["s2_b"][:, :], 0.0)

                @block.vector
                def _(dve):
                    own = Chain(dve, own_s)
                    own(nc.vector.tensor_scalar(row[:, :], iota_col0[0:2 * NE, :], float(NE), float(-NE), ALU.is_ge, ALU.mult))
                    own(nc.vector.tensor_tensor(row[:, :], row[:, :], iota_col0[0:2 * NE, :], ALU.add))
                    own(nc.vector.tensor_tensor(w["pick_row"][:, :, :].bitcast(FR),
                                                iota_row0[0:2 * NE, 0:NE].unsqueeze(2).to_broadcast([2 * NE, NE, P]),
                                                row[:, :].unsqueeze(2).to_broadcast([2 * NE, NE, P]), ALU.is_equal))
            return w

        def load_experts(l, w):
            def prologue(sp, small, large):
                count = {small: 0, large: 0}

                def go(dst, src, sem=small):
                    sp.dma_start(dst, src).then_inc(sem, 16)
                    count[sem] += 16

                with nc.allow_non_contiguous_dma("router rows and columns of biases"):
                    go(w["router"][:, :, 0:NE], t["L1_gnn_router_W"][l, :, :].rearrange("(k p) f -> p k f", p=P))
                    for k in range(2):
                        go(w["router"][:, k, NE:NE + 1], t["L1_gnn_conf_W"][l, k * P:(k + 1) * P, :])
                    for e in range(NW):
                        go(w["weak_b"][:, e, :], t["L1_gnn_weak_b"][l, e, :].rearrange("(m p) -> p m", p=P))
                        go(w["s1_b"][:, e, :], t["L1_gnn_strong_b1"][l, e, :].rearrange("(m p) -> p m", p=P))
                for k in range(2):
                    go(w["s2_b"][k * NE + NW:(k + 1) * NE, :], t["L1_gnn_strong_b2"][l, :, :])
                go(w["router_b"][:, 0:NE], bcast_vec(t["L1_gnn_router_b"][l, :]))
                go(w["router_b"][:, NE:NE + 1], bcast_vec(t["L1_gnn_conf_b"][l, :]))
                for k in range(4):
                    rows = slice(k * P, (k + 1) * P)
                    if k < 2:
                        go(w["weak"][:, k, :, :], t["L1_gnn_weak_W"][l, :, rows, :].rearrange("e p f -> p e f"), large)
                        go(w["s1"][:, k, :, :], t["L1_gnn_strong_W1"][l, :, rows, :].rearrange("e p f -> p e f"), large)
                    go(w["s2"][:, k, :, :], t["L1_gnn_strong_W2"][l, :, rows, :].rearrange("e p f -> p e f"), large)
                assert (count[small], count[large]) == (w["small"], w["large"]), count

            return prologue

        def layer3_weights(lay):
            w3 = [lay.enter_context(sbuf("w3", [P, 3, D])) for _ in range(3)]
            with ExitStack() as tmp:
                raw = tmp.enter_context(sbuf("raw", [P, 3, 2, D]))
                pt = tmp.enter_context(psum("pt", [P, 3, 512]))
                with phase(nc, bank, "loaded", "done") as (block, (loaded, done)):
                    @block.sync
                    def _(sp):
                        for l in range(3):
                            sp.dma_start(raw[:, l, 0, :], t["L3_gnn_Wl"][l, :, :]).then_inc(loaded, 16)
                            sp.dma_start(raw[:, l, 1, :], t["L3_gnn_Wr"][l, :, :]).then_inc(loaded, 16)
                            sp.dma_start(w3[l][:, 2, :], bcast_vec(t["L3_gnn_bl"][l, :])).then_inc(loaded, 16)
                        sp.wait_ge(loaded, 16 * 9)

                    @block.tensor
                    def _(pe):
                        pe.wait_ge(loaded, 16 * 9)
                        for l in range(3):
                            for a in range(2):
                                last = nc.tensor.transpose(pt[:, l, a * D:(a + 1) * D], raw[:, l, a, :], ident[:, :])
                        last.then_inc(done, 1)

                    @block.vector
                    def _(dve):
                        dve.wait_ge(done, 1)
                        for l in range(3):
                            nc.vector.tensor_copy(w3[l][:, 0:2, :], pt[:, l, 0:2 * D].rearrange("p (a j) -> p a j", j=D))
            return w3

        setup()
        first_norm()
        start_sums()
        with ExitStack() as lay:
            def weight(name, shape):
                return lay.enter_context(sbuf(name, shape))

            wn, wl, w_in, b_in = (weight("wn", [P, D]), weight("wl", [P, D]), weight("w_in", [P, H]), weight("b_in", [P, H]))
            emb = weight("emb", [P, REL_BLOCKS, D])
            with phase(nc, bank, "zeroed") as (block, _sems):
                @block.gpsimd
                def _(pool):
                    nc.gpsimd.memset(emb[:, REL_BLOCKS - 1, :], 0.0)
            whole = (REL_BLOCKS - 1) * P
            load([(wn[:, :], t["L0_gnn_W_neighbor"]), (wl[:, :], t["L0_gnn_loop_weight"]), (w_in[:, :], t["L1_gnn_W_in"]),
                  (b_in[:, :], bcast_vec(t["L1_gnn_b_in"])),
                  (emb[:, 0:REL_BLOCKS - 1, :], t["L0_gnn_rel_emb"][0:whole, :].rearrange("(m p) d -> p m d", p=P)),
                  (emb[0:RELS - whole, REL_BLOCKS - 1, :], t["L0_gnn_rel_emb"][whole:RELS, :])])
            edge_pass(rows128[0], D, Layer0(wn[:, :], wl[:, :], w_in[:, :], b_in[:, :]), rel_emb=emb)

        with ExitStack() as lay:
            def weight(name, shape):
                return lay.enter_context(sbuf(name, shape))

            w = expert_tables(lay)
            w_out, b_out, w1 = weight("w_out", [P, 2, D]), weight("b_out", [P, D]), weight("w1", [P, D])
            load([(w_out[:, :, :], t["L1_gnn_W_out"].rearrange("(k p) d -> p k d", p=P)),
                  (b_out[:, :], bcast_vec(t["L1_gnn_b_out"])), (w1[:, :], t["L2_gnn_W1"])])
            last = {"w_out": w_out, "b_out": b_out[:, :], "w1": w1[:, :]}
            for l in range(3):
                edge_pass(rows256[l % 2], H, Layer1(l % 2, (l + 1) % 2, w, last if l == 2 else None),
                          prologue=load_experts(l, w))

        with ExitStack() as lay:
            w4, b4, c2 = (lay.enter_context(sbuf(n, s)) for n, s in (("w4", [P, D]), ("b4", [P, D]), ("c2", [P, 3])))
            load([(w4[:, :], t["L2_gnn_W4"]), (b4[:, :], bcast_vec(t["L2_gnn_b4"])),
                  (c2[:, 0:1], t["L2_gnn_b1"].rearrange("(p o) -> p o", o=1)), (c2[:, 1:2], t["L2_gnn_W2"]),
                  (c2[:, 2:3], bcast_vec(t["L2_gnn_b2"]))])
            edge_pass(rows256[1], H, Layer2(1, w4[:, :], b4[:, :]), edge_net=(c2[:, 0:1], c2[:, 1:2], c2[:, 2:3]))

        with ExitStack() as lay:
            w3 = layer3_weights(lay)
            for l in range(3):
                edge_pass(rows128[l % 2], D, Layer3(l % 2, (l + 1) % 2 if l < 2 else None, w3[l]))


def bcast_vec(vec):
    return vec.rearrange("(o j) -> o j", o=1).to_broadcast((P, vec.shape[0]))


_INS = ['x', 'src', 'dst', 'edge_type_500', 'L0_gnn_rel_emb', 'L0_gnn_W_neighbor', 'L0_gnn_loop_weight',
        'L1_gnn_W_in', 'L1_gnn_b_in', 'L1_gnn_router_W', 'L1_gnn_router_b', 'L1_gnn_weak_W', 'L1_gnn_weak_b',
        'L1_gnn_strong_W1', 'L1_gnn_strong_b1', 'L1_gnn_strong_W2', 'L1_gnn_strong_b2', 'L1_gnn_conf_W',
        'L1_gnn_conf_b', 'L1_gnn_W_out', 'L1_gnn_b_out', 'L2_gnn_W1', 'L2_gnn_b1', 'L2_gnn_W2', 'L2_gnn_b2',
        'L2_gnn_W4', 'L2_gnn_b4', 'L3_gnn_Wl', 'L3_gnn_bl', 'L3_gnn_Wr']


def kernel(**inputs):
    import numpy as _np
    import concourse.bacc as _bacc
    from concourse import mybir as _mybir
    from concourse.bass_utils import run_bass_kernel_spmd as _run

    nc = _bacc.Bacc("TRN2", target_bir_lowering=False, num_devices=1)
    arrays, handles = {}, {}
    for name in _INS:
        a = _np.ascontiguousarray(inputs[name])
        arrays[f"in_{name}"] = a
        handles[name] = nc.dram_tensor(f"in_{name}", a.shape, _mybir.dt.from_np(a.dtype), kind="ExternalInput").ap()
    out = nc.dram_tensor("out_x", (NPAD, D), _mybir.dt.float32, kind="ExternalOutput").ap()
    gnn_kernel(nc, handles, out)
    r = _run(nc, [arrays], core_ids=[0])
    return r.results[0]["out_x"][:N]
```

```python
import concourse.bass as bass
from concourse import mybir
from contextlib import ExitStack, contextmanager

N = 6250
E = 106250
D = 128
H = 256
RELS = 500
NE = 8
NW = 4
P = 128

GROUP = 4
WIN = 64
RING = 16
HALF = RING // 2
GROUPS = RING // GROUP
TILES = -(-E // P)
STEPS = -(-TILES // RING)
ROW = GROUP * P
SETS = -(-E // (ROW * P))
TCOLS = SETS * P * GROUP
GCOLS = SETS * P
NB = -(-N // P) + 1
SPARE_BLOCK = NB - 1
NPAD = NB * P
SPARE = SPARE_BLOCK * P
LAST = N // P
LASTN = N - LAST * P
REL_BLOCKS = -(-RELS // P)
LN_EPS = 1e-5
L2_EPS = 1e-12
TINY = 1e-35

FP = mybir.dt.float32
F16 = mybir.dt.float16
B16 = mybir.dt.bfloat16
PARTS = 3
YH = 2 * D
FR = mybir.dt.float32r
I32 = mybir.dt.int32
U32 = mybir.dt.uint32
ALU = mybir.AluOpType
ACT = mybir.ActivationFunctionType
AX = mybir.AxisListType


@contextmanager
def phase(nc, bank, *names, pool_dmas=()):
    assert len(names) <= len(bank), len(names)
    with nc.Block() as block:
        yield block, bank[:len(names)]
    if pool_dmas:
        numbers = range(pool_dmas[0].num, pool_dmas[-1].num + 1)
        nc.gpsimd.dma_reset(numbers)
        nc.all_engine_barrier(sems_to_clear=numbers)
    nc.all_engine_barrier(sems_to_clear=range(bank[0].num, bank[-1].num + 1))


class Chain:

    def __init__(self, eng, sem):
        self.eng, self.sem, self.n = eng, sem, 0

    def __call__(self, ins):
        self.n = self.n + 1
        ins.then_inc(self.sem, 1)
        self.eng.wait_ge(self.sem, self.n)


class Results:

    def __init__(self, sem, names):
        self.sem, self.names = sem, names.split()
        assert len(set(self.names)) == len(self.names)

    def at(self, name, i):
        return i * len(self.names) + (len(self.names) + self.names.index(name) + 1)

    def before(self, name, i):
        return i * len(self.names) + (self.names.index(name) + 1)


class Maker:

    def __init__(self, eng, mine, i):
        self.eng, self.mine, self.i, self.next = eng, mine, i, 0

    def done(self, name, ins, wait=False):
        assert self.mine.names[self.next] == name, (self.mine.names[self.next], name)
        self.next += 1
        ins.then_inc(self.mine.sem, 1)
        if wait:
            self.need(self.mine, name)

    def need(self, results, name):
        self.eng.wait_ge(results.sem, results.at(name, self.i))

    def need_before(self, results, name):
        self.eng.wait_ge(results.sem, results.before(name, self.i))

    def apart(self):
        self.eng.nop(nofuse=True)


def gnn_kernel(nc, t, out):
    ctx = ExitStack()
    with ctx:
        def sb(name, shape, dt=FP):
            return ctx.enter_context(nc.sbuf_tensor(name, shape, dt))

        def dram(name, shape, dt=FP):
            return nc.dram_tensor(name, shape, dt, kind="Internal").ap()

        bank = [ctx.enter_context(nc.semaphore(f"signal{k}")) for k in range(32)]
        gathered = [ctx.enter_context(nc.semaphore(f"gathered{k}")) for k in range(RING)]
        for some in (bank, gathered):
            assert [s.num for s in some] == list(range(some[0].num, some[0].num + len(some)))
        uses = [0]

        def sbuf(name, shape, dt=FP):
            uses[0] += 1
            return nc.sbuf_tensor(f"{name}_{uses[0]}", shape, dt)

        def psum(name, shape):
            uses[0] += 1
            return nc.psum_tensor(f"{name}_{uses[0]}", shape, FP)

        rows128 = [dram(f"rows128_{k}", [NPAD, D]) for k in range(2)]
        rows256 = [dram(f"rows256_{k}", [NPAD, H]) for k in range(2)]
        parts128 = [dram(f"parts128_{k}", [NPAD, PARTS * D], B16) for k in range(2)]
        parts256 = [dram(f"parts256_{k}", [NPAD, PARTS * H], B16) for k in range(2)]
        rows_yh = dram("rows_yh", [NPAD, YH])
        parts_yb = dram("parts_yb", [NPAD, PARTS * D], B16)
        x_rows = dram("x_rows", [NPAD, D])
        rdeg_dram = dram("rdeg_dram", [P, NPAD])
        rel_rows = dram("rel_rows", [GCOLS, ROW])
        win_dram = dram("win_dram", [SETS, P], I32)

        acc = sb("acc", [P, 2, NPAD])
        big = sb("big", [P, 2, 10240])
        src_idx = sb("src_idx", [P, TCOLS], I32)
        types = sb("types", [P, TCOLS])
        rel = sb("rel", [P, TCOLS])
        win_base = sb("win_base", [1, GCOLS], I32)
        win = sb("win", [1, GCOLS], I32)
        more = sb("more", [1, 1], I32)
        step_block = sb("step_block", [1, STEPS], I32)
        tail_start = sb("tail_start", [1, 1], I32)
        iota_row0 = sb("iota_row0", [P, P])
        iota_row = sb("iota_row", [P, WIN])
        iota_col0 = sb("iota_col0", [P, 1])
        iota_col = sb("iota_col", [P, 1])
        ident = sb("ident", [P, P])
        ones = sb("ones", [P, P])
        mean_col = sb("mean_col", [P, 1])
        zeros = sb("zeros", [P, P])
        node_rdeg = sb("node_rdeg", [P, NB])
        node_deg = sb("node_deg", [P, NB])
        x_nodes = big[:, 0, 0:NB * D].rearrange("p (b d) -> p b d", d=D)

        def setup():
            with ExitStack() as tmp:
                ip = tmp.enter_context(psum("setup_ps", [P, 8, 512]))
                stage = acc[:, :, :].rearrange("p a n -> p (a n)")
                at = [0]

                def part(n, rows=P):
                    at[0] += n
                    return stage[0:rows, at[0] - n:at[0]]

                irow = [part(TCOLS).bitcast(I32) for _ in range(3)]
                frow = [part(TCOLS) for _ in range(3)]
                least, most, span = part(SETS), part(SETS), part(1)
                spani = part(1, 1).bitcast(I32)
                mayber, morer = part(1, 1), part(1, 1)
                wini = part(P, SETS).bitcast(I32)
                basef = part(GCOLS, 1)
                minr = part(STEPS, 1)
                endr = part(NB, 1)
                stepr = part(STEPS, 1)
                br = part(NB, 1)
                touch = part(NB * STEPS, 1).rearrange("o (b s) -> o b s", s=STEPS)
                lastr, timer = part(NB, 1), part(NB, 1)
                hit = part(STEPS * NB, 1).rearrange("o (s b) -> o s b", b=NB)
                blockr, tailr = part(STEPS, 1), part(1, 1)
                whole = (SETS - 1) * P * ROW
                rest = (E - whole) // ROW
                tail = E - whole - rest * ROW
                cols = (SETS - 1) * ROW
                vecs = (t["src"], t["dst"], t["edge_type_500"])
                with phase(nc, bank, "zeroed", "loaded", "filled", "pool_own", "consts", "own_s", "masked",
                           "transposed", "spilled", "wrote", "moved", "x_loaded", "x_zero") as (block, sems):
                    (zeroed, loaded, filled, pool_own, consts, own_s, masked, transposed, spilled, wrote, moved,
                     x_loaded, x_zero) = sems

                    @block.sync
                    def _(sp):
                        for k, v in enumerate(vecs):
                            sp.dma_start(irow[k][:, 0:cols].rearrange("p (a j) -> p a j", j=ROW),
                                         v[0:whole].rearrange("(a p j) -> p a j", p=P, j=ROW)).then_inc(loaded, 16)
                        sp.dma_start(irow[1][:, cols:TCOLS], vecs[1][E - ROW:E].rearrange("(o j) -> o j", o=1)
                                     .to_broadcast((P, ROW))).then_inc(filled, 16)
                        sp.wait_ge(filled, 16)
                        sp.wait_ge(zeroed, 1)
                        for k, v in enumerate(vecs):
                            sp.dma_start(irow[k][0:rest, cols:TCOLS],
                                         v[whole:whole + rest * ROW].rearrange("(p j) -> p j", j=ROW)).then_inc(loaded, 16)
                            sp.dma_start(irow[k][rest:rest + 1, cols:cols + tail],
                                         v[E - tail:E].rearrange("(p j) -> p j", p=1)).then_inc(loaded, 16)
                        sp.wait_ge(x_zero, 1)
                        sp.dma_start(x_nodes[:, 0:LAST, :],
                                     t["x"][0:LAST * P, :].rearrange("(b p) d -> p b d", p=P)).then_inc(x_loaded, 16)
                        sp.dma_start(x_nodes[0:LASTN, LAST, :], t["x"][LAST * P:N, :]).then_inc(x_loaded, 16)
                        sp.wait_ge(masked, 1)
                        sp.dma_start(rel_rows.rearrange("(a p) j -> p a j", p=P),
                                     frow[1].rearrange("p (a j) -> p a j", j=ROW)).then_inc(wrote, 16)
                        sp.wait_ge(spilled, 1)
                        sp.dma_start(win_dram, wini).then_inc(moved, 16)
                        sp.wait_ge(moved, 16)
                        sp.dma_start(win_base[0:1, :], win_dram.rearrange("a p -> (a p)").rearrange("(o n) -> o n", o=1)
                                     ).then_inc(moved, 16)
                        sp.wait_ge(x_loaded, 32)
                        sp.dma_start(x_rows.rearrange("(b p) d -> p b d", p=P), x_nodes).then_inc(wrote, 16)
                        sp.wait_ge(wrote, 32)

                    @block.gpsimd
                    def _(pool):
                        nc.gpsimd.memset(irow[0][:, cols:TCOLS], 0)
                        nc.gpsimd.memset(irow[2][:, cols:TCOLS], 0).then_inc(zeroed, 1)
                        nc.gpsimd.memset(ident[:, :], 0.0).then_inc(pool_own, 1)
                        nc.gpsimd.memset(zeros[:, :], 0.0)
                        nc.gpsimd.iota(iota_row0[:, :], pattern=[[1, P]], base=0, channel_multiplier=0,
                                       allow_small_or_imprecise_dtypes=True)
                        nc.gpsimd.iota(iota_col0[:, :], pattern=[[1, 1]], base=0, channel_multiplier=1,
                                       allow_small_or_imprecise_dtypes=True)
                        nc.gpsimd.iota(endr, pattern=[[P, NB]], base=P - 1, channel_multiplier=0,
                                       allow_small_or_imprecise_dtypes=True)
                        nc.gpsimd.iota(stepr, pattern=[[1, STEPS]], base=0, channel_multiplier=0,
                                       allow_small_or_imprecise_dtypes=True)
                        nc.gpsimd.iota(br, pattern=[[1, NB]], base=0, channel_multiplier=0,
                                       allow_small_or_imprecise_dtypes=True)
                        nc.gpsimd.memset(ones[:, :], 1.0)
                        nc.gpsimd.memset(mean_col[:, :], 1.0 / P)
                        pool.wait_ge(pool_own, 1)
                        nc.gpsimd.affine_select(out=ident[:, :], in_=ident[:, :], compare_op=ALU.not_equal, fill=1.0,
                                                base=0, pattern=[[-1, P]], channel_multiplier=1).then_inc(consts, 1)
                        pool.wait_ge(own_s, 6)
                        for a in range(SETS):
                            last = nc.gpsimd.affine_select(
                                out=frow[1][:, a * ROW:(a + 1) * ROW], in_=frow[1][:, a * ROW:(a + 1) * ROW],
                                compare_op=ALU.is_ge, fill=-1.0, base=E - 1 - a * P * ROW,
                                pattern=[[-1, ROW]], channel_multiplier=-ROW)
                        last.then_inc(masked, 1)

                    @block.vector
                    def _(dve):
                        own = Chain(dve, own_s)
                        nc.vector.memset(x_nodes[:, LAST:NB, :], 0.0).then_inc(x_zero, 1)
                        dve.wait_ge(loaded, 16 * 9)
                        for k in (0, 2, 1):
                            own(nc.vector.tensor_copy(frow[k], irow[k]))
                        v = frow[1].rearrange("p (a j) -> p a j", j=ROW)
                        own(nc.vector.tensor_reduce(least, v, AX.X, ALU.min))
                        own(nc.vector.tensor_reduce(most, v, AX.X, ALU.max))
                        own(nc.vector.tensor_tensor(v, v, least.unsqueeze(2).to_broadcast([P, SETS, ROW]), ALU.subtract))
                        own(nc.vector.tensor_tensor(most, most, least, ALU.subtract))
                        own(nc.vector.tensor_reduce(span, most, AX.X, ALU.max))
                        dve.wait_ge(transposed, 1)
                        nc.vector.tensor_copy(wini, ip[0:SETS, 6, 0:P]).then_inc(spilled, 1)
                        for k, dst in ((0, src_idx), (1, rel), (2, types)):
                            for a in range(SETS):
                                own(nc.vector.tensor_copy(
                                    dst[:, a * ROW:(a + 1) * ROW].rearrange("p (g q) -> p q g", q=GROUP),
                                    ip[:, SETS * k + a, :].rearrange("p (q g) -> p q g", q=GROUP)))
                        own(nc.vector.tensor_reduce(morer, ip[0:1, 7, 0:P], AX.X, ALU.max))
                        own(nc.vector.tensor_copy(spani, morer))
                        own(nc.vector.tensor_scalar(more[0:1, 0:1], spani, WIN.bit_length() - 1, None,
                                                    ALU.logical_shift_right))
                        own(nc.vector.tensor_copy(mayber, more[0:1, 0:1]))
                        dve.wait_ge(moved, 32)
                        dve.wait_ge(consts, 1)
                        own(nc.vector.tensor_copy(basef, win_base[0:1, :]))
                        own(nc.vector.tensor_reduce(minr, basef[:, 0:STEPS * GROUPS].rearrange("o (s g) -> o s g", g=GROUPS),
                                                    AX.X, ALU.min))
                        own(nc.vector.tensor_tensor(touch, minr.unsqueeze(1).to_broadcast([1, NB, STEPS]),
                                                    endr.unsqueeze(2).to_broadcast([1, NB, STEPS]), ALU.is_le))
                        own(nc.vector.tensor_tensor(touch, touch, stepr.unsqueeze(1).to_broadcast([1, NB, STEPS]), ALU.mult))
                        own(nc.vector.tensor_reduce(lastr, touch, AX.X, ALU.max))
                        own(nc.vector.tensor_tensor(lastr, lastr, br, ALU.subtract))
                        own(nc.vector.tensor_tensor_scan(timer, lastr, lastr, 0.0, ALU.max, ALU.max))
                        own(nc.vector.tensor_tensor(timer, timer, br, ALU.add))
                        own(nc.vector.tensor_scalar(mayber, mayber, float(2 * STEPS), 1.0, ALU.mult, ALU.add))
                        own(nc.vector.tensor_scalar(timer, timer, mayber, None, ALU.add))
                        own(nc.vector.tensor_tensor(hit, timer.unsqueeze(1).to_broadcast([1, STEPS, NB]),
                                                    stepr.unsqueeze(2).to_broadcast([1, STEPS, NB]), ALU.is_equal))
                        own(nc.vector.memset(hit[:, STEPS - 1:STEPS, :], 0.0))
                        own(nc.vector.tensor_reduce(tailr, hit.rearrange("o s b -> o (s b)"), AX.X, ALU.add))
                        own(nc.vector.tensor_copy(tail_start[0:1, :], tailr))
                        own(nc.vector.tensor_scalar(br, br, float(-SPARE_BLOCK), None, ALU.add))
                        own(nc.vector.tensor_tensor(hit, hit, br.unsqueeze(1).to_broadcast([1, STEPS, NB]), ALU.mult))
                        own(nc.vector.tensor_reduce(blockr, hit, AX.X, ALU.add))
                        nc.vector.tensor_scalar(step_block[0:1, :], blockr, float(SPARE_BLOCK), None, ALU.add)

                    @block.tensor
                    def _(pe):
                        pe.wait_ge(consts, 1)
                        pe.wait_ge(masked, 1)
                        pe.wait_ge(own_s, 8)
                        for k in range(3):
                            for a in range(SETS):
                                for q in range(GROUP):
                                    c = a * ROW + q * P
                                    nc.tensor.transpose(ip[:, SETS * k + a, q * P:(q + 1) * P], frow[k][:, c:c + P],
                                                        ident[:, :])
                        nc.tensor.transpose(ip[0:SETS, 6, 0:P], least, ident[:, :])
                        nc.tensor.transpose(ip[0:1, 7, 0:P], span, ident[:, :]).then_inc(transposed, 1)

        def first_norm():
            with ExitStack() as tmp:
                st = tmp.enter_context(sbuf("st", [P, NB, 6]))
                mean, var, rstd, shift = (tmp.enter_context(sbuf(f"c{k}", [P, NB]))[:, :] for k in range(4))
                acc_all = acc[:, :, :].rearrange("p a n -> p (a n)")
                h_nodes = acc_all[:, 0:NB * D].rearrange("p (b d) -> p b d", d=D)
                r_nodes = acc_all[:, NB * D:2 * NB * D].rearrange("p (b d) -> p b d", d=D)
                cut = (big[:, :, :].rearrange("p a n -> p (a n)")[:, NB * D:NB * D + NB * PARTS * D // 2].bitcast(B16)
                       .rearrange("p (b c d) -> p b c d", c=PARTS, d=D))
                parts = 5
                per = NB // parts
                with phase(nc, bank, "own_s", "var_s", "root", "scaled", "h_done", "first", "second", "left", "third",
                           "stored") as (block, sems):
                    own_s, var_s, root, scaled, h_done, first, second, left, third, stored = sems

                    @block.vector
                    def _(dve):
                        own = Chain(dve, own_s)
                        with dve.Fori(0, NB) as b:
                            nc.vector.bn_stats(st[:, bass.ds(b, 1), :], x_nodes[:, bass.ds(b, 1), :]).then_inc(own_s, 1)
                        dve.wait_ge(own_s, NB)
                        own.n = NB
                        m0, v0, m1, v1 = st[:, :, 1], st[:, :, 2], st[:, :, 4], st[:, :, 5]
                        own(nc.vector.tensor_tensor(mean, m0, m1, ALU.subtract))
                        own(nc.vector.tensor_scalar(mean, mean, 0.5, None, ALU.mult))
                        own(nc.vector.tensor_tensor(rstd, mean, mean, ALU.mult))
                        own(nc.vector.tensor_tensor(var, v0, v1, ALU.add))
                        own(nc.vector.tensor_scalar(var, var, 1.0 / D, LN_EPS, ALU.mult, ALU.add))
                        own(nc.vector.tensor_tensor(var, var, rstd, ALU.add))
                        own(nc.vector.tensor_tensor(mean, m0, m1, ALU.add))
                        nc.vector.tensor_scalar(mean, mean, -0.5, None, ALU.mult).then_inc(var_s, 1)
                        dve.wait_ge(root, 1)
                        own(nc.vector.reciprocal(rstd, rstd))
                        nc.vector.tensor_tensor(shift, mean, rstd, ALU.mult).then_inc(scaled, 1)
                        for q in range(parts):
                            some = slice(q * per, (q + 1) * per)
                            dve.wait_ge(first, q + 1)
                            nc.vector.tensor_tensor(r_nodes[:, some, :], h_nodes[:, some, :], cut[:, some, 0, :],
                                                    ALU.subtract).then_inc(left, 1)
                            dve.wait_ge(second, q + 1)
                            nc.vector.tensor_tensor(cut[:, some, 2, :], r_nodes[:, some, :], cut[:, some, 1, :],
                                                    ALU.subtract).then_inc(third, 1)

                    @block.scalar
                    def _(act):
                        act.wait_ge(var_s, 1)
                        nc.scalar.activation(rstd, var, ACT.Sqrt).then_inc(root, 1)
                        act.wait_ge(scaled, 1)
                        for q in range(parts):
                            with act.Fori(q * per, (q + 1) * per) as b:
                                one = bass.ds(b, 1)
                                nc.scalar.activation(h_nodes[:, one, :].rearrange("p b d -> p (b d)"),
                                                     x_nodes[:, one, :].rearrange("p b d -> p (b d)"),
                                                     ACT.Relu, bias=shift[:, one], scale=rstd[:, one]).then_inc(h_done, 1)
                            some = slice(q * per, (q + 1) * per)
                            act.wait_ge(h_done, per * (q + 1))
                            nc.scalar.copy(cut[:, some, 0, :], h_nodes[:, some, :]).then_inc(first, 1)
                            act.wait_ge(left, q + 1)
                            nc.scalar.copy(cut[:, some, 1, :], r_nodes[:, some, :]).then_inc(second, 1)

                    @block.sync
                    def _(sp):
                        for q in range(parts):
                            some = slice(q * per, (q + 1) * per)
                            nodes = slice(q * per * P, (q + 1) * per * P)
                            sp.wait_ge(h_done, per * (q + 1))
                            sp.dma_start(rows128[0][nodes, :].rearrange("(b p) d -> p b d", p=P),
                                         h_nodes[:, some, :]).then_inc(stored, 16)
                            sp.wait_ge(third, q + 1)
                            sp.dma_start(parts128[0][nodes, :].rearrange("(b p) d -> p b d", p=P),
                                         cut[:, some, :, :].rearrange("p b c d -> p b (c d)")).then_inc(stored, 16)
                        sp.wait_ge(stored, 32 * parts)

        def start_sums():
            with phase(nc, bank, "none") as (block, _sems):
                @block.vector
                def _(dve):
                    nc.vector.memset(acc[:, 0, :], 0.0)

                @block.gpsimd
                def _(pool):
                    nc.gpsimd.memset(acc[:, 1, :], 0.0)

        def first_round():
            with phase(nc, bank, "none") as (block, _sems):
                @block.vector
                def _(dve):
                    nc.vector.tensor_copy(win[0:1, :], win_base[0:1, :])
                    nc.vector.tensor_copy(iota_row[:, :], iota_row0[:, 0:WIN])
                    nc.vector.tensor_copy(iota_col[:, :], iota_col0[:, :])

        def next_round():
            with phase(nc, bank, "none") as (block, _sems):
                @block.vector
                def _(dve):
                    nc.vector.tensor_scalar(iota_row[:, :], iota_row[:, :], float(WIN), None, ALU.add)
                    nc.vector.tensor_scalar(iota_col[:, :], iota_col[:, :], float(WIN), None, ALU.add)
                    nc.vector.tensor_scalar(win[0:1, :], win[0:1, :], WIN, SPARE, ALU.add, ALU.min)

        def edge_pass(table, width, work, rel_emb=None, edge_net=None, prologue=None):
            first_round()
            two = width == H or rel_emb is not None
            n_sums = 2 if (two or edge_net) else 1
            rounds = nc.values_load(more[0:1, 0:1], min_val=0, max_val=NPAD // WIN) + 1
            with ExitStack() as tmp:
                ring = tmp.enter_context(sbuf("ring", [P, RING, YH], FP) if edge_net
                                         else sbuf("ring", [P, RING, PARTS * width], B16))
                onehot = tmp.enter_context(sbuf("onehot", [P, 2, HALF, WIN], FP if edge_net else B16))
                idx = tmp.enter_context(sbuf("idx", [P, 2, HALF], I32))
                sums = tmp.enter_context(psum("sums", [P, 2, 512]))
                bufs = work.buffers(tmp)
                names = ["idx_ready", "onehot_ready", "tiles_done", "added", "finished", "block_in", "late_in", "block_out",
                         "pe_result", "act_result", "dve_result", "pe_late", "act_late", "dve_late",
                         "small_loaded", "large_loaded"]
                if rel_emb is not None:
                    iota16 = tmp.enter_context(sbuf("iota16", [P, REL_BLOCKS * P], F16))
                    ones16 = tmp.enter_context(sbuf("ones16", [P, P], B16))
                    type_hot = tmp.enter_context(sbuf("type_hot", [P, HALF, REL_BLOCKS * P], B16))
                    counts = tmp.enter_context(sbuf("counts", [P, 2, REL_BLOCKS, WIN]))
                    counts_ps = tmp.enter_context(psum("counts_ps", [P, 2, 512]))
                    names += ["type_hot_ready", "counted", "counts_ready", "consts_ready"]
                if edge_net:
                    (w2, b2) = edge_net
                    onehot_t = tmp.enter_context(sbuf("onehot_t", [WIN, 2, HALF * P], B16))
                    relb = tmp.enter_context(sbuf("relb", [WIN, 2, HALF * P]))
                    ywin = tmp.enter_context(sbuf("ywin", [WIN, GROUPS, PARTS * D], B16))
                    hidden = tmp.enter_context(sbuf("hidden", [P, GROUP, D]))
                    dot = tmp.enter_context(sbuf("dot", [P, 2, GROUP]))
                    weight = tmp.enter_context(sbuf("weight", [P, 2, GROUP]))
                    onehot_w = tmp.enter_context(sbuf("onehot_w", [P, 2, GROUP, WIN]))
                    zt = tmp.enter_context(psum("zt", [P, 2, GROUP, P]))
                    names += ["rel_loaded0", "rel_loaded1", "z_done", "net_own", "dot_done", "weight_done",
                              "weighted"] + [f"ywin_loaded{g}" for g in range(GROUPS)]

                def programs(block, sems, loop):
                    sem = dict(zip(names, sems))
                    tiles_done, added, finished = sem["tiles_done"], sem["added"], sem["finished"]
                    idx_ready, onehot_ready = sem["idx_ready"], sem["onehot_ready"]
                    work.bind(sem, bufs, loop == "edges")

                    def over(eng, per_tile, per_tile_last=None):
                        def step(i, works, per_tile=per_tile):
                            due = [[w, 0] for w in works]
                            for k in range(RING):
                                per_tile(i, k)
                                for one in due:
                                    while one[1] <= k:
                                        one[1] = next(one[0], RING)
                            for w, _ in due:
                                assert next(w, None) is None, "all of a block's work has its place in the step"

                        def when_due(load):
                            return load if work.LATE and eng is not nc.sync else load()

                        def block_at(i):
                            return eng.value_load(step_block[0:1, bass.ds(i, 1)], min_val=0, max_val=SPARE_BLOCK)

                        if loop == "edges":
                            work.credits(eng)
                            step(0, [work.part(eng, 0, when_due(lambda: SPARE_BLOCK), BANKS_FREE)] if work.LATE else [])

                            def full_step(i, per_tile):
                                b = None if eng is nc.tensor else when_due(lambda: block_at(i))
                                added_before = i * GROUPS + BANKS_FREE
                                if work.LATE:
                                    works = [work.late_part(eng, i - 1, block_at(i - 1) if eng is nc.sync else None), work.part(eng, i, b, added_before)]
                                    step(i, works[::-1] if eng is nc.sync else works, per_tile)
                                else:
                                    step(i, [work.part(eng, i - 1, b, added_before)], per_tile)

                            with eng.Fori(1, STEPS - (1 if per_tile_last else 0)) as i:
                                full_step(i, per_tile)
                            if per_tile_last:
                                full_step(STEPS - 1, per_tile_last)
                            work.leave(eng, STEPS - 1)
                        else:
                            start = eng.value_load(tail_start[0:1, 0:1], min_val=0, max_val=LAST)
                            work.credits(eng)
                            with eng.Fori(0, LAST + 1 - start) as i:
                                b = nc.s_assert_within(start + i, 0, LAST, skip_runtime_bounds_check_because="i ends at LAST")
                                for _ in work.part(eng, i, when_due(lambda: b), None):
                                    pass
                                if work.LATE:
                                    for _ in work.late_part(eng, i, b):
                                        pass

                    BANKS_FREE = 2

                    @block.gpsimd
                    def _(pool):
                        if loop != "edges":
                            return
                        with pool.Fori(0, STEPS) as i:
                            for k in range(RING):
                                h, c = divmod(k, HALF)
                                if c == 0:
                                    pool.wait_ge(idx_ready, i * 2 + (h + 1))
                                pool.wait_ge(tiles_done, i * RING + (k + 1))
                                pool.nop(nofuse=True)
                                nc.gpsimd.indirect_dma_start(
                                    ring[:, k, :], None, table,
                                    bass.IndirectOffsetOnAxis(ap=idx[:, h, c:c + 1].bitcast(U32), axis=0),
                                ).then_inc(gathered[k], 16)

                    @block.scalar
                    def _(act):
                        def load_rel(i, h):
                            act.wait_ge(onehot_ready, (i - 1) * 2 + (h + 1))
                            load_targets(i, h)

                        def load_targets(i, h):
                            act.dma_start(relb[:, h, :].rearrange("p (g j) -> p g j", j=ROW),
                                          rel_rows[bass.ds(i * GROUPS + h * 2, 2), :].unsqueeze(0).to_broadcast((WIN, 2, ROW))
                                          ).then_inc(sem[f"rel_loaded{h}"], 16)

                        def load_window(i, g):
                            w = act.value_load(win[0:1, bass.ds(i * GROUPS + g, 1)], min_val=0, max_val=SPARE)
                            act.wait_ge(tiles_done, i * RING + GROUP * (g + 1))
                            act.dma_start(ywin[:, g, :], parts_yb[bass.ds(w, WIN), :]).then_inc(sem[f"ywin_loaded{g}"], 16)

                        def stage(i, h, col):
                            nc.scalar.copy(idx[:, h, :], src_idx[:, bass.ds(col, HALF)]).then_inc(idx_ready, 1)

                        stage_at = HALF - 1 if n_sums == 1 else GROUP

                        def tile(i, k):
                            g, q = divmod(k, GROUP)
                            if k % HALF == stage_at:
                                for j in range(k // HALF * HALF, (k // HALF + 1) * HALF):
                                    act.wait_ge(gathered[j], i * 16 + 16)
                                act.nop(nofuse=True)
                                stage(i, k // HALF, (i + 1) * RING + k // HALF * HALF)
                            if rel_emb is not None and q == 0:
                                act.wait_ge(sem["counted"], i * GROUPS + (g + 1))
                                nc.scalar.copy(counts[:, g % 2, :, :].bitcast(FR),
                                               counts_ps[:, g % 2, 0:REL_BLOCKS * WIN].rearrange("p (m j) -> p m j", j=WIN)
                                               ).then_inc(sem["counts_ready"], 1)
                            if edge_net and q == 0:
                                if g % 2 == 0:
                                    load_rel(i + 1, g // 2)
                                load_window(i + (g + 2) // GROUPS, (g + 2) % GROUPS)
                                act.wait_ge(sem["dot_done"], i * GROUPS + (g + 1))
                                nc.scalar.activation(weight[:, g % 2, :], dot[:, g % 2, :], ACT.Sigmoid,
                                                     bias=b2).then_inc(sem["weight_done"], 1)

                        if loop == "edges":
                            for h in range(2):
                                stage(0, h, h * HALF)
                            if edge_net:
                                for k in range(2):
                                    load_targets(0, k)
                                    load_window(0, k)
                        over(act, tile)
                        if edge_net and loop == "edges":
                            for k in range(2):
                                act.wait_ge(sem[f"rel_loaded{k}"], STEPS * 16 + 16)
                                act.wait_ge(sem[f"ywin_loaded{k}"], STEPS * 16 + 16)

                    @block.sync
                    def _(sp):
                        if prologue and loop == "edges":
                            prologue(sp, sem["small_loaded"], sem["large_loaded"])

                        over(sp, lambda i, k: None)

                    @block.vector
                    def _(dve):
                        def one_hots(i, h):
                            dve.wait_ge(tiles_done, i * RING + HALF * (h + 1))
                            cols = rel[:, bass.ds(i * RING + h * HALF, HALF)].unsqueeze(2).to_broadcast([P, HALF, WIN])
                            places = iota_row[:, :].unsqueeze(1).to_broadcast([P, HALF, WIN])
                            if edge_net:
                                dve.wait_ge(sem[f"rel_loaded{h}"], i * 16 + 16)
                                nc.vector.tensor_scalar(onehot_t[:, h, :], relb[:, h, :], iota_col[0:WIN, 0:1], None,
                                                        ALU.is_equal)
                            nc.vector.tensor_tensor(onehot[:, h, :, :], places, cols, ALU.is_equal).then_inc(onehot_ready, 1)

                        def type_hots(i, g):
                            if rel_emb is not None:
                                dve.wait_ge(tiles_done, i * RING + GROUP * (g + 3))
                                for q in range(GROUP):
                                    k = g * GROUP + q
                                    last = nc.vector.tensor_scalar(type_hot[:, k % HALF, :], iota16[:, :],
                                                                   types[:, bass.ds(i * RING + k, 1)], None, ALU.is_equal)
                                last.then_inc(sem["type_hot_ready"], 1)

                        def dots(i, g):
                            n = i * (2 * GROUPS) + 2 * g
                            k = g * GROUP
                            dve.wait_ge(sem["z_done"], i * GROUPS + (g + 1))
                            nc.vector.tensor_tensor(hidden[:, :, :], zt[:, g % 2, :, :], ring[:, k:k + GROUP, 0:D],
                                                    ALU.subtract).then_inc(sem["net_own"], 1)
                            dve.wait_ge(sem["net_own"], n + 1)
                            nc.vector.scalar_tensor_tensor(
                                out=hidden[:, :, :], in0=hidden[:, :, :], scalar=0.0,
                                in1=w2.unsqueeze(1).to_broadcast([P, GROUP, D]), op0=ALU.max,
                                op1=ALU.mult).then_inc(sem["net_own"], 1)
                            dve.wait_ge(sem["net_own"], n + 2)
                            nc.vector.tensor_reduce(dot[:, g % 2, :], hidden[:, :, :], AX.X,
                                                    ALU.add).then_inc(sem["dot_done"], 1)

                        def tile(i, k, ahead=True):
                            g, q = divmod(k, GROUP)
                            if edge_net and q == 0:
                                dve.wait_ge(sem["weight_done"], i * GROUPS + (g + 1))
                                dve.wait_ge(tiles_done, i * RING + GROUP * (g + 3))
                                j = g * GROUP % HALF
                                nc.vector.tensor_tensor(onehot_w[:, g % 2, :, :], onehot[:, g // 2, j:j + GROUP, :],
                                                        weight[:, g % 2, :].unsqueeze(2).to_broadcast([P, GROUP, WIN]),
                                                        ALU.mult).then_inc(sem["weighted"], 1)
                            if q == 0 and g % 2 == 0:
                                one_hots(i + g // 2, 1 - g // 2)
                            if q == 0:
                                type_hots(i + (g + 1) // GROUPS, (g + 1) % GROUPS)
                            if q < GROUP - 1:
                                return
                            if edge_net and (ahead or g < GROUPS - 1):
                                dots(i + (g + 1) // GROUPS, (g + 1) % GROUPS)
                            w = dve.value_load(win[0:1, bass.ds(i * GROUPS + g, 1)], min_val=0, max_val=SPARE)
                            dve.wait_ge(tiles_done, i * RING + (GROUP * (g + 1) + RING))
                            dve.wait_ge(added, i * GROUPS + (g + 2))
                            if edge_net:
                                nc.vector.tensor_tensor(acc[0:1, 1, bass.ds(w, WIN)], acc[0:1, 1, bass.ds(w, WIN)],
                                                        sums[0:1, g % 2, WIN:2 * WIN], ALU.add)
                            n = 1 if edge_net else n_sums
                            nc.vector.tensor_tensor(
                                acc[:, 0:n, bass.ds(w, WIN)], acc[:, 0:n, bass.ds(w, WIN)],
                                sums[:, g % 2, 0:n * WIN].rearrange("p (a j) -> p a j", j=WIN),
                                ALU.add).then_inc(added, 1)

                        if loop == "edges":
                            dve.sem_inc(added, 2)
                            if rel_emb is not None:
                                nc.vector.memset(ones16[:, :], 1.0)
                                for m in range(REL_BLOCKS):
                                    last = nc.vector.tensor_scalar(iota16[:, m * P:(m + 1) * P], iota_row0[:, :],
                                                                   float(m * P), None, ALU.add)
                                last.then_inc(sem["consts_ready"], 1)
                                dve.wait_ge(sem["consts_ready"], 1)
                            one_hots(0, 0)
                            if rel_emb is not None:
                                dve.wait_ge(tiles_done, RING)
                                for q in range(GROUP):
                                    last = nc.vector.tensor_scalar(type_hot[:, q, :], iota16[:, :], types[:, q:q + 1],
                                                                   None, ALU.is_equal)
                                last.then_inc(sem["type_hot_ready"], 1)
                        if edge_net:
                            if loop == "edges":
                                dots(0, 0)
                            over(dve, tile, lambda i, k: tile(i, k, ahead=False))
                        else:
                            over(dve, tile)

                    @block.tensor
                    def _(pe):
                        def tile_sum(ap, lhs, rhs, first, last=False):
                            return nc.tensor.matmul(ap, lhs, rhs, start=first, stop=last, skip_group_check=True)

                        def hidden_net(i, k):
                            g, q = divmod(k, GROUP)
                            if k % HALF == 0:
                                pe.wait_ge(onehot_ready, i * 2 + (k // HALF + 1))
                            pe.wait_ge(gathered[k], i * 16 + 16)
                            if q == 0:
                                pe.wait_ge(sem[f"ywin_loaded{g}"], i * 16 + 16)
                            for c in range(PARTS):
                                last = nc.tensor.matmul(zt[:, g % 2, q, :], onehot_t[:, g // 2, (k % HALF) * P:(k % HALF + 1) * P],
                                                        ywin[:, g, c * D:(c + 1) * D], start=(c == 0), stop=(c == PARTS - 1))
                            if q == GROUP - 1:
                                last.then_inc(sem["z_done"], 1)

                        def net_tile(i, k, ahead=True):
                            g, q = divmod(k, GROUP)
                            if k + GROUP < RING:
                                hidden_net(i, k + GROUP)
                            elif ahead:
                                hidden_net(i + 1, k + GROUP - RING)
                            if q < GROUP - 1:
                                return
                            pe.wait_ge(added, i * GROUPS + (g + 1))
                            pe.wait_ge(sem["weighted"], i * GROUPS + (g + 1))
                            for j in range(GROUP):
                                hot = onehot_w[:, g % 2, j, :]
                                tile_sum(sums[:, g % 2, 0:WIN], ring[:, g * GROUP + j, D:YH], hot, j == 0)
                                last = tile_sum(sums[0:1, g % 2, WIN:2 * WIN], ones[:, 0:1], hot, False, j == GROUP - 1)
                            last.then_inc(tiles_done, GROUP)

                        def count_types(i, g):
                            pe.wait_ge(sem["type_hot_ready"], i * GROUPS + (g + 1))
                            for q in range(GROUP):
                                j = (g * GROUP + q) % HALF
                                for m in range(REL_BLOCKS):
                                    last = tile_sum(counts_ps[:, g % 2, m * WIN:(m + 1) * WIN],
                                                    type_hot[:, j, m * P:(m + 1) * P], onehot[:, g // 2, j, :],
                                                    q == 0 and m == 0, q == GROUP - 1 and m == REL_BLOCKS - 1)
                            last.then_inc(sem["counted"], 1)

                        def tile(i, k):
                            g, q = divmod(k, GROUP)
                            if k % HALF == 0:
                                pe.wait_ge(onehot_ready, i * 2 + (k // HALF + 1))
                            if q == 0:
                                pe.wait_ge(added, i * GROUPS + (g + 1))
                                if rel_emb is not None:
                                    count_types(i, g)
                            pe.wait_ge(gathered[k], i * 16 + 16)
                            hot = onehot[:, g // 2, k % HALF, :]
                            if rel_emb is None:
                                for a in range(width // D):
                                    for c in range(PARTS):
                                        lo = c * width + a * D
                                        last = tile_sum(sums[:, g % 2, a * WIN:(a + 1) * WIN], ring[:, k, lo:lo + D],
                                                        hot, q == 0 and a == 0 and c == 0, q == GROUP - 1)
                            else:
                                for c in range(PARTS):
                                    tile_sum(sums[:, g % 2, 0:WIN], ring[:, k, c * D:(c + 1) * D], hot, q == 0 and c == 0)
                                last = tile_sum(sums[:, g % 2, WIN:2 * WIN], ones16[:, :], hot, False)
                                if q == GROUP - 1:
                                    pe.wait_ge(sem["counts_ready"], i * GROUPS + (g + 1))
                                    for part in range(2):
                                        for m in range(REL_BLOCKS):
                                            last = tile_sum(sums[:, g % 2, 0:WIN], rel_emb[:, part, m, :].bitcast(FR),
                                                            counts[:, g % 2, m, :].bitcast(FR), False,
                                                            part == 1 and m == REL_BLOCKS - 1)
                            if q == GROUP - 1:
                                last.then_inc(tiles_done, GROUP)

                        if loop == "edges":
                            pe.sem_inc(tiles_done, RING)
                            if edge_net:
                                for k in range(GROUP):
                                    hidden_net(0, k)
                        if edge_net:
                            over(pe, net_tile, lambda i, k: net_tile(i, k, ahead=False))
                        else:
                            over(pe, tile)

                with nc.Fori(0, rounds):
                    with phase(nc, bank, *names, pool_dmas=gathered) as (block, sems):
                        programs(block, sems, "edges")
                    next_round()
                with phase(nc, bank, *names) as (block, sems):
                    programs(block, sems, "blocks")

        class Work:
            LATE = False

            def bind(self, sem, bufs, in_pass):
                self.sem, self.b, self.in_pass = sem, bufs, in_pass
                self.pe = Results(sem["pe_result"], self.PE)
                self.act = Results(sem["act_result"], self.ACT)
                self.dve = Results(sem["dve_result"], self.DVE)
                self.pe2 = self.act2 = self.dve2 = None
                if self.LATE:
                    self.pe2 = Results(sem["pe_late"], self.PE_LATE)
                    self.act2 = Results(sem["act_late"], self.ACT_LATE)
                    self.dve2 = Results(sem["dve_late"], self.DVE_LATE)

            def results(self, eng):
                for e, both in ((nc.tensor, (self.pe, self.pe2)), (nc.scalar, (self.act, self.act2)),
                                (nc.vector, (self.dve, self.dve2))):
                    if e is eng:
                        return both
                return (None, None)

            def credits(self, eng):
                for r in self.results(eng):
                    if r is not None:
                        eng.sem_inc(r.sem, len(r.names))
                if eng is nc.sync:
                    eng.sem_inc(self.sem["finished"], 1)
                    eng.sem_inc(self.sem["block_out"], 16)

            def part(self, eng, i, b, added):
                for e, f in ((nc.tensor, self.on_pe), (nc.scalar, self.on_act), (nc.vector, self.on_dve), (nc.sync, self.on_sp)):
                    if e is eng:
                        if not self.LATE:
                            eng.wait_ge(self.sem["finished"], i + 1)
                        yield from f(eng, Maker(eng, self.results(eng)[0], i), i, b, added)

            def late_part(self, eng, i, b):
                for e, f in ((nc.tensor, self.late_pe), (nc.scalar, self.late_act), (nc.vector, self.late_dve),
                             (nc.sync, self.late_sp)):
                    if e is eng:
                        yield from f(eng, Maker(eng, self.results(eng)[1], i), i, b)

            def leave(self, eng, blocks):
                pass

            def loads(self, m, pairs):
                m.apart()
                for dst, src in pairs:
                    m.eng.dma_start(dst, src).then_inc(self.sem["block_in"], 16)

            def loaded(self, m, n):
                m.eng.wait_ge(self.sem["block_in"], m.i * (16 * n) + 16 * n)

            def sums_ready(self, m, added):
                if added is not None:
                    m.eng.wait_ge(self.sem["added"], added)
                m.apart()

            def stored(self, m, stores):
                m.apart()
                for dst, src in stores:
                    m.eng.dma_start(dst, src).then_inc(self.sem["block_out"], 16)

            def finish(self, m, n):
                m.eng.wait_ge(self.sem["block_out"], m.i * (16 * n) + (16 * n + 16))
                m.apart()
                m.eng.sem_inc(self.sem["finished"], 1)

            CUT = " cut0 left cut1 cut2"

            def cut_dve(self, m, x, left, cut):
                m.done("cut0", nc.vector.tensor_copy(cut[0], x), wait=True)
                m.done("left", nc.vector.tensor_tensor(left, x, cut[0], ALU.subtract), wait=True)
                m.done("cut1", nc.vector.tensor_copy(cut[1], left), wait=True)
                m.done("cut2", nc.vector.tensor_tensor(cut[2], left, cut[1], ALU.subtract))

            NORM_DVE = "stats meanvar var_eps rstd shift"
            NORM_ACT = "norm_root h_row"

            def norm_dve(self, m, x, s, at):
                m.done("stats", nc.vector.bn_stats(s[:, 0:6], x), wait=True)
                m.eng.nop(nofuse=True)
                m.done("meanvar", nc.vector.bn_aggr(s[:, 6:8], s[:, 0:6]), wait=True)
                m.done("var_eps", nc.vector.tensor_scalar(s[:, 8:9], s[:, 7:8], LN_EPS, None, ALU.add))
                yield at
                m.need(self.act, "norm_root")
                m.done("rstd", nc.vector.reciprocal(s[:, 10:11], s[:, 9:10]), wait=True)
                m.done("shift", nc.vector.scalar_tensor_tensor(out=s[:, 11:12], in0=s[:, 6:7], scalar=-1.0,
                                                               in1=s[:, 10:11], op0=ALU.mult, op1=ALU.mult))

            def norm_act(self, m, x, s, h, at):
                m.need(self.dve, "var_eps")
                m.done("norm_root", nc.scalar.activation(s[:, 9:10], s[:, 8:9], ACT.Sqrt))
                yield at
                m.need(self.dve, "shift")
                m.done("h_row", nc.scalar.activation(h, x, ACT.Relu, bias=s[:, 11:12], scale=s[:, 10:11]))

        def rows_of(table, b, lo=0, hi=None):
            return table[bass.ds(b * P, P), lo:(hi or table.shape[1])]

        class Layer0(Work):
            PE = "agg_w deg_col h_t h_wl h2_t h_win"
            ACT = "sums_in cleared deg_root norm_root h_row h2_t_sb"
            DVE = ("deg_sb deg1 rdeg rdeg_row1 rdeg_row norm scaled_agg h_t_sb joined new_x "
                   + Work.NORM_DVE + " next_row" + Work.CUT)

            def __init__(self, wn, wl, w_in, b_in):
                self.wn, self.wl, self.w_in, self.b_in = wn, wl, w_in, b_in

            def buffers(self, tmp):
                s = {n: tmp.enter_context(sbuf(n, [P, w])) for n, w in
                     (("h", D), ("x", D), ("agg", P), ("deg", P), ("ht", P), ("rdeg", P), ("u", D), ("col", 4),
                      ("st", 12), ("h2", D), ("h2t", P), ("row", H), ("left", H))}
                s["cut"] = tmp.enter_context(sbuf("cut", [P, PARTS, H], B16))
                p = {n: tmp.enter_context(psum(n, [P, 512])) for n in ("pa", "pb", "pc")}
                return s, p

            def on_sp(self, sp, m, i, b, added):
                s, _ = self.b
                self.loads(m, [(s["h"][:, :], rows_of(rows128[0], b)), (s["x"][:, :], rows_of(x_rows, b))])
                m.need(self.dve, "rdeg_row")
                self.stored(m, [(rdeg_dram[:, bass.ds(b * P, P)], s["rdeg"][:, :])])
                m.need(self.dve, "new_x")
                self.stored(m, [(rows_of(x_rows, b), s["x"][:, :])])
                m.need(self.dve, "next_row")
                self.stored(m, [(rows_of(rows256[0], b), s["row"][:, :])])
                m.need(self.dve, "cut2")
                self.stored(m, [(rows_of(parts256[0], b), s["cut"][:, :, :].rearrange("p c d -> p (c d)"))])
                self.finish(m, 4)
                yield RING

            def on_act(self, act, m, i, b, added):
                s, p = self.b
                blk = bass.ds(b * P, P)
                self.sums_ready(m, added)
                nc.scalar.copy(s["agg"][:, :], acc[:, 0, blk])
                m.done("sums_in", nc.scalar.copy(s["deg"][:, :], acc[:, 1, blk]), wait=True)
                m.apart()
                nc.scalar.copy(acc[:, 0, blk], zeros[:, :])
                m.done("cleared", nc.scalar.copy(acc[:, 1, blk], zeros[:, :]))
                yield 3
                m.need(self.dve, "deg1")
                m.done("deg_root", nc.scalar.activation(s["col"][:, 2:3], s["col"][:, 1:2], ACT.Sqrt))
                yield 7
                yield from self.norm_act(m, s["x"][:, :], s["st"], s["h2"][:, :], 8)
                yield 9
                m.need(self.pe, "h2_t")
                m.done("h2_t_sb", nc.scalar.copy(s["h2t"][:, :], p["pa"][:, 0:P]))

            def on_dve(self, dve, m, i, b, added):
                s, p = self.b
                col = s["col"]
                yield 2
                m.need(self.pe, "deg_col")
                m.done("deg_sb", nc.vector.tensor_copy(node_deg[:, bass.ds(b, 1)], p["pb"][:, P:P + 1]))
                m.done("deg1", nc.vector.tensor_scalar(col[:, 1:2], p["pb"][:, P:P + 1], 1.0, None, ALU.max), wait=True)
                m.done("rdeg", nc.vector.reciprocal(node_rdeg[:, bass.ds(b, 1)], col[:, 1:2]))
                m.done("rdeg_row1", nc.vector.tensor_scalar(s["rdeg"][:, :], s["deg"][:, :], 1.0, None, ALU.max), wait=True)
                m.done("rdeg_row", nc.vector.reciprocal(s["rdeg"][:, :], s["rdeg"][:, :]))
                yield 4
                m.need(self.act, "deg_root")
                m.done("norm", nc.vector.reciprocal(col[:, 3:4], col[:, 2:3]), wait=True)
                m.need(self.pe, "agg_w")
                m.done("scaled_agg", nc.vector.tensor_scalar(s["u"][:, :], p["pb"][:, 0:D], col[:, 3:4], None, ALU.mult))
                m.need(self.pe, "h_t")
                m.done("h_t_sb", nc.vector.tensor_copy(s["ht"][:, :], p["pa"][:, 0:P]))
                yield 6
                m.need(self.dve, "scaled_agg")
                m.need(self.pe, "h_wl")
                m.done("joined", nc.vector.tensor_tensor(s["u"][:, :], s["u"][:, :], p["pc"][:, 0:D], ALU.add), wait=True)
                self.loaded(m, 2)
                m.done("new_x", nc.vector.scalar_tensor_tensor(out=s["x"][:, :], in0=s["u"][:, :], scalar=0.0,
                                                               in1=s["x"][:, :], op0=ALU.max, op1=ALU.add), wait=True)
                yield from self.norm_dve(m, s["x"][:, :], s["st"], 8)
                yield 11
                m.need(self.pe, "h_win")
                m.done("next_row", nc.vector.tensor_tensor(s["row"][:, :], p["pc"][:, 0:H], self.b_in, ALU.add), wait=True)
                self.cut_dve(m, s["row"][:, :], s["left"][:, :], [s["cut"][:, c, :] for c in range(PARTS)])

            def on_pe(self, pe, m, i, b, added):
                s, p = self.b
                yield 1
                m.need(self.act, "sums_in")
                m.done("agg_w", nc.tensor.matmul(p["pb"][:, 0:D], s["agg"][:, :], self.wn, start=True, stop=True))
                m.done("deg_col", nc.tensor.matmul(p["pb"][:, P:P + 1], s["deg"][:, :], mean_col[:, :], start=True,
                                                   stop=True))
                yield 3
                self.loaded(m, 2)
                m.done("h_t", nc.tensor.transpose(p["pa"][:, 0:P], s["h"][:, :], ident[:, :]))
                yield 5
                m.need(self.dve, "h_t_sb")
                m.done("h_wl", nc.tensor.matmul(p["pc"][:, 0:D], s["ht"][:, :], self.wl, start=True, stop=True))
                yield 9
                m.need(self.act, "h_row")
                m.done("h2_t", nc.tensor.transpose(p["pa"][:, 0:P], s["h2"][:, :], ident[:, :]))
                yield 10
                m.need(self.act, "h2_t_sb")
                m.done("h_win", nc.tensor.matmul(p["pc"][:, 0:H], s["h2t"][:, :], self.w_in, start=True, stop=True))

        class Layer1(Work):
            LATE = True
            PE = "h_t logits"
            ACT = "cleared exps"
            DVE = "h_t_sb agg logits_sb top topi topf diff neg_conf plus1 recips gate0 gate1 pick0 pick1 gates gates_hi gates_lo"
            PE_LATE = "weak0 weak1 gate_t gate_rows up0 up1 down0 up2 down1 up3 down2 down3 moe_t"
            ACT_LATE = "agg_kept h_kept weak_relu0 weak_relu1 gates_kept relu0 relu1 relu2 relu3"
            DVE_LATE = "weak_scaled weak_sum scaled0 scaled1 scaled2 scaled3 moe next_row" + Work.CUT
            PE_LAST = " h2_t h2_w"
            ACT_LAST = " norm_root h_row h2_t_sb"
            DVE_LAST = " new_h_t x_part new_x " + Work.NORM_DVE + " next_y y_b1" + Work.CUT + " next_h"

            def __init__(self, cur, nxt, w, last=None):
                self.cur, self.nxt, self.w, self.last = cur, nxt, w, last
                if last:
                    self.PE_LATE = self.PE_LATE.replace(" moe_t", " h_out") + self.PE_LAST
                    self.ACT_LATE = self.ACT_LATE.replace(" h_kept", " h_t_kept") + self.ACT_LAST
                    self.DVE_LATE = self.DVE_LATE.replace(" next_row" + Work.CUT, "") + self.DVE_LAST

            def buffers(self, tmp):
                s = {n: tmp.enter_context(sbuf(n, sh)) for n, sh in
                     (("h", [P, H]), ("ht", [P, 2, P]), ("agg", [P, 2, P]), ("rdeg", [P, P]), ("lg", [P, NE + 1]),
                      ("top", [P, 8]), ("topf", [P, 2]), ("col", [P, 8]), ("ecol", [P, 2]), ("g1", [P, NE]),
                      ("g2", [P, NE]), ("gate", [P, NE]), ("gates", [P, 2 * NE]),
                      ("gt", [2 * NE, P]), ("agg2", [P, 2, P]), ("h2", [P, H]),
                      ("weak", [P, NE, P]), ("strong", [P, 2, 4, P]), ("moe", [P, 2, P]), ("row", [P, H]))}
                s["topi"] = tmp.enter_context(sbuf("topi", [P, 8], U32))
                s["left"] = tmp.enter_context(sbuf("left", [P, H]))
                s["cut"] = tmp.enter_context(sbuf("cut", [P, PARTS * (D if self.last else H)], B16))
                if self.last:
                    s |= {n: tmp.enter_context(sbuf(n, sh)) for n, sh in
                          (("ht2", [P, 2, P]), ("x", [P, D]), ("st", [P, 12]), ("hn", [P, D]), ("hnt", [P, P]), ("u", [P, D]))}
                p = {"hid": tmp.enter_context(psum("hid", [P, 2, 4, P])), "gb": tmp.enter_context(psum("gb", [P, NE, P])),
                     "y": tmp.enter_context(psum("y", [P, 512])), "misc": tmp.enter_context(psum("misc", [P, 512]))}
                return s, p

            def on_sp(self, sp, m, i, b, added):
                s, _ = self.b
                m.need_before(self.act2, "gates_kept")
                self.loads(m, [(s["h"][:, :], rows_of(rows256[self.cur], b)), (s["rdeg"][:, :], rdeg_dram[:, bass.ds(b * P, P)])])
                yield RING

            def on_act(self, act, m, i, b, added):
                s, p = self.b
                yield 9
                b = b()
                m.need(self.dve, "agg")
                m.apart()
                for a in range(2):
                    ins = nc.scalar.copy(acc[:, a, bass.ds(b * P, P)], zeros[:, :])
                m.done("cleared", ins)
                yield 13
                m.need(self.dve, "neg_conf")
                m.done("exps", nc.scalar.activation(s["ecol"][:, :], s["col"][:, 0:2], ACT.Exp))

            def on_dve(self, dve, m, i, b, added):
                s, p = self.b
                col = s["col"]
                yield 9
                b = b()
                m.need(self.pe, "h_t")
                m.need_before(self.act2, "gates_kept")
                m.done("h_t_sb", nc.vector.tensor_copy(s["ht"][:, :, :], p["misc"][:, 0:H].rearrange("p (a j) -> p a j", j=P)))
                self.sums_ready(m, added)
                self.loaded(m, 2)
                m.done("agg", nc.vector.tensor_tensor(s["agg"][:, :, :], acc[:, :, bass.ds(b * P, P)],
                                                      s["rdeg"][:, :].unsqueeze(1).to_broadcast([P, 2, P]), ALU.mult))
                yield 13
                if self.in_pass:
                    dve.wait_ge(self.sem["small_loaded"], self.w["small"])
                m.need(self.pe, "logits")
                lg = s["lg"][:, 0:NE]
                m.done("logits_sb", nc.vector.tensor_tensor(s["lg"][:, :], p["misc"][:, 0:NE + 1],
                                                            self.w["router_b"][:, :], ALU.add), wait=True)
                dve.nop(nofuse=True)
                m.done("top", nc.vector.max(s["top"][:, :], lg), wait=True)
                dve.nop(nofuse=True)
                m.done("topi", nc.vector.max_index(s["topi"][:, :], s["top"][:, :], lg), wait=True)
                m.done("topf", nc.vector.tensor_copy(s["topf"][:, :], s["topi"][:, 0:2]))
                m.done("diff", nc.vector.tensor_tensor(col[:, 0:1], s["top"][:, 1:2], s["top"][:, 0:1], ALU.subtract))
                m.done("neg_conf", nc.vector.tensor_scalar(col[:, 1:2], s["lg"][:, NE:NE + 1], -1.0, None, ALU.mult))
                yield 14
                m.need(self.act, "exps")
                m.done("plus1", nc.vector.tensor_scalar(col[:, 2:4], s["ecol"][:, :], 1.0, None, ALU.add), wait=True)
                m.done("recips", nc.vector.reciprocal(col[:, 4:6], col[:, 2:4]), wait=True)
                m.done("gate0", nc.vector.tensor_tensor(col[:, 6:7], col[:, 4:5], col[:, 5:6], ALU.mult), wait=True)
                m.done("gate1", nc.vector.tensor_tensor(col[:, 7:8], col[:, 6:7], s["ecol"][:, 0:1], ALU.mult), wait=True)
                m.done("pick0", nc.vector.tensor_scalar(s["g1"][:, :], iota_row0[:, 0:NE], s["topf"][:, 0:1], col[:, 6:7],
                                                        ALU.is_equal, ALU.mult))
                m.done("pick1", nc.vector.tensor_scalar(s["g2"][:, :], iota_row0[:, 0:NE], s["topf"][:, 1:2], col[:, 7:8],
                                                        ALU.is_equal, ALU.mult), wait=True)
                m.done("gates", nc.vector.tensor_tensor(s["gate"][:, :], s["g1"][:, :], s["g2"][:, :], ALU.add), wait=True)
                m.done("gates_hi", nc.vector.tensor_copy(s["gates"][:, 0:NE].bitcast(FR), s["gate"][:, :]), wait=True)
                m.done("gates_lo", nc.vector.tensor_tensor(s["gates"][:, NE:2 * NE].bitcast(FR), s["gate"][:, :],
                                                           s["gates"][:, 0:NE], ALU.subtract))

            def on_pe(self, pe, m, i, b, added):
                s, p = self.b
                w = self.w
                yield 8
                if self.in_pass:
                    pe.wait_ge(self.sem["small_loaded"], w["small"])
                self.loaded(m, 2)
                m.need_before(self.act2, "gates_kept")
                for a in range(2):
                    ins = nc.tensor.transpose(p["misc"][:, a * P:(a + 1) * P], s["h"][:, a * P:(a + 1) * P], ident[:, :])
                m.done("h_t", ins)
                yield 12
                m.need(self.dve, "agg")
                cols = [s["ht"][:, k, :] for k in range(2)] + [s["agg"][:, k, :] for k in range(2)]
                for k in range(4):
                    ins = nc.tensor.matmul(p["misc"][:, 0:NE + 1], cols[k], w["router"][:, k, :], start=(k == 0),
                                           stop=(k == 3))
                m.done("logits", ins)

            def late_sp(self, sp, m, i, b):
                s, _ = self.b
                n = 3 if self.last else 2
                if self.last:
                    sp.wait_ge(self.sem["block_out"], i * (16 * n) + 16)
                    sp.nop(nofuse=True)
                    sp.dma_start(s["x"][:, :], rows_of(x_rows, b)).then_inc(self.sem["late_in"], 16)
                    m.need(self.dve2, "new_x")
                    self.stored(m, [(rows_of(x_rows, b), s["x"][:, :])])
                if not self.last:
                    m.need(self.dve2, "next_row")
                    self.stored(m, [(rows_of(rows256[self.nxt], b), s["row"][:, :])])
                m.need(self.dve2, "next_h" if self.last else "cut2")
                self.stored(m, [(rows_of(parts_yb if self.last else parts256[self.nxt], b), s["cut"][:, :])]
                            + ([(rows_of(rows_yh, b), s["row"][:, :])] if self.last else []))
                if not self.in_pass:
                    sp.wait_ge(self.sem["block_out"], i * (16 * n) + (16 * n + 16))
                    sp.nop(nofuse=True)
                yield RING

            def leave(self, eng, blocks):
                if eng is nc.sync:
                    eng.wait_ge(self.sem["block_out"], blocks * (48 if self.last else 32) + 16)
                    eng.nop(nofuse=True)

            def late_act(self, act, m, i, b):
                s, p = self.b
                m.need(self.dve, "agg")
                m.need_before(self.pe2, "up3")
                m.done("agg_kept", nc.scalar.copy(s["agg2"][:, :, :], s["agg"][:, :, :]))
                yield 1
                if self.last:
                    m.need_before(self.dve2, "new_h_t")
                    m.done("h_t_kept", nc.scalar.copy(s["ht2"][:, :, :], s["ht"][:, :, :]))
                else:
                    m.need_before(self.dve2, "next_row")
                    self.loaded(m, 2)
                    m.done("h_kept", nc.scalar.copy(s["h2"][:, :], s["h"][:, :]))
                if self.in_pass:
                    act.wait_ge(self.sem["small_loaded"], self.w["small"])
                for q in range(2):
                    if q:
                        yield 2
                    m.need(self.pe2, f"weak{q}")
                    m.need_before(self.dve2, "weak_sum")
                    for j in range(4):
                        e, mm = 2 * q + j // 2, j % 2
                        ins = nc.scalar.activation(s["weak"][:, 2 * e + mm, :], p["hid"][:, q, j, :], ACT.Relu,
                                                   bias=self.w["weak_b"][:, e, mm:mm + 1])
                    m.done(f"weak_relu{q}", ins)
                m.need(self.pe2, "gate_t")
                m.need_before(self.pe2, "down0")
                m.done("gates_kept", nc.scalar.copy(s["gt"][:, :].bitcast(FR), p["misc"][0:2 * NE, 16:16 + P]))
                for e, at in enumerate((4, 5, 8, 10)):
                    yield at
                    m.need(self.pe2, f"up{e}")
                    if e >= 2:
                        m.need(self.pe2, f"down{e - 2}")
                    else:
                        m.need_before(self.pe2, f"down{e + 2}")
                    for j in range(4):
                        ins = nc.scalar.activation(s["strong"][:, e % 2, j, :], p["hid"][:, e % 2, j, :], ACT.Relu,
                                                   bias=self.w["s1_b"][:, e, j:j + 1])
                    m.done(f"relu{e}", ins)
                if self.last:
                    yield 14
                    m.need(self.dve2, "var_eps")
                    m.done("norm_root", nc.scalar.activation(s["st"][:, 9:10], s["st"][:, 8:9], ACT.Sqrt))
                    m.need(self.dve2, "shift")
                    m.done("h_row", nc.scalar.activation(s["hn"][:, :], s["x"][:, :], ACT.Relu, bias=s["st"][:, 11:12],
                                                         scale=s["st"][:, 10:11]))
                    yield 15
                    m.need(self.pe2, "h2_t")
                    m.done("h2_t_sb", nc.scalar.copy(s["hnt"][:, :], p["hid"][:, 0, 0, :]))

            def late_dve(self, dve, m, i, b):
                s, p = self.b
                yield 4
                m.need(self.pe2, "gate_rows")
                m.need(self.act2, "weak_relu1")
                m.need_before(self.pe2, "h_out" if self.last else "moe_t")
                gb = p["gb"]
                wh = s["weak"][:, :, :].rearrange("p (e m) n -> p e m n", m=2)
                m.done("weak_scaled", nc.vector.tensor_tensor(
                    wh, wh, gb[:, 0:NW, :].unsqueeze(2).to_broadcast([P, NW, 2, P]), ALU.mult))
                yield 5
                m.need(self.dve2, "weak_scaled")
                m.done("weak_sum", nc.vector.tensor_reduce(
                    s["moe"][:, :, :], s["weak"][:, :, :].rearrange("p (e m) n -> p m n e", m=2), AX.X, ALU.add))
                for e, at in enumerate((5, 6, 8, 10)):
                    yield at
                    m.need(self.act2, f"relu{e}")
                    m.done(f"scaled{e}", nc.vector.tensor_tensor(
                        s["strong"][:, e % 2, :, :], s["strong"][:, e % 2, :, :],
                        gb[:, NW + e, :].unsqueeze(1).to_broadcast([P, 4, P]), ALU.mult))
                yield 13
                m.need(self.pe2, "down3")
                m.need(self.dve2, "weak_sum")
                m.done("moe", nc.vector.tensor_tensor(s["moe"][:, :, :], s["moe"][:, :, :],
                                                      p["y"][:, 0:H].rearrange("p (m n) -> p m n", n=P), ALU.add),
                       wait=bool(self.last))
                if not self.last:
                    yield 15
                    m.need(self.pe2, "moe_t")
                    dve.wait_ge(self.sem["block_out"], i * 32 + 16)
                    m.done("next_row", nc.vector.tensor_tensor(
                        s["row"][:, :].rearrange("p (a j) -> p a j", j=P), s["h2"][:, :].rearrange("p (a j) -> p a j", j=P),
                        p["hid"][:, 1, 0:2, :], ALU.add), wait=True)
                    self.cut_dve(m, s["row"][:, :], s["left"][:, :], [s["cut"][:, c * H:(c + 1) * H] for c in range(PARTS)])
                    return
                m.need(self.act2, "h_t_kept")
                m.done("new_h_t", nc.vector.tensor_tensor(s["ht2"][:, :, :], s["ht2"][:, :, :], s["moe"][:, :, :], ALU.add))
                yield 14
                m.need(self.pe2, "h_out")
                m.done("x_part", nc.vector.tensor_tensor(s["u"][:, :], p["hid"][:, 1, 0, :], self.last["b_out"], ALU.add),
                       wait=True)
                dve.wait_ge(self.sem["late_in"], i * 16 + 16)
                m.done("new_x", nc.vector.tensor_tensor(s["x"][:, :], s["x"][:, :], s["u"][:, :], ALU.add), wait=True)
                x, st = s["x"][:, :], s["st"]
                m.done("stats", nc.vector.bn_stats(st[:, 0:6], x))
                m.need(self.dve2, "stats")
                dve.nop(nofuse=True)
                m.done("meanvar", nc.vector.bn_aggr(st[:, 6:8], st[:, 0:6]), wait=True)
                m.done("var_eps", nc.vector.tensor_scalar(st[:, 8:9], st[:, 7:8], LN_EPS, None, ALU.add))
                m.need(self.act2, "norm_root")
                m.done("rstd", nc.vector.reciprocal(st[:, 10:11], st[:, 9:10]), wait=True)
                m.done("shift", nc.vector.scalar_tensor_tensor(out=st[:, 11:12], in0=st[:, 6:7], scalar=-1.0,
                                                               in1=st[:, 10:11], op0=ALU.mult, op1=ALU.mult))
                yield 15
                m.need(self.pe2, "h2_w")
                dve.wait_ge(self.sem["block_out"], i * 48 + 16)
                m.done("next_y", nc.vector.tensor_copy(s["row"][:, 0:D], p["y"][:, 0:D]))
                m.done("y_b1", nc.vector.tensor_tensor(s["u"][:, :], p["y"][:, 0:D], self.last["b1"], ALU.add), wait=True)
                self.cut_dve(m, s["u"][:, :], s["left"][:, 0:D], [s["cut"][:, c * D:(c + 1) * D] for c in range(PARTS)])
                m.done("next_h", nc.vector.tensor_copy(s["row"][:, D:H], s["hn"][:, :]))

            def late_pe(self, pe, m, i, b):
                s, p = self.b
                w = self.w
                if self.in_pass:
                    pe.wait_ge(self.sem["large_loaded"], w["large"])

                def product(ap, weights):
                    for k in range(2):
                        ins = nc.tensor.matmul(ap, weights(k), s["agg2"][:, k, :], start=(k == 0), stop=(k == 1))
                    return ins

                m.need(self.act2, "agg_kept")
                for q in range(2):
                    if q == 0:
                        m.need_before(self.act2, "h2_t_sb" if self.last else "relu2")
                    else:
                        yield 1
                        m.need_before(self.dve2, "x_part" if self.last else "next_row")
                    for j in range(4):
                        e, mm = 2 * q + j // 2, j % 2
                        ins = product(p["hid"][:, q, j, :], lambda k: w["weak"][:, k, e, mm * P:(mm + 1) * P])
                    m.done(f"weak{q}", ins)

                def up(e):
                    m.need(self.act2, f"weak_relu{e}" if e < 2 else f"relu{e - 2}")
                    for j in range(4):
                        ins = product(p["hid"][:, e % 2, j, :], lambda k: w["s1"][:, k, e, j * P:(j + 1) * P])
                    m.done(f"up{e}", ins)

                def down(e):
                    m.need(self.dve2, f"scaled{e}")
                    for mm in range(2):
                        for k in range(4):
                            ins = nc.tensor.matmul(p["y"][:, mm * P:(mm + 1) * P], w["s2"][:, k, e, mm * P:(mm + 1) * P],
                                                   s["strong"][:, e % 2, k, :], start=False,
                                                   stop=(e == NW - 1 and k == 3), skip_group_check=True)
                    m.done(f"down{e}", ins)

                yield 2
                m.need(self.dve, "gates_lo")
                m.done("gate_t", nc.tensor.matmul(p["misc"][0:2 * NE, 16:16 + P], s["gates"][:, :], ident[:, :], start=True,
                                                  stop=True))
                yield 3
                m.need(self.act2, "gates_kept")
                m.need_before(self.dve2, "y_b1" if self.last else "moe")
                for e in range(NE):
                    ins = nc.tensor.matmul(p["gb"][:, e, :], w["pick_row"][:, e, :].bitcast(FR), s["gt"][:, :].bitcast(FR),
                                           start=True, stop=True)
                m.done("gate_rows", ins)
                up(0)
                yield 4
                up(1)
                yield 6
                for mm in range(2):
                    nc.tensor.matmul(p["y"][:, mm * P:(mm + 1) * P], w["s2_b"][:, mm * P:(mm + 1) * P], s["gt"][:, :],
                                     start=(mm == 0), stop=False, skip_group_check=True)
                down(0)
                yield 7
                up(2)
                yield 8
                down(1)
                yield 9
                up(3)
                yield 11
                down(2)
                yield 12
                down(3)
                yield 13 if self.last else 15
                if not self.last:
                    m.need(self.dve2, "moe")
                    for a in range(2):
                        ins = nc.tensor.transpose(p["hid"][:, 1, a, :], s["moe"][:, a, :], ident[:, :])
                    m.done("moe_t", ins)
                    return
                m.need(self.dve2, "new_h_t")
                for k in range(2):
                    ins = nc.tensor.matmul(p["hid"][:, 1, 0, :], s["ht2"][:, k, :], self.last["w_out"][:, k, :],
                                           start=(k == 0), stop=(k == 1))
                m.done("h_out", ins)
                yield 15
                m.need(self.act2, "h_row")
                m.done("h2_t", nc.tensor.transpose(p["hid"][:, 0, 0, :], s["hn"][:, :], ident[:, :]))
                m.need(self.act2, "h2_t_sb")
                m.done("h2_w", nc.tensor.matmul(p["y"][:, 0:D], s["hnt"][:, :], self.last["w1"], start=True, stop=True))

        class Layer2(Work):
            PE = "agg_t w_col h_t h_w4"
            ACT = "sums_in cleared norm_root h_row"
            DVE = "w_sb h_t_sb part0 part1 part2 new_x " + Work.NORM_DVE + Work.CUT

            def __init__(self, w4, b4):
                self.w4, self.b4 = w4, b4

            def buffers(self, tmp):
                s = {n: tmp.enter_context(sbuf(n, [P, w])) for n, w in
                     (("h", D), ("x", D), ("agg", P), ("wsum", P), ("ht", P), ("u", D), ("v", D), ("col", 1),
                      ("st", 12), ("h2", D), ("left", D))}
                s["cut"] = tmp.enter_context(sbuf("cut", [P, PARTS, D], B16))
                p = {n: tmp.enter_context(psum(n, [P, 512])) for n in ("pa", "pb", "pc")}
                return s, p

            def on_sp(self, sp, m, i, b, added):
                s, _ = self.b
                self.loads(m, [(s["h"][:, :], rows_of(rows_yh, b, D, YH)), (s["x"][:, :], rows_of(x_rows, b))])
                m.need(self.dve, "new_x")
                self.stored(m, [(rows_of(x_rows, b), s["x"][:, :])])
                m.need(self.act, "h_row")
                self.stored(m, [(rows_of(rows128[0], b), s["h2"][:, :])])
                m.need(self.dve, "cut2")
                self.stored(m, [(rows_of(parts128[0], b), s["cut"][:, :, :].rearrange("p c d -> p (c d)"))])
                self.finish(m, 3)
                yield RING

            def on_act(self, act, m, i, b, added):
                s, _ = self.b
                blk = bass.ds(b * P, P)
                self.sums_ready(m, added)
                nc.scalar.copy(s["agg"][:, :], acc[:, 0, blk])
                m.done("sums_in", nc.scalar.copy(s["wsum"][0:1, :], acc[0:1, 1, blk]), wait=True)
                m.apart()
                nc.scalar.copy(acc[:, 0, blk], zeros[:, :])
                m.done("cleared", nc.scalar.copy(acc[0:1, 1, blk], zeros[0:1, :]))
                yield 8
                yield from self.norm_act(m, s["x"][:, :], s["st"], s["h2"][:, :], 10)

            def on_dve(self, dve, m, i, b, added):
                s, p = self.b
                yield 2
                m.need(self.pe, "w_col")
                m.done("w_sb", nc.vector.tensor_copy(s["col"][:, :], p["pb"][:, P:P + 1]))
                yield 5
                m.need(self.pe, "h_t")
                m.done("h_t_sb", nc.vector.tensor_copy(s["ht"][:, :], p["pa"][:, 0:P]))
                self.loaded(m, 2)
                m.need(self.dve, "w_sb")
                m.done("part0", nc.vector.scalar_tensor_tensor(out=s["u"][:, :], in0=s["h"][:, :], scalar=s["col"][:, :],
                                                               in1=p["pb"][:, 0:P], op0=ALU.mult, op1=ALU.subtract))
                yield 7
                m.need(self.pe, "h_w4")
                m.done("part1", nc.vector.tensor_tensor(s["v"][:, :], p["pc"][:, 0:D], self.b4, ALU.add), wait=True)
                m.done("part2", nc.vector.scalar_tensor_tensor(out=s["v"][:, :], in0=s["v"][:, :],
                                                               scalar=node_deg[:, bass.ds(b, 1)], in1=s["u"][:, :],
                                                               op0=ALU.mult, op1=ALU.add), wait=True)
                m.done("new_x", nc.vector.tensor_tensor(s["x"][:, :], s["x"][:, :], s["v"][:, :], ALU.add), wait=True)
                yield from self.norm_dve(m, s["x"][:, :], s["st"], 9)
                yield 10
                m.need(self.act, "h_row")
                self.cut_dve(m, s["h2"][:, :], s["left"][:, :], [s["cut"][:, c, :] for c in range(PARTS)])

            def on_pe(self, pe, m, i, b, added):
                s, p = self.b
                yield 1
                m.need(self.act, "sums_in")
                m.done("agg_t", nc.tensor.transpose(p["pb"][:, 0:P], s["agg"][:, :], ident[:, :]))
                m.done("w_col", nc.tensor.matmul(p["pb"][:, P:P + 1], s["wsum"][0:1, :], ones[0:1, 0:1], start=True, stop=True))
                yield 4
                self.loaded(m, 2)
                m.done("h_t", nc.tensor.transpose(p["pa"][:, 0:P], s["h"][:, :], ident[:, :]))
                yield 6
                m.need(self.dve, "h_t_sb")
                m.done("h_w4", nc.tensor.matmul(p["pc"][:, 0:D], s["ht"][:, :], self.w4, start=True, stop=True))

        class Layer3(Work):
            PE = "agg_w agg_sq h_t h_w"
            ACT = "sums_in squares cleared roots"
            DVE = "h_t_sb h_sq big0 big1 root_deg floor scales scale_deg part0 part1 next_row" + Work.CUT

            def __init__(self, cur, nxt, w3):
                self.cur, self.nxt, self.w3 = cur, nxt, w3
                if nxt is None:
                    self.DVE = self.DVE.replace(Work.CUT, "")

            def buffers(self, tmp):
                s = {n: tmp.enter_context(sbuf(n, [P, w])) for n, w in
                     (("h", D), ("x", D), ("agg", P), ("sq", P), ("ht", P), ("u", D), ("n", 5), ("row", D), ("left", D))}
                s["cut"] = tmp.enter_context(sbuf("cut", [P, PARTS, D], B16))
                p = {n: tmp.enter_context(psum(n, [P, 512])) for n in ("pa", "pb", "pc")}
                return s, p

            def on_sp(self, sp, m, i, b, added):
                s, _ = self.b
                pairs = [(s["h"][:, :], rows_of(rows128[self.cur], b))]
                if self.nxt is None:
                    pairs.append((s["x"][:, :], rows_of(x_rows, b)))
                self.loads(m, pairs)
                m.need(self.dve, "next_row")
                self.stored(m, [(rows_of(out if self.nxt is None else rows128[self.nxt], b), s["row"][:, :])])
                if self.nxt is not None:
                    m.need(self.dve, "cut2")
                    self.stored(m, [(rows_of(parts128[self.nxt], b), s["cut"][:, :, :].rearrange("p c d -> p (c d)"))])
                self.finish(m, 1 if self.nxt is None else 2)
                yield RING

            def on_act(self, act, m, i, b, added):
                s, _ = self.b
                blk = bass.ds(b * P, P)
                self.sums_ready(m, added)
                m.done("sums_in", nc.scalar.copy(s["agg"][:, :], acc[:, 0, blk]))
                m.done("squares", nc.scalar.activation(s["sq"][:, :], acc[:, 0, blk], ACT.Square), wait=True)
                m.apart()
                m.done("cleared", nc.scalar.copy(acc[:, 0, blk], zeros[:, :]))
                yield 6
                m.need(self.dve, "big1")
                m.done("roots", nc.scalar.activation(s["n"][:, 3:5], s["n"][:, 1:3], ACT.Sqrt))

            def on_dve(self, dve, m, i, b, added):
                s, p = self.b
                n = s["n"]
                rdeg = node_rdeg[:, bass.ds(b, 1)]
                nl = 2 if self.nxt is None else 1
                yield 4
                m.need(self.pe, "h_t")
                m.done("h_t_sb", nc.vector.tensor_copy(s["ht"][:, :], p["pa"][:, 0:P]))
                self.loaded(m, nl)
                m.done("h_sq", nc.vector.tensor_tensor_reduce(out=s["u"][:, :], in0=s["h"][:, :], in1=s["h"][:, :],
                                                              scale=1.0, scalar=0.0, op0=ALU.mult, op1=ALU.add,
                                                              accum_out=n[:, 0:1]), wait=True)
                m.need(self.pe, "agg_sq")
                m.done("big0", nc.vector.tensor_scalar(n[:, 1:2], p["pb"][:, D:D + 1], TINY, None, ALU.max))
                m.done("big1", nc.vector.tensor_scalar(n[:, 2:3], n[:, 0:1], TINY, None, ALU.max))
                yield 6
                m.need(self.act, "roots")
                m.done("root_deg", nc.vector.tensor_scalar(n[:, 3:4], n[:, 3:4], rdeg, None, ALU.mult), wait=True)
                m.done("floor", nc.vector.tensor_scalar(n[:, 3:5], n[:, 3:5], L2_EPS, None, ALU.max), wait=True)
                m.done("scales", nc.vector.reciprocal(n[:, 3:5], n[:, 3:5]), wait=True)
                m.done("scale_deg", nc.vector.tensor_scalar(n[:, 3:4], n[:, 3:4], rdeg, None, ALU.mult), wait=True)
                m.need(self.pe, "h_w")
                m.done("part0", nc.vector.scalar_tensor_tensor(out=s["u"][:, :], in0=p["pb"][:, 0:D], scalar=n[:, 3:4],
                                                               in1=self.w3[:, 2, :], op0=ALU.mult, op1=ALU.add), wait=True)
                m.done("part1", nc.vector.scalar_tensor_tensor(out=s["u"][:, :], in0=p["pc"][:, 0:D], scalar=n[:, 4:5],
                                                               in1=s["u"][:, :], op0=ALU.mult, op1=ALU.add), wait=True)
                if self.nxt is None:
                    m.done("next_row", nc.vector.tensor_tensor(s["row"][:, :], s["u"][:, :], s["x"][:, :], ALU.add))
                else:
                    m.done("next_row", nc.vector.tensor_scalar(s["row"][:, :], s["u"][:, :], 0.0, None, ALU.max), wait=True)
                    self.cut_dve(m, s["row"][:, :], s["left"][:, :], [s["cut"][:, c, :] for c in range(PARTS)])

            def on_pe(self, pe, m, i, b, added):
                s, p = self.b
                yield 1
                m.need(self.act, "squares")
                m.done("agg_w", nc.tensor.matmul(p["pb"][:, 0:D], s["agg"][:, :], self.w3[:, 0, :], start=True, stop=True))
                m.done("agg_sq", nc.tensor.matmul(p["pb"][:, D:D + 1], s["sq"][:, :], ones[:, 0:1], start=True, stop=True))
                yield 3
                self.loaded(m, 2 if self.nxt is None else 1)
                m.done("h_t", nc.tensor.transpose(p["pa"][:, 0:P], s["h"][:, :], ident[:, :]))
                yield 5
                m.need(self.dve, "h_t_sb")
                m.done("h_w", nc.tensor.matmul(p["pc"][:, 0:D], s["ht"][:, :], self.w3[:, 1, :], start=True, stop=True))

        def load(pairs):
            with phase(nc, bank, "loaded") as (block, (loaded,)):
                @block.sync
                def _(sp):
                    for dst, src in pairs:
                        sp.dma_start(dst, src).then_inc(loaded, 16)
                    sp.wait_ge(loaded, 16 * len(pairs))

        def expert_tables(lay):
            w = {
                "weak": big[:, 0, 0:2048].rearrange("p (k e f) -> p k e f", k=2, e=NW),
                "s1": big[:, 0, 2048:6144].rearrange("p (k e f) -> p k e f", k=2, e=NW),
                "s2": big[:, 0, 6144:10240].rearrange("p (k e f) -> p k e f", k=4, e=NW),
                "router": lay.enter_context(sbuf("router", [P, 4, NE + 1])),
                "router_b": lay.enter_context(sbuf("router_b", [P, NE + 1])),
                "weak_b": lay.enter_context(sbuf("weak_b", [P, NW, 2])),
                "s1_b": lay.enter_context(sbuf("s1_b", [P, NW, 4])),
                "s2_b": lay.enter_context(sbuf("s2_b", [2 * NE, H])),
                "pick_row": lay.enter_context(sbuf("pick_row", [2 * NE, NE, P])),
                "small": 16 * 15, "large": 16 * 8,
            }
            row = lay.enter_context(sbuf("row", [2 * NE, 1]))
            with phase(nc, bank, "own_s") as (block, (own_s,)):
                @block.gpsimd
                def _(pool):
                    nc.gpsimd.memset(w["router"][:, :, NE:NE + 1], 0.0)
                    nc.gpsimd.memset(w["s2_b"][:, :], 0.0)

                @block.vector
                def _(dve):
                    own = Chain(dve, own_s)
                    own(nc.vector.tensor_scalar(row[:, :], iota_col0[0:2 * NE, :], float(NE), float(-NE), ALU.is_ge, ALU.mult))
                    own(nc.vector.tensor_tensor(row[:, :], row[:, :], iota_col0[0:2 * NE, :], ALU.add))
                    own(nc.vector.tensor_tensor(w["pick_row"][:, :, :].bitcast(FR),
                                                iota_row0[0:2 * NE, 0:NE].unsqueeze(2).to_broadcast([2 * NE, NE, P]),
                                                row[:, :].unsqueeze(2).to_broadcast([2 * NE, NE, P]), ALU.is_equal))
            return w

        def load_experts(l, w):
            def prologue(sp, small, large):
                count = {small: 0, large: 0}

                def go(dst, src, sem=small):
                    sp.dma_start(dst, src).then_inc(sem, 16)
                    count[sem] += 16

                with nc.allow_non_contiguous_dma("router rows and columns of biases"):
                    go(w["router"][:, :, 0:NE], t["L1_gnn_router_W"][l, :, :].rearrange("(k p) f -> p k f", p=P))
                    for k in range(2):
                        go(w["router"][:, k, NE:NE + 1], t["L1_gnn_conf_W"][l, k * P:(k + 1) * P, :])
                    for e in range(NW):
                        go(w["weak_b"][:, e, :], t["L1_gnn_weak_b"][l, e, :].rearrange("(m p) -> p m", p=P))
                        go(w["s1_b"][:, e, :], t["L1_gnn_strong_b1"][l, e, :].rearrange("(m p) -> p m", p=P))
                for k in range(2):
                    go(w["s2_b"][k * NE + NW:(k + 1) * NE, :], t["L1_gnn_strong_b2"][l, :, :])
                go(w["router_b"][:, 0:NE], bcast_vec(t["L1_gnn_router_b"][l, :]))
                go(w["router_b"][:, NE:NE + 1], bcast_vec(t["L1_gnn_conf_b"][l, :]))
                for k in range(4):
                    rows = slice(k * P, (k + 1) * P)
                    if k < 2:
                        go(w["weak"][:, k, :, :], t["L1_gnn_weak_W"][l, :, rows, :].rearrange("e p f -> p e f"), large)
                        go(w["s1"][:, k, :, :], t["L1_gnn_strong_W1"][l, :, rows, :].rearrange("e p f -> p e f"), large)
                    go(w["s2"][:, k, :, :], t["L1_gnn_strong_W2"][l, :, rows, :].rearrange("e p f -> p e f"), large)
                assert (count[small], count[large]) == (w["small"], w["large"]), count

            return prologue

        def layer3_weights(lay):
            w3 = [lay.enter_context(sbuf("w3", [P, 3, D])) for _ in range(3)]
            with ExitStack() as tmp:
                raw = tmp.enter_context(sbuf("raw", [P, 3, 2, D]))
                pt = tmp.enter_context(psum("pt", [P, 3, 512]))
                with phase(nc, bank, "loaded", "done") as (block, (loaded, done)):
                    @block.sync
                    def _(sp):
                        for l in range(3):
                            sp.dma_start(raw[:, l, 0, :], t["L3_gnn_Wl"][l, :, :]).then_inc(loaded, 16)
                            sp.dma_start(raw[:, l, 1, :], t["L3_gnn_Wr"][l, :, :]).then_inc(loaded, 16)
                            sp.dma_start(w3[l][:, 2, :], bcast_vec(t["L3_gnn_bl"][l, :])).then_inc(loaded, 16)
                        sp.wait_ge(loaded, 16 * 9)

                    @block.tensor
                    def _(pe):
                        pe.wait_ge(loaded, 16 * 9)
                        for l in range(3):
                            for a in range(2):
                                last = nc.tensor.transpose(pt[:, l, a * D:(a + 1) * D], raw[:, l, a, :], ident[:, :])
                        last.then_inc(done, 1)

                    @block.vector
                    def _(dve):
                        dve.wait_ge(done, 1)
                        for l in range(3):
                            nc.vector.tensor_copy(w3[l][:, 0:2, :], pt[:, l, 0:2 * D].rearrange("p (a j) -> p a j", j=D))
            return w3

        setup()
        first_norm()
        start_sums()
        with ExitStack() as lay:
            def weight(name, shape):
                return lay.enter_context(sbuf(name, shape))

            wn, wl, w_in, b_in = (weight("wn", [P, D]), weight("wl", [P, D]), weight("w_in", [P, H]), weight("b_in", [P, H]))
            emb = weight("emb", [P, REL_BLOCKS, D])
            emb_parts = weight("emb_parts", [P, 2, REL_BLOCKS, D])
            with phase(nc, bank, "zeroed") as (block, _sems):
                @block.gpsimd
                def _(pool):
                    nc.gpsimd.memset(emb[:, REL_BLOCKS - 1, :], 0.0)
            whole = (REL_BLOCKS - 1) * P
            load([(wn[:, :], t["L0_gnn_W_neighbor"]), (wl[:, :], t["L0_gnn_loop_weight"]), (w_in[:, :], t["L1_gnn_W_in"]),
                  (b_in[:, :], bcast_vec(t["L1_gnn_b_in"])),
                  (emb[:, 0:REL_BLOCKS - 1, :], t["L0_gnn_rel_emb"][0:whole, :].rearrange("(m p) d -> p m d", p=P)),
                  (emb[0:RELS - whole, REL_BLOCKS - 1, :], t["L0_gnn_rel_emb"][whole:RELS, :])])
            with phase(nc, bank, "own_s") as (block, (own_s,)):
                @block.vector
                def _(dve):
                    own = Chain(dve, own_s)
                    own(nc.vector.tensor_copy(emb_parts[:, 0, :, :].bitcast(FR), emb[:, :, :]))
                    nc.vector.tensor_tensor(emb_parts[:, 1, :, :].bitcast(FR), emb[:, :, :], emb_parts[:, 0, :, :],
                                            ALU.subtract)
            edge_pass(parts128[0], D, Layer0(wn[:, :], wl[:, :], w_in[:, :], b_in[:, :]), rel_emb=emb_parts)

        with ExitStack() as lay:
            def weight(name, shape):
                return lay.enter_context(sbuf(name, shape))

            w = expert_tables(lay)
            w_out, b_out, w1, b1 = weight("w_out", [P, 2, D]), weight("b_out", [P, D]), weight("w1", [P, D]), weight("b1", [P, D])
            load([(w_out[:, :, :], t["L1_gnn_W_out"].rearrange("(k p) d -> p k d", p=P)),
                  (b_out[:, :], bcast_vec(t["L1_gnn_b_out"])), (w1[:, :], t["L2_gnn_W1"]),
                  (b1[:, :], bcast_vec(t["L2_gnn_b1"]))])
            last = {"w_out": w_out, "b_out": b_out[:, :], "w1": w1[:, :], "b1": b1[:, :]}
            for l in range(3):
                edge_pass(parts256[l % 2], H, Layer1(l % 2, (l + 1) % 2, w, last if l == 2 else None),
                          prologue=load_experts(l, w))

        with ExitStack() as lay:
            w4, b4, w2, b2 = (lay.enter_context(sbuf(n, s)) for n, s in (("w4", [P, D]), ("b4", [P, D]), ("w2", [P, D]),
                                                                         ("b2", [P, 1])))
            load([(w4[:, :], t["L2_gnn_W4"]), (b4[:, :], bcast_vec(t["L2_gnn_b4"])),
                  (w2[:, :], bcast_vec(t["L2_gnn_W2"].rearrange("p o -> (p o)"))), (b2[:, :], bcast_vec(t["L2_gnn_b2"]))])
            edge_pass(rows_yh, H, Layer2(w4[:, :], b4[:, :]), edge_net=(w2[:, :], b2[:, :]))

        with ExitStack() as lay:
            w3 = layer3_weights(lay)
            for l in range(3):
                edge_pass(parts128[l % 2], D, Layer3(l % 2, (l + 1) % 2 if l < 2 else None, w3[l]))


def bcast_vec(vec):
    return vec.rearrange("(o j) -> o j", o=1).to_broadcast((P, vec.shape[0]))


_INS = ['x', 'src', 'dst', 'edge_type_500', 'L0_gnn_rel_emb', 'L0_gnn_W_neighbor', 'L0_gnn_loop_weight',
        'L1_gnn_W_in', 'L1_gnn_b_in', 'L1_gnn_router_W', 'L1_gnn_router_b', 'L1_gnn_weak_W', 'L1_gnn_weak_b',
        'L1_gnn_strong_W1', 'L1_gnn_strong_b1', 'L1_gnn_strong_W2', 'L1_gnn_strong_b2', 'L1_gnn_conf_W',
        'L1_gnn_conf_b', 'L1_gnn_W_out', 'L1_gnn_b_out', 'L2_gnn_W1', 'L2_gnn_b1', 'L2_gnn_W2', 'L2_gnn_b2',
        'L2_gnn_W4', 'L2_gnn_b4', 'L3_gnn_Wl', 'L3_gnn_bl', 'L3_gnn_Wr']


def kernel(**inputs):
    import numpy as _np
    import concourse.bacc as _bacc
    from concourse import mybir as _mybir
    from concourse.bass_utils import run_bass_kernel_spmd as _run

    nc = _bacc.Bacc("TRN2", target_bir_lowering=False, num_devices=1)
    arrays, handles = {}, {}
    for name in _INS:
        a = _np.ascontiguousarray(inputs[name])
        arrays[f"in_{name}"] = a
        handles[name] = nc.dram_tensor(f"in_{name}", a.shape, _mybir.dt.from_np(a.dtype), kind="ExternalInput").ap()
    out = nc.dram_tensor("out_x", (NPAD, D), _mybir.dt.float32, kind="ExternalOutput").ap()
    gnn_kernel(nc, handles, out)
    r = _run(nc, [arrays], core_ids=[0])
    return r.results[0]["out_x"][:N]
```
